# Optimizing a Trainium2 kernel written in Bass

```python
import numpy as np
import jax
import jax.numpy as jnp

def _softmax(x, axis=-1):
    return jax.nn.softmax(x, axis=axis)

def _gelu(x):
    return jax.nn.gelu(x, approximate=True)

def _silu(x):
    return jax.nn.silu(x)

def _sigmoid(x):
    return jax.nn.sigmoid(x)

def _layernorm(x, axis=-1, eps=1e-05):
    m = jnp.mean(x, axis=axis, keepdims=True)
    v = jnp.var(x, axis=axis, keepdims=True)
    return (x - m) / jnp.sqrt(v + eps)

def _scatter_add(tgt, idx, src, axis=0):
    return tgt.at[idx].add(src)

def _segment_sum(src, seg, n):
    return jax.ops.segment_sum(src, seg, n)
kernel_name = 'mk_macaron_d1_jaxref_r8_475aeb'

def setup_inputs(seed: int=0):
    np.random.seed(seed)
    _w = jnp.asarray

    def _L0_attn_setup():
        import jax, jax.numpy as jnp
        import numpy as np
        B, S, D = (2, 256, 256)
        H, DH, GROUPS = (16, 128, 4)
        KV = H // GROUPS
        G = GROUPS
        key = jax.random.key(seed)
        ks = jax.random.split(key, 5)
        sd = 1.0 / np.sqrt(D)
        return {'x': jax.random.normal(ks[0], (B, S, D), dtype=jnp.float32), 'Wq': jax.random.normal(ks[1], (D, H * DH), dtype=jnp.float32) * sd, 'bq': jnp.zeros((H * DH,), dtype=jnp.float32), 'Wk': jax.random.normal(ks[2], (D, KV * DH), dtype=jnp.float32) * sd, 'bk': jnp.zeros((KV * DH,), dtype=jnp.float32), 'Wv': jax.random.normal(ks[3], (D, KV * DH), dtype=jnp.float32) * sd, 'bv': jnp.zeros((KV * DH,), dtype=jnp.float32), 'Wo': jax.random.normal(ks[4], (H * DH, D), dtype=jnp.float32) * (1.0 / np.sqrt(H * DH)), 'bo': jnp.zeros((D,), dtype=jnp.float32)}
    _L0_attn_in = _L0_attn_setup()

    def _L0_ffn_setup():
        import jax, jax.numpy as jnp
        import numpy as np
        B, T, D = (2, 128, 256)
        E, K, H = (64, 4, 64)
        S, HS = (2, H * K)
        CAP = 64
        key = jax.random.key(seed)
        ks = jax.random.split(key, 9)
        scale = 0.02
        return {'x': jax.random.normal(ks[0], (B, T, D), jnp.float32), 'Wr': jax.random.normal(ks[1], (D, E), jnp.float32) * scale, 'router_bias': jnp.zeros((E,), jnp.float32), 'Wg': jax.random.normal(ks[2], (E, D, H), jnp.float32) * scale, 'Wu': jax.random.normal(ks[3], (E, D, H), jnp.float32) * scale, 'Wd': jax.random.normal(ks[4], (E, H, D), jnp.float32) * scale, 'Sg': jax.random.normal(ks[5], (S, D, HS), jnp.float32) * scale, 'Su': jax.random.normal(ks[6], (S, D, HS), jnp.float32) * scale, 'Sd': jax.random.normal(ks[7], (S, HS, D), jnp.float32) * scale}
    _L0_ffn_in = _L0_ffn_setup()
    _d = {'L0_attn_x': _L0_attn_in['x'], 'L0_attn_Wq': _L0_attn_in['Wq'], 'L0_attn_bq': _L0_attn_in['bq'], 'L0_attn_Wk': _L0_attn_in['Wk'], 'L0_attn_bk': _L0_attn_in['bk'], 'L0_attn_Wv': _L0_attn_in['Wv'], 'L0_attn_bv': _L0_attn_in['bv'], 'L0_attn_Wo': _L0_attn_in['Wo'], 'L0_attn_bo': _L0_attn_in['bo'], 'L0_ffn_Wr': _L0_ffn_in['Wr'], 'L0_ffn_router_bias': _L0_ffn_in['router_bias'], 'L0_ffn_Wg': _L0_ffn_in['Wg'], 'L0_ffn_Wu': _L0_ffn_in['Wu'], 'L0_ffn_Wd': _L0_ffn_in['Wd'], 'L0_ffn_Sg': _L0_ffn_in['Sg'], 'L0_ffn_Su': _L0_ffn_in['Su'], 'L0_ffn_Sd': _L0_ffn_in['Sd']}
    _x0 = _d['L0_attn_x']
    _d['L0_attn_x'] = jax.random.normal(jax.random.fold_in(jax.random.key(seed), 1), (8, 256, 256), dtype=_x0.dtype)
    del _x0
    return _d

def reference(L0_attn_x, L0_attn_Wq, L0_attn_bq, L0_attn_Wk, L0_attn_bk, L0_attn_Wv, L0_attn_bv, L0_attn_Wo, L0_attn_bo, L0_ffn_Wr, L0_ffn_router_bias, L0_ffn_Wg, L0_ffn_Wu, L0_ffn_Wd, L0_ffn_Sg, L0_ffn_Su, L0_ffn_Sd):

    def _L0_attn_ref(x, Wq, bq, Wk, bk, Wv, bv, Wo, bo):
        import jax, jax.numpy as jnp
        import numpy as np
        B, S, D = (2, 256, 256)
        H, DH, GROUPS = (16, 128, 4)
        KV = H // GROUPS
        G = GROUPS
        b, s, _ = x.shape
        Q = (x @ Wq + bq).reshape(b, s, KV, G, DH)
        K = (x @ Wk + bk).reshape(b, s, KV, DH)
        V = (x @ Wv + bv).reshape(b, s, KV, DH)
        scale = 1.0 / np.sqrt(DH).astype(np.float32)
        scores = jnp.einsum('bqkgd,bpkd->bkgqp', Q, K) * scale
        attn = jax.nn.softmax(scores, axis=-1)
        out = jnp.einsum('bkgqp,bpkd->bqkgd', attn, V)
        out = out.reshape(b, s, H * DH)
        return out @ Wo + bo

    def _L0_ffn_ref(x, Wr, router_bias, Wg, Wu, Wd, Sg, Su, Sd):
        import jax, jax.numpy as jnp
        import numpy as np
        B, T, D = (2, 128, 256)
        E, K, H = (64, 4, 64)
        S, HS = (2, H * K)
        CAP = 64
        Bx, Tx, Dx = x.shape
        N = Bx * Tx
        flat = x.reshape(N, Dx)
        logits = flat @ Wr + router_bias
        scores = jax.nn.softmax(logits, axis=-1)
        topk_scores, topk_idx = jax.lax.top_k(scores, K)
        topk_scores = topk_scores / topk_scores.sum(-1, keepdims=True)
        eid = topk_idx.reshape(-1)
        w = topk_scores.reshape(-1)
        tok = jnp.repeat(jnp.arange(N), K)
        oh = jax.nn.one_hot(eid, E, dtype=jnp.int32)
        pos = (jnp.cumsum(oh, axis=0) * oh).sum(-1) - 1
        valid = pos < CAP
        xb = jnp.zeros((E, CAP, Dx), x.dtype).at[eid, pos].set(flat[tok], mode='drop')
        h = jax.nn.silu(jnp.einsum('ecd,edh->ech', xb, Wg)) * jnp.einsum('ecd,edh->ech', xb, Wu)
        yb = jnp.einsum('ech,ehd->ecd', h, Wd)
        y = yb[eid, jnp.minimum(pos, CAP - 1)] * (w * valid)[:, None]
        out = jnp.zeros((N, Dx), x.dtype).at[tok].add(y)
        hs = jax.nn.silu(jnp.einsum('nd,sdh->nsh', flat, Sg)) * jnp.einsum('nd,sdh->nsh', flat, Su)
        out = out + jnp.einsum('nsh,shd->nd', hs, Sd)
        return out.reshape(Bx, Tx, Dx)
    x = L0_attn_x
    x = x + 0.5 * _L0_ffn_ref(_layernorm(x, axis=-1), L0_ffn_Wr, L0_ffn_router_bias, L0_ffn_Wg, L0_ffn_Wu, L0_ffn_Wd, L0_ffn_Sg, L0_ffn_Su, L0_ffn_Sd)
    x = x + _L0_attn_ref(_layernorm(x, axis=-1), L0_attn_Wq, L0_attn_bq, L0_attn_Wk, L0_attn_bk, L0_attn_Wv, L0_attn_bv, L0_attn_Wo, L0_attn_bo)
    x = x + 0.5 * _L0_ffn_ref(_layernorm(x, axis=-1), L0_ffn_Wr, L0_ffn_router_bias, L0_ffn_Wg, L0_ffn_Wu, L0_ffn_Wd, L0_ffn_Sg, L0_ffn_Su, L0_ffn_Sd)
    return x

_drawn_inputs = setup_inputs


def setup_inputs(seed=0):
    import zlib

    import numpy as np

    out = dict(_drawn_inputs(seed))
    spreads = {'L0_attn_bq': (0.0, 0.733),
     'L0_attn_bk': (0.0, 0.8),
     'L0_attn_bv': (0.0, 0.1),
     'L0_attn_bo': (0.0, 0.1),
     'L0_ffn_router_bias': (0.0, 0.8)}
    factors = {'L0_ffn_Wr': 8.0, 'L0_ffn_Wg': 8.0, 'L0_ffn_Wu': 8.0, 'L0_ffn_Wd': 8.0}
    for name, (base, spread) in spreads.items():
        noise = np.random.default_rng([zlib.crc32(name.encode()), seed]).standard_normal(out[name].shape)
        drawn = base * np.exp(spread * noise) if base else spread * noise
        out[name] = jnp.asarray(drawn.astype(out[name].dtype))
    for name, factor in factors.items():
        out[name] = (out[name] * factor).astype(out[name].dtype)
    return out
```

```python
from contextlib import ExitStack

import concourse.bass as bass
from concourse import mybir

F32 = mybir.dt.float32
F32R = mybir.dt.float32r
BF16 = mybir.dt.bfloat16
U32 = mybir.dt.uint32
ALU = mybir.AluOpType
ACT = mybir.ActivationFunctionType
AX = mybir.AxisListType

P = 128
D = 256
C = D // P
NB = 8
S = 256
J = S // P
H, DH, KV = 16, 128, 4
GROUP = H // KV
E, K, HID, CAP = 64, 4, 64, 64
HS = 512
HC = HS // P
SCALE = float(DH) ** -0.5
EPS = 1e-5
DROPPED = 8192
CREDIT = 2
DMA = 16


def at(n):
    return n + CREDIT


def settle(engine, passed):
    engine.sem_inc(passed, 1)


def split_product(pe, out, left, right, start, stop):
    pe.matmul(out, left[1], right[0], start=start, stop=False)
    pe.matmul(out, left[0], right[1], start=False, stop=False)
    return pe.matmul(out, left[0], right[0], start=False, stop=stop)


class Memory:

    def __init__(self, nc, ctx, phase):
        self.nc, self.ctx, self.phase = nc, ctx, phase

    def sb(self, name, shape, dt=F32):
        return self.ctx.enter_context(self.nc.sbuf_tensor(f"{self.phase}_{name}", shape, dt))

    def ps(self, name, shape, dt=F32):
        return self.ctx.enter_context(self.nc.psum_tensor(f"{self.phase}_ps_{name}", shape, dt))

    def sem(self, name):
        return self.ctx.enter_context(self.nc.semaphore(f"{self.phase}_{name}"))

    def sems(self, names):
        return [self.sem(n) for n in names.split()]


def setup_phase(nc, W, a):
    with ExitStack() as ctx:
        m = Memory(nc, ctx, "setup")
        raw_gate = m.sb("raw_gate", [P, C, HS])
        raw_up = m.sb("raw_up", [P, C, HS])
        raw_router = m.sb("raw_router", [P, C, P])
        bias_rows = m.sb("bias_rows", [25, P])
        zeros = m.sb("zeros", [P, 8 * D])
        bias_cols = m.ps("bias_cols", [P, 512])
        made, filled, x_in, w_in, b_in, zero_out, cols_done, hi_done, lo_done, pool_done = m.sems(
            "made filled x_in w_in b_in zero_out cols_done hi_done lo_done pool_done")
        with nc.Block() as block:

            @block.sync
            def _(sp):
                sp.dma_start(W["x"][:, :, :, :], a["L0_attn_x"].rearrange("b (j p) d -> p b j d", p=P)).then_inc(x_in, DMA)
                for s in range(2):
                    half = HS // 2
                    sp.dma_start(raw_gate[:, :, s * half:(s + 1) * half],
                                 a["L0_ffn_Sg"][s].rearrange("(p c) h -> p c h", c=C)).then_inc(w_in, DMA)
                    sp.dma_start(raw_up[:, :, s * half:(s + 1) * half],
                                 a["L0_ffn_Su"][s].rearrange("(p c) h -> p c h", c=C)).then_inc(w_in, DMA)
                sp.dma_start(W["shared_down"][:, :, :],
                             a["L0_ffn_Sd"].rearrange("s (q p) d -> p (s q) d", p=P)).then_inc(w_in, DMA)
                sp.dma_start(W["bo"][:, :], a["L0_attn_bo"].partition_broadcast(P)).then_inc(w_in, DMA)
                sp.wait_ge(filled, 1)
                sp.dma_start(raw_router[:, :, 0:E], a["L0_ffn_Wr"].rearrange("(p c) e -> p c e", c=C)).then_inc(w_in, DMA)
                sp.dma_start(bias_rows[0:16, :], a["L0_attn_bq"].rearrange("(h p) -> h p", p=P)).then_inc(b_in, DMA)
                sp.dma_start(bias_rows[16:20, :], a["L0_attn_bk"].rearrange("(h p) -> h p", p=P)).then_inc(b_in, DMA)
                sp.dma_start(bias_rows[20:24, :], a["L0_attn_bv"].rearrange("(h p) -> h p", p=P)).then_inc(b_in, DMA)
                sp.dma_start(bias_rows[24:25, 0:E], a["L0_ffn_router_bias"].rearrange("(h p) -> h p", p=E)).then_inc(b_in, DMA)
                slots = W["slot_x"].rearrange("(p r) d -> p (r d)", p=P)
                for n in range(4):
                    sp.dma_start(slots[:, n * 8 * D:(n + 1) * 8 * D], zeros[:, :]).then_inc(zero_out, DMA)
                sp.wait_ge(x_in, DMA)
                sp.wait_ge(zero_out, 4 * DMA)

            @block.gpsimd
            def _(pool):
                pool.memset(W["ident"][:, :], 0.0).then_inc(pool_done, 1)
                pool.memset(W["before"][:, :], 1.0).then_inc(pool_done, 1)
                pool.memset(W["ones"][:, :], 1.0)
                pool.memset(W["half"][:, :], -0.5)
                pool.iota(W["expert_of"][:, :], pattern=[[1, E]], base=0, channel_multiplier=0,
                          allow_small_or_imprecise_dtypes=True)
                pool.wait_ge(pool_done, 2)
                pool.affine_select(out=W["ident"][:, :], in_=W["ident"][:, :], compare_op=ALU.not_equal, fill=1.0,
                                   base=0, pattern=[[-1, P]], channel_multiplier=1)
                pool.affine_select(out=W["before"][:, :], in_=W["before"][:, :], compare_op=ALU.is_gt, fill=0.0,
                                   base=0, pattern=[[1, P]], channel_multiplier=-1).then_inc(made, 1)

            @block.vector
            def _(dve):
                dve.memset(raw_router[:, :, :], 0.0)
                dve.memset(bias_rows[:, :], 0.0)
                dve.memset(zeros[:, :], 0.0).then_inc(filled, 1)
                dve.wait_ge(hi_done, 1)
                dve.tensor_tensor(W["gate"][1][:, :, :], raw_gate[:, :, :], W["gate"][0][:, :, :].bitcast(F32), ALU.subtract)
                dve.wait_ge(hi_done, 2)
                dve.tensor_tensor(W["up"][1][:, :, :], raw_up[:, :, :], W["up"][0][:, :, :].bitcast(F32), ALU.subtract)
                dve.wait_ge(hi_done, 3)
                dve.tensor_tensor(W["router"][1][:, :, :], raw_router[:, :, :], W["router"][0][:, :, :].bitcast(F32), ALU.subtract)
                dve.wait_ge(cols_done, 1)
                dve.tensor_copy(W["bias"][:, :], bias_cols[:, 0:25])

            @block.scalar
            def _(act):
                act.wait_ge(w_in, 7 * DMA)
                act.activation(W["gate"][0][:, :, :], raw_gate[:, :, :], ACT.Copy).then_inc(hi_done, 1)
                act.activation(W["up"][0][:, :, :], raw_up[:, :, :], ACT.Copy).then_inc(hi_done, 1)
                act.activation(W["router"][0][:, :, :], raw_router[:, :, :], ACT.Copy).then_inc(hi_done, 1)

            @block.tensor
            def _(pe):
                pe.wait_ge(made, 1)
                pe.wait_ge(b_in, 4 * DMA)
                pe.transpose(bias_cols[:, 0:25], bias_rows[:, :], W["ident"][0:25, 0:25]).then_inc(cols_done, 1)


class Experts:

    QE = 4
    PAIRS = QE // 2
    QUADS = E // QE
    RING = 4

    def __init__(self, nc, ctx, W, a, phase, banks_t, banks_gu, banks_y, split=None):
        m = Memory(nc, ctx, phase)
        self.W, self.a, self.split = W, a, split
        R, PAIRS = self.RING, self.PAIRS
        self.w_gate = [m.sb(f"w_gate{n}", [P, self.QE, C, HID]) for n in range(R)]
        self.w_up = [m.sb(f"w_up{n}", [P, self.QE, C, HID]) for n in range(R)]
        self.w_down = [m.sb(f"w_down{n}", [P, PAIRS, D]) for n in range(R)]
        self.slot_in = [m.sb(f"slot_in{n}", [P, PAIRS, D]) for n in range(R)]
        self.slot_out = [m.sb(f"slot_out{n}", [P, PAIRS, D]) for n in range(R)]
        self.slot_t = [m.sb(f"slot_t{n}", [P, PAIRS, C, P]) for n in range(2)]
        self.tanh = [m.sb(f"tanh{n}", [P, PAIRS, CAP]) for n in range(2)]
        self.gate = [m.sb(f"gate{n}", [P, PAIRS, CAP]) for n in range(2)]
        self.hidden = [m.sb(f"hidden{n}", [P, PAIRS, P]) for n in range(2)]
        self.ps_t = banks_t
        self.ps_gu = [b[:, 0:2 * PAIRS * CAP].rearrange("p (s r t) -> p s r t", s=2, t=CAP) for b in banks_gu]
        self.ps_y = [b[:, :].rearrange("p (r d) -> p r d", d=D) for b in banks_y]
        self.t_psum, self.gu_psum, self.y_psum, self.passed = m.sems("t_psum gu_psum y_psum passed")
        self.t_ready, self.tanh_ready, self.out_ready, self.split_hi = m.sems("t_ready tanh_ready out_ready split_hi")
        self.hidden_ready, self.split_lo = m.sems("hidden_ready split_lo")
        self.w_dma = [m.sem(f"w_dma{n}") for n in range(R)]
        self.slot_dma = [m.sem(f"slot_dma{n}") for n in range(R)]
        self.store_dma = [m.sem(f"store_dma{n}") for n in range(R)]
        if split:
            self.raw_q = [m.sb(f"raw_q{n}", [P, C, DH]) for n in range(2)]
            self.raw_o = [m.sb(f"raw_o{n}", [P, D]) for n in range(2)]
            self.raw_dma = [m.sem(f"raw_dma{n}") for n in range(2)]

    def exists(self, i, n):
        return not isinstance(i, int) or 0 <= self.RING * i + n < self.QUADS

    def steps(self, engine, step):
        with engine.Fori(0, self.QUADS // self.RING - 1) as i:
            for n in range(self.RING):
                step(i, n)
        for n in range(self.RING):
            step(self.QUADS // self.RING - 1, n)

    def uses(self, i, n):
        return i + n // self.RING + 1

    def stored(self, engine):
        for n in range(self.RING):
            engine.wait_ge(self.store_dma[n], DMA * (self.QUADS // self.RING))


    def load_weights(self, sp, i, n):
        q, r = self.RING * i + n, n % self.RING
        for buffer, name in ((self.w_gate, "L0_ffn_Wg"), (self.w_up, "L0_ffn_Wu")):
            sp.dma_start(buffer[r][:, :, :, :], self.a[name].rearrange("e (p c) h -> p e c h", c=C)[
                :, bass.ds(q * self.QE, self.QE), :, :]).then_inc(self.w_dma[r], DMA)
        sp.dma_start(self.w_down[r][:, :, :], self.a["L0_ffn_Wd"].rearrange("(r two) h d -> (two h) r d", two=2)[
            :, bass.ds(q * self.PAIRS, self.PAIRS), :]).then_inc(self.w_dma[r], DMA)

    def load_slots(self, sp, i, n):
        q, r = self.RING * i + n, n % self.RING
        sp.dma_start(self.slot_in[r][:, :, :], self.W["slot_x"].rearrange("(q r p) d -> q p r d", p=P, r=self.PAIRS)[
            q]).then_inc(self.slot_dma[r], DMA)

    def load_split(self, sp, i, n):
        q = self.RING * i + n
        sp.dma_start(self.raw_q[n % 2][:, :, :], self.a["L0_attn_Wq"].rearrange("(p c) n -> p c n", c=C)[
            :, :, bass.ds(q * DH, DH)]).then_inc(self.raw_dma[n % 2], DMA)
        sp.dma_start(self.raw_o[n % 2][:, :], self.a["L0_attn_Wo"].rearrange("(h p) d -> h p d", p=P)[q]
                     ).then_inc(self.raw_dma[n % 2], DMA)

    def sp_steps(self, sp):
        def step(i, n):
            q, r = self.RING * i + n, n % self.RING
            if self.split and self.exists(i, n + 2):
                sp.wait_ge(self.split_lo, at(q + 1))
                self.load_split(sp, i, n + 2)
            sp.wait_ge(self.out_ready, at(q + 1))
            sp.dma_start(self.W["slot_y"].rearrange("(q r p) d -> q p r d", p=P, r=self.PAIRS)[q],
                         self.slot_out[r][:, :, :]).then_inc(self.store_dma[r], DMA)
            if self.exists(i, n + self.RING):
                self.load_weights(sp, i, n + self.RING)
                self.load_slots(sp, i, n + self.RING)

        for n in range(self.RING):
            self.load_slots(sp, 0, n)
        if self.split:
            for n in range(2):
                self.load_split(sp, 0, n)
        self.steps(sp, step)


    def pe_credits(self, pe):
        for s in (self.t_psum, self.gu_psum, self.y_psum):
            pe.sem_inc(s, CREDIT)

    def pe_steps(self, pe):
        W = self.W

        def columns(i, n):
            q = self.RING * i + n
            pe.wait_ge(self.slot_dma[n % self.RING], DMA * self.uses(i, n))
            pe.wait_ge(self.t_ready, at(q - 1))
            for r in range(self.PAIRS):
                for c in range(C):
                    mm = pe.transpose(self.ps_t[n % 2][:, r, c, :], self.slot_in[n % self.RING][:, r, c:D:C], W["ident"][:, :])
            mm.then_inc(self.t_psum, 1)

        def gate_up(i, n):
            q = self.RING * i + n
            pe.wait_ge(self.w_dma[n % self.RING], 3 * DMA * self.uses(i, n))
            pe.wait_ge(self.t_ready, at(q + 1))
            pe.wait_ge(self.hidden_ready, at(q - 1))
            settle(pe, self.passed)
            for k in range(self.QE):
                r, odd = k // 2, (k % 2) * CAP
                x = self.slot_t[n % 2][:, r, :, odd:odd + CAP]
                for s, w in enumerate((self.w_gate[n % self.RING], self.w_up[n % self.RING])):
                    for c in range(C):
                        mm = pe.matmul(self.ps_gu[n % 2][odd:odd + HID, s, r, :], w[:, k, c, :], x[:, c, :],
                                       start=(c == 0), stop=(c == C - 1))
            mm.then_inc(self.gu_psum, 1)

        def down(i, n):
            q = self.RING * i + n
            pe.wait_ge(self.hidden_ready, at(q + 1))
            pe.wait_ge(self.out_ready, at(q - 1))
            for r in range(self.PAIRS):
                mm = pe.matmul(self.ps_y[n % 2][:, r, :], self.hidden[n % 2][:, r, :], self.w_down[n % self.RING][:, r, :],
                               start=True, stop=True)
            mm.then_inc(self.y_psum, 1)

        def step(i, n):
            if self.exists(i, n + 1):
                gate_up(i, n + 1)
            if self.exists(i, n + 2):
                columns(i, n + 2)
            down(i, n)

        columns(0, 0)
        columns(0, 1)
        gate_up(0, 0)
        self.steps(pe, step)


    def act_credits(self, act):
        for s in (self.t_ready, self.tanh_ready, self.out_ready, self.split_hi):
            act.sem_inc(s, CREDIT)

    def act_steps(self, act):
        W = self.W

        def columns(i, n):
            q = self.RING * i + n
            act.wait_ge(self.t_psum, at(q + 1))
            act.wait_ge(self.gu_psum, at(q - 1))
            act.activation(self.slot_t[n % 2][:, :, :, :], self.ps_t[n % 2][:, :, :, :], ACT.Copy).then_inc(self.t_ready, 1)

        def tanh(i, n):
            q = self.RING * i + n
            act.wait_ge(self.gu_psum, at(q + 1))
            act.wait_ge(self.hidden_ready, at(q - 1))
            act.activation(self.tanh[n % 2][:, :, :], self.ps_gu[n % 2][:, 0, :, :], ACT.Tanh, scale=0.5
                           ).then_inc(self.tanh_ready, 1)

        def results(i, n):
            q = self.RING * i + n
            act.wait_ge(self.y_psum, at(q + 1))
            if not isinstance(i, int) or i > 0:
                act.wait_ge(self.store_dma[n], DMA * i)
            act.activation(self.slot_out[n][:, :, :], self.ps_y[n % 2][:, :, :], ACT.Copy).then_inc(self.out_ready, 1)

        def split(i, n):
            q = self.RING * i + n
            act.wait_ge(self.raw_dma[n % 2], 2 * DMA * (self.RING // 2 * i + n // 2 + 1))
            act.activation(W["wq"][0][:, :, bass.ds(q * DH, DH)], self.raw_q[n % 2][:, :, :], ACT.Copy)
            act.activation(W["wo"][0][:, q, :], self.raw_o[n % 2][:, :], ACT.Copy).then_inc(self.split_hi, 1)

        def step(i, n):
            if self.exists(i, n + 1):
                tanh(i, n + 1)
            if self.exists(i, n + 2):
                columns(i, n + 2)
            results(i, n)
            if self.split:
                split(i, n)

        columns(0, 0)
        columns(0, 1)
        tanh(0, 0)
        for n in range(self.RING):
            step(0, n)
        with act.Fori(1, self.QUADS // self.RING - 1) as i:
            for n in range(self.RING):
                step(i, n)
        for n in range(self.RING):
            step(self.QUADS // self.RING - 1, n)


    def dve_credits(self, dve):
        for s in (self.hidden_ready, self.split_lo):
            dve.sem_inc(s, CREDIT)
        for n in range(2):
            dve.memset(self.hidden[n][:, :, :], 0.0)

    def dve_steps(self, dve):
        W = self.W

        def hidden(i, n):
            q = self.RING * i + n
            dve.wait_ge(self.tanh_ready, at(q + 1))
            gate, up = self.ps_gu[n % 2][:, 0, :, :], self.ps_gu[n % 2][:, 1, :, :]
            dve.scalar_tensor_tensor(out=self.gate[n % 2][:, :, :], in0=self.tanh[n % 2][:, :, :], scalar=1.0, in1=gate,
                                     op0=ALU.add, op1=ALU.mult)
            dve.drain()
            dve.wait_ge(self.y_psum, at(q - 1))
            for odd in range(0, P, CAP):
                op = dve.scalar_tensor_tensor(out=self.hidden[n % 2][odd:odd + HID, :, odd:odd + CAP],
                                              in0=self.gate[n % 2][odd:odd + HID, :, :], scalar=0.5,
                                              in1=up[odd:odd + HID, :, :], op0=ALU.mult, op1=ALU.mult)
            op.then_inc(self.hidden_ready, 1)

        def split(i, n):
            q = self.RING * i + n
            dve.wait_ge(self.split_hi, at(q + 1))
            hi, lo = (w[:, :, bass.ds(q * DH, DH)] for w in W["wq"])
            dve.tensor_tensor(lo, self.raw_q[n % 2][:, :, :], hi.bitcast(F32), ALU.subtract)
            hi, lo = (w[:, q, :] for w in W["wo"])
            dve.tensor_tensor(lo, self.raw_o[n % 2][:, :], hi.bitcast(F32), ALU.subtract).then_inc(self.split_lo, 1)

        def step(i, n):
            if self.exists(i, n + 1):
                hidden(i, n + 1)
            if self.split:
                split(i, n)

        hidden(0, 0)
        self.steps(dve, step)


def ffn_phase(nc, W, a, layer):
    last_layer = layer == 1
    with ExitStack() as ctx:
        m = Memory(nc, ctx, f"ffn{layer}")
        X = W["x"]
        stats = m.sb("stats", [P, J, 6])
        moments = m.sb("moments", [P, J, 2])
        variance = m.sb("variance", [P, J])
        rstd = m.sb("rstd", [P, J])
        xn = [m.sb(f"xn{u}", [P, J, D]) for u in range(2)]
        xt = [[m.sb(f"xt{u}{part}", [P, C, S], F32R) for part in ("hi", "lo")] for u in range(2)]
        logits_t = m.sb("logits_t", [E, S])
        logits = m.sb("logits", [P, J, E])
        top = m.sb("top", [P, J, 8])
        top_at = m.sb("top_at", [P, J, 8], U32)
        expert = m.sb("expert", [P, J, K])
        below_top = m.sb("below_top", [P, J, K])
        expo = m.sb("expo", [P, J, K])
        expo_sum = m.sb("expo_sum", [P, J])
        expo_rec = m.sb("expo_rec", [P, J])
        chosen = m.sb("chosen", [P, J, K, E])
        chosen_rank = m.sb("chosen_rank", [P, J, K, E])
        mask = m.sb("mask", [P, J, E], BF16)
        mask_sum = m.sb("mask_sum", [P, E], BF16)
        rank = m.sb("rank", [P, J * K])
        rank_cut = m.sb("rank_cut", [P, J * K])
        first_slot = m.sb("first_slot", [P, J * K])
        kept = m.sb("kept", [P, J * K])
        lost = m.sb("lost", [P, J * K])
        slot_sum = m.sb("slot_sum", [P, J * K])
        scatter_at = m.sb("scatter_at", [P, J * K], U32)
        weight_raw = m.sb("weight_raw", [P, J, K])
        tanh = [m.sb(f"tanh{n}", [P, S]) for n in range(2)]
        act_gate = [m.sb(f"act_gate{n}", [P, S]) for n in range(2)]
        hidden = m.sb("hidden", [P, HC, S])
        if last_layer:
            gather_at = [m.sb(f"gather_at{u}", [P, J * K], U32) for u in range(2)]
            gathered = [m.sb(f"gathered{u}", [P, J * K, D]) for u in range(2)]
        else:
            raw_kv = m.sb("raw_kv", [P, C, KV * DH])
        ps_xt = m.ps("xt", [P, C, S])
        ps_logits_t = m.ps("logits_t", [P, 512])
        ps_route = m.ps("route", [P, 512])
        ps_gu = [m.ps(f"gate_up{n}", [P, 2, S]) for n in range(2)]
        ps_y = [m.ps(f"y{n}", [P, J, D]) for n in range(2)]
        ps_slot_t = m.ps("slot_t", [P, 2, C, P])
        experts = Experts(nc, ctx, W, a, f"experts{layer}", [ps_xt[:, :, :].rearrange("p r (c m) -> p r c m", c=C), ps_slot_t],
                          [t[:, :, :].rearrange("p s t -> p (s t)") for t in ps_gu], [t[:, :, :].rearrange("p j d -> p (j d)") for t in ps_y], split=not last_layer)
        ps_logits = ps_route[:, 0:J * E].rearrange("p (j e) -> p j e", e=E)
        ps_rank = ps_route[:, J * E:2 * J * E].rearrange("p (j e) -> p j e", e=E)

        xt_psum, logits_t_psum, logits_psum, gu_psum, rank_psum, y_psum = m.sems(
            "xt_psum logits_t_psum logits_psum gu_psum rank_psum y_psum")
        xt_hi, logits_t_out, expo_ready, tanh_ready, raw_hi = m.sems("xt_hi logits_t_out expo_ready tanh_ready raw_hi")
        var_ready, xn_ready, xt_ready, below_ready, mask_ready, slots_ready, hidden_ready, x_added, raw_lo, combined = m.sems(
            "var_ready xn_ready xt_ready below_ready mask_ready slots_ready hidden_ready x_added raw_lo combined")
        rstd_ready, scattered, index_ready, passed = m.sems("rstd_ready scattered index_ready passed")
        scatter_dma, out_dma, kv_dma = m.sems("scatter_dma out_dma kv_dma")
        gather_dma = [m.sem(f"gather_dma{u}") for u in range(2)]

        with nc.Block() as block:

            @block.sync
            def _(sp):
                if not last_layer:
                    sp.dma_start(raw_kv[:, :, :], a["L0_attn_Wk"].rearrange("(p c) n -> p c n", c=C)).then_inc(kv_dma, DMA)
                for n in range(experts.RING):
                    experts.load_weights(sp, 0, n)
                sp.wait_ge(scattered, at(NB))
                if not last_layer:
                    sp.wait_ge(raw_lo, 1)
                    sp.dma_start(raw_kv[:, :, :], a["L0_attn_Wv"].rearrange("(p c) n -> p c n", c=C)).then_inc(kv_dma, DMA)
                experts.sp_steps(sp)
                experts.stored(sp)
                if last_layer:
                    with sp.Fori(0, NB) as b:
                        sp.wait_ge(combined, at(b + 1))
                        sp.dma_start(a["out"].rearrange("b (j p) d -> b p j d", p=P)[b],
                                     X[:, b, :, :]).then_inc(out_dma, DMA)
                    sp.wait_ge(out_dma, NB * DMA)

            @block.gpsimd
            def _(pool):
                for s in (rstd_ready, scattered, index_ready):
                    pool.sem_inc(s, CREDIT)

                def inverse_deviation(b):
                    pool.wait_ge(var_ready, at(b + 1))
                    pool.tensor_tensor(rstd[:, :], variance[:, :], W["half"][:, :], ALU.pow).then_inc(rstd_ready, 1)

                def dispatch(b, u):
                    pool.wait_ge(slots_ready, at(b + 1))
                    settle(pool, passed)
                    for jk in range(J * K):
                        pool.indirect_dma_start(
                            W["slot_x"], bass.IndirectOffsetOnAxis(ap=scatter_at[:, jk:jk + 1], axis=0),
                            xn[u][:, jk // K, :], None, bounds_check=E * CAP - 1, oob_is_err=False,
                        ).then_inc(scatter_dma, DMA)
                    pool.wait_ge(scatter_dma, DMA * J * K * (b + 1))
                    pool.sem_inc(scattered, 1)

                inverse_deviation(0)
                with pool.Fori(0, NB // 2 - 1) as i:
                    for u in range(2):
                        inverse_deviation(2 * i + u + 1)
                        dispatch(2 * i + u, u)
                inverse_deviation(NB - 1)
                dispatch(NB - 2, 0)
                dispatch(NB - 1, 1)
                if last_layer:
                    experts.stored(pool)
                    with pool.Fori(0, NB // 2) as i:
                        for u in range(2):
                            b = 2 * i + u
                            pool.wait_ge(combined, at(b - 1))
                            settle(pool, passed)
                            pool.tensor_copy(gather_at[u][:, :], W["slot_of"][:, b, :]).then_inc(index_ready, 1)
                            pool.wait_ge(index_ready, at(b + 1))
                            settle(pool, passed)
                            for jk in range(J * K):
                                pool.indirect_dma_start(
                                    gathered[u][:, jk, :], None, W["slot_y"],
                                    bass.IndirectOffsetOnAxis(ap=gather_at[u][:, jk:jk + 1], axis=0),
                                ).then_inc(gather_dma[u], DMA)

            @block.tensor
            def _(pe):
                for s in (xt_psum, logits_t_psum, logits_psum, gu_psum, rank_psum, y_psum):
                    pe.sem_inc(s, CREDIT)
                experts.pe_credits(pe)

                def batch(b, u):
                    pe.wait_ge(xn_ready, at(b + 1))
                    pe.wait_ge(xt_ready, at(b))
                    for c in range(C):
                        for j in range(J):
                            mm = pe.transpose(ps_xt[:, c, j * P:(j + 1) * P], xn[u][:, j, c:D:C], W["ident"][:, :])
                    mm.then_inc(xt_psum, 1)
                    pe.wait_ge(xt_ready, at(b + 1))
                    pe.wait_ge(logits_t_out, at(b))
                    for c in range(C):
                        mm = split_product(pe, ps_logits_t[:, 0:S], [w[:, c, :] for w in W["router"]],
                                           [x[:, c, :] for x in xt[u]], c == 0, c == C - 1)
                    mm.then_inc(logits_t_psum, 1)
                    for q in range(HC):
                        pe.wait_ge(hidden_ready, at(HC * b + q - 1))
                        for n, w in enumerate((W["gate"], W["up"])):
                            for c in range(C):
                                mm = split_product(pe, ps_gu[q % 2][:, n, :], [v[:, c, q * P:(q + 1) * P] for v in w],
                                                   [x[:, c, :] for x in xt[u]], c == 0, c == C - 1)
                        mm.then_inc(gu_psum, 1)
                        if q == 0:
                            pe.wait_ge(logits_t_out, at(b + 1))
                            pe.wait_ge(slots_ready, at(b))
                            settle(pe, passed)
                            for j in range(J):
                                mm = pe.transpose(ps_logits[:, j, :], logits_t[:, j * P:(j + 1) * P], W["ident"][0:E, 0:E])
                            mm.then_inc(logits_psum, 1)
                        if q == 2:
                            pe.wait_ge(mask_ready, at(b + 1))
                            for j in range(J):
                                pe.matmul(ps_rank[:, j, :], W["ones"][:, :], mask_sum[:, :], start=True, stop=False)
                                for k in range(j):
                                    pe.matmul(ps_rank[:, j, :], W["ones"][:, :], mask[:, k, :], start=False, stop=False)
                                mm = pe.matmul(ps_rank[:, j, :], W["before"][:, :], mask[:, j, :], start=False, stop=True)
                            mm.then_inc(rank_psum, 1)
                    pe.wait_ge(hidden_ready, at(HC * (b + 1)))
                    pe.wait_ge(x_added, at(b))
                    for j in range(J):
                        for q in range(HC):
                            mm = pe.matmul(ps_y[0][:, j, :], hidden[:, q, j * P:(j + 1) * P],
                                           W["shared_down"][:, q, :], start=(q == 0), stop=(q == HC - 1))
                    mm.then_inc(y_psum, 1)

                with pe.Fori(0, NB // 2) as i:
                    for u in range(2):
                        batch(2 * i + u, u)

                pe.wait_ge(x_added, at(NB))
                experts.pe_steps(pe)

            @block.scalar
            def _(act):
                for s in (xt_hi, logits_t_out, expo_ready, tanh_ready):
                    act.sem_inc(s, CREDIT)
                experts.act_credits(act)

                def tanh_of_gate(b, q):
                    act.wait_ge(gu_psum, at(HC * b + q + 1))
                    act.wait_ge(hidden_ready, at(HC * b + q - 1))
                    act.activation(tanh[q % 2][:, :], ps_gu[q % 2][:, 0, :], ACT.Tanh, scale=0.5).then_inc(tanh_ready, 1)

                def batch(b, u):
                    act.wait_ge(xt_psum, at(b + 1))
                    act.activation(xt[u][0][:, :, :], ps_xt[:, :, :], ACT.Copy).then_inc(xt_hi, 1)
                    act.wait_ge(logits_t_psum, at(b + 1))
                    act.wait_ge(logits_psum, at(b))
                    act.activation(logits_t[:, :], ps_logits_t[0:E, 0:S], ACT.Identity,
                                   bias=W["bias"][0:E, 24:25]).then_inc(logits_t_out, 1)
                    tanh_of_gate(b, 0)
                    tanh_of_gate(b, 1)
                    act.wait_ge(below_ready, at(b + 1))
                    act.activation(expo[:, :, :], below_top[:, :, :], ACT.Exp).then_inc(expo_ready, 1)
                    tanh_of_gate(b, 2)
                    tanh_of_gate(b, 3)

                with act.Fori(0, NB // 2) as i:
                    for u in range(2):
                        batch(2 * i + u, u)

                if not last_layer:
                    for n, w in enumerate((W["wk"], W["wv"])):
                        act.wait_ge(kv_dma, DMA * (n + 1))
                        act.activation(w[0][:, :, :], raw_kv[:, :, :], ACT.Copy).then_inc(raw_hi, 1)
                experts.act_steps(act)

            @block.vector
            def _(dve):
                for s in (var_ready, xn_ready, xt_ready, below_ready, mask_ready, slots_ready, hidden_ready, x_added,
                          combined):
                    dve.sem_inc(s, CREDIT)
                experts.dve_credits(dve)

                def moments_of(b):
                    for j in range(J):
                        dve.bn_stats(stats[:, j, :], X[:, b, j, :])
                    dve.drain()
                    for j in range(J):
                        dve.bn_aggr(moments[:, j, :], stats[:, j, :])
                    dve.drain()
                    dve.tensor_scalar(variance[:, :], moments[:, :, 1], EPS, None, ALU.add).then_inc(var_ready, 1)

                def normalise(b, u):
                    dve.wait_ge(rstd_ready, at(b + 1))
                    dve.wait_ge(scattered, at(b - 1))
                    for j in range(J):
                        op = dve.tensor_scalar(xn[u][:, j, :], X[:, b, j, :], moments[:, j, 0:1], rstd[:, j:j + 1],
                                               ALU.subtract, ALU.mult)
                    op.then_inc(xn_ready, 1)

                def hidden_chunk(b, q):
                    dve.wait_ge(tanh_ready, at(HC * b + q + 1))
                    dve.scalar_tensor_tensor(out=act_gate[q % 2][:, :], in0=tanh[q % 2][:, :], scalar=1.0,
                                             in1=ps_gu[q % 2][:, 0, :], op0=ALU.add, op1=ALU.mult)
                    dve.drain()
                    dve.tensor_tensor(hidden[:, q, :], act_gate[q % 2][:, :], ps_gu[q % 2][:, 1, :], ALU.mult).then_inc(hidden_ready, 1)

                def choose(b):
                    dve.wait_ge(logits_psum, at(b + 1))
                    dve.tensor_copy(logits[:, :, :], ps_logits)
                    dve.drain()
                    for j in range(J):
                        dve.max(top[:, j, :], logits[:, j, :])
                    dve.drain()
                    for j in range(J):
                        dve.max_index(top_at[:, j, :], top[:, j, :], logits[:, j, :])
                    dve.tensor_tensor(below_top[:, :, :], top[:, :, 0:K], top[:, :, 0:1].to_broadcast([P, J, K]),
                                      ALU.subtract).then_inc(below_ready, 1)
                    dve.drain()
                    dve.tensor_copy(expert[:, :, :], top_at[:, :, 0:K])
                    dve.drain()
                    for j in range(J):
                        dve.tensor_tensor(chosen[:, j, :, :], W["expert_of"][:, :].unsqueeze(1).to_broadcast([P, K, E]),
                                          expert[:, j, :].unsqueeze(2).to_broadcast([P, K, E]), ALU.is_equal)
                    dve.tensor_scalar(first_slot[:, :], expert[:, :, :].rearrange("p j k -> p (j k)"), float(CAP), None, ALU.mult)
                    dve.drain()
                    with nc.allow_low_precision("counts of at most K"):
                        dve.tensor_reduce(mask[:, :, :], chosen[:, :, :, :].rearrange("p j k e -> p j e k"), AX.X,
                                          ALU.add).then_inc(mask_ready, 1)

                def place(b):
                    dve.wait_ge(rank_psum, at(b + 1))
                    for j in range(J):
                        dve.tensor_tensor(chosen_rank[:, j, :, :], chosen[:, j, :, :],
                                          ps_rank[:, j, :].unsqueeze(1).to_broadcast([P, K, E]), ALU.mult)
                    dve.tensor_tensor(mask_sum[:, :], mask_sum[:, :], mask[:, 0, :], ALU.add)
                    dve.drain()
                    dve.tensor_tensor(mask_sum[:, :], mask_sum[:, :], mask[:, 1, :], ALU.add)
                    dve.tensor_reduce(rank[:, :], chosen_rank[:, :, :, :].rearrange("p j k e -> p (j k) e"), AX.X, ALU.add)
                    dve.wait_ge(expo_ready, at(b + 1))
                    dve.tensor_reduce(expo_sum[:, :], expo[:, :, :], AX.X, ALU.add)
                    dve.drain()
                    dve.reciprocal(expo_rec[:, :], expo_sum[:, :])
                    dve.tensor_scalar(rank_cut[:, :], rank[:, :], float(CAP - 1), None, ALU.min)
                    dve.tensor_scalar(kept[:, :], rank[:, :], float(CAP), 0.5, ALU.is_lt, ALU.mult)
                    dve.tensor_scalar(lost[:, :], rank[:, :], float(CAP), float(DROPPED), ALU.is_ge, ALU.mult)
                    dve.tensor_tensor(slot_sum[:, :], rank[:, :], first_slot[:, :], ALU.add)
                    dve.drain()
                    dve.wait_ge(scattered, at(b))
                    dve.tensor_tensor(scatter_at[:, :], slot_sum[:, :], lost[:, :], ALU.add).then_inc(slots_ready, 1)
                    dve.tensor_tensor(W["slot_of"][:, b, :], rank_cut[:, :], first_slot[:, :], ALU.add)
                    dve.tensor_tensor(weight_raw[:, :, :], expo[:, :, :], expo_rec[:, :].unsqueeze(2).to_broadcast([P, J, K]), ALU.mult)
                    dve.drain()
                    dve.tensor_tensor(W["weight"][:, b, :], weight_raw[:, :, :].rearrange("p j k -> p (j k)"),
                                      kept[:, :], ALU.mult)

                def batch(b, u, has_next):
                    dve.wait_ge(xt_hi, at(b + 1))
                    dve.tensor_tensor(xt[u][1][:, :, :], ps_xt[:, :, :], xt[u][0][:, :, :].bitcast(F32),
                                      ALU.subtract).then_inc(xt_ready, 1)
                    hidden_chunk(b, 0)
                    choose(b)
                    hidden_chunk(b, 1)
                    if has_next:
                        moments_of(b + 1)
                    hidden_chunk(b, 2)
                    place(b)
                    hidden_chunk(b, 3)
                    if has_next:
                        normalise(b + 1, 1 - u)
                    dve.wait_ge(y_psum, at(b + 1))
                    dve.scalar_tensor_tensor(out=X[:, b, :, :], in0=ps_y[0][:, :, :], scalar=0.25, in1=X[:, b, :, :],
                                             op0=ALU.mult, op1=ALU.add).then_inc(x_added, 1)

                dve.memset(mask_sum[:, :], 0.0)
                moments_of(0)
                normalise(0, 0)
                with dve.Fori(0, NB // 2 - 1) as i:
                    for u in range(2):
                        batch(2 * i + u, u, True)
                batch(NB - 2, 0, True)
                batch(NB - 1, 1, False)

                if not last_layer:
                    for n, w in enumerate((W["wk"], W["wv"])):
                        dve.wait_ge(raw_hi, n + 1)
                        dve.tensor_tensor(w[1][:, :, :], raw_kv[:, :, :], w[0][:, :, :].bitcast(F32), ALU.subtract).then_inc(raw_lo, 1)
                experts.dve_steps(dve)
                if last_layer:
                    with dve.Fori(0, NB // 2) as i:
                        for u in range(2):
                            dve.wait_ge(gather_dma[u], DMA * J * K * (i + 1))
                            combine(dve, X, W, gathered[u], 2 * i + u, combined)


def combine(dve, X, W, gathered, b, done):
    for k in range(K):
        for j in range(J):
            op = dve.scalar_tensor_tensor(out=X[:, b, j, :], in0=gathered[:, j * K + k, :],
                                          scalar=W["weight"][:, b, j * K + k:j * K + k + 1], in1=X[:, b, j, :],
                                          op0=ALU.mult, op1=ALU.add)
        if k < K - 1:
            dve.drain()
    op.then_inc(done, 1)


def attention_phase(nc, W, a):
    HEADS = NB * H
    with ExitStack() as ctx:
        m = Memory(nc, ctx, "attn")
        X = W["x"]
        stats = m.sb("stats", [P, J, 6])
        moments = m.sb("moments", [P, J, 2])
        variance = m.sb("variance", [P, J])
        rstd = m.sb("rstd", [P, J])
        xn = m.sb("xn", [P, J, D])
        gather_at = m.sb("gather_at", [P, J * K], U32)
        gathered = m.sb("gathered", [P, J * K, D])

        def halves(name, shape):
            return [m.sb(f"{name}_{part}", shape, F32R) for part in ("hi", "lo")]

        xt = [halves(f"xt{u}", [P, C, S]) for u in range(2)]
        keys = [halves(f"keys{u}", [P, KV, S]) for u in range(2)]
        vals = [halves(f"vals{u}", [P, J, KV * DH]) for u in range(2)]
        qt = [halves(f"qt{n}", [P, S]) for n in range(2)]
        prob = [m.sb(f"prob{n}", [P, J, S]) for n in range(2)]
        prob_t = [halves(f"prob_t{n}", [P, J, S]) for n in range(2)]
        ot = [halves(f"ot{n}", [P, S]) for n in range(2)]
        row_max = m.sb("row_max", [P, J])
        neg_max = [m.sb(f"neg_max{n}", [P, J]) for n in range(2)]
        row_sum = [m.sb(f"row_sum{n}", [P, J]) for n in range(2)]
        row_rec = m.sb("row_rec", [P, J])

        ps_prep = m.ps("prep", [P, 512])
        ps_q = m.ps("q", [P, 512])
        ps_s = [m.ps(f"s{n}", [P, J, S]) for n in range(2)]
        ps_pt = [m.ps(f"pt{n}", [P, J, S]) for n in range(2)]
        ps_o = m.ps("o", [P, 512])
        ps_y = m.ps("y", [P, J, D])

        q_psum, s_psum, pt_psum, o_psum, y_psum, xt_psum, k_psum, v_psum = m.sems(
            "q_psum s_psum pt_psum o_psum y_psum xt_psum k_psum v_psum")
        q_hi, exp_ready, pt_hi, o_hi, xt_hi, k_hi, v_hi = m.sems("q_hi exp_ready pt_hi o_hi xt_hi k_hi v_hi")
        q_ready, max_ready, p_ready, pt_ready, o_ready, xt_ready, k_ready, v_ready, x_added, var_ready, xn_ready, combined = m.sems(
            "q_ready max_ready p_ready pt_ready o_ready xt_ready k_ready v_ready x_added var_ready xn_ready combined")
        rstd_ready, index_ready, gather_dma, passed = m.sems("rstd_ready index_ready gather_dma passed")

        LOOPS = NB // 2 - 1
        TWO = 2 * H

        def exists(i, c):
            return not isinstance(i, int) or 0 <= TWO * i + c < HEADS

        def next_batch(i, u):
            return not isinstance(i, int) or 2 * i + u + 1 < NB

        def bias(first, n):
            return W["bias"][:, first + n:first + n + 1]

        COMBINE, MOMENTS, NORMALISE, COLUMNS, KEYS, VALUES = 1, 3, 4, 5, 6, 10

        with nc.Block() as block:

            @block.gpsimd
            def _(pool):
                for s in (rstd_ready, index_ready):
                    pool.sem_inc(s, CREDIT)

                def fetch(b):
                    pool.wait_ge(combined, at(b))
                    settle(pool, passed)
                    pool.tensor_copy(gather_at[:, :], W["slot_of"][:, b, :]).then_inc(index_ready, 1)
                    pool.wait_ge(index_ready, at(b + 1))
                    settle(pool, passed)
                    for jk in range(J * K):
                        pool.indirect_dma_start(
                            gathered[:, jk, :], None, W["slot_y"],
                            bass.IndirectOffsetOnAxis(ap=gather_at[:, jk:jk + 1], axis=0),
                        ).then_inc(gather_dma, DMA)
                    pool.wait_ge(var_ready, at(b + 1))
                    pool.tensor_tensor(rstd[:, :], variance[:, :], W["half"][:, :], ALU.pow).then_inc(rstd_ready, 1)

                with pool.Fori(0, NB) as b:
                    fetch(b)

            @block.tensor
            def _(pe):
                for s in (q_psum, s_psum, pt_psum, o_psum, y_psum, xt_psum, k_psum, v_psum):
                    pe.sem_inc(s, CREDIT)

                def columns(b):
                    pe.wait_ge(xn_ready, at(b + 1))
                    pe.wait_ge(v_ready, at(J * b))
                    for c in range(C):
                        for j in range(J):
                            mm = pe.transpose(ps_prep[:, c * S + j * P:c * S + (j + 1) * P], xn[:, j, c:D:C], W["ident"][:, :])
                    mm.then_inc(xt_psum, 1)

                def key_group(b, u, g):
                    pe.wait_ge(xt_ready, at(b + 1))
                    pe.wait_ge(k_ready, at(KV * b + g))
                    for c in range(C):
                        mm = split_product(pe, ps_prep[:, 0:S], [w[:, c, g * DH:(g + 1) * DH] for w in W["wk"]],
                                           [x[:, c, :] for x in xt[u]], c == 0, c == C - 1)
                    mm.then_inc(k_psum, 1)

                def value_tile(b, u, j):
                    pe.wait_ge(k_ready, at(KV * (b + 1)))
                    pe.wait_ge(v_ready, at(J * b + j))
                    for c in range(C):
                        mm = split_product(pe, ps_prep[:, :], [x[:, c, j * P:(j + 1) * P] for x in xt[u]],
                                           [w[:, c, :] for w in W["wv"]], c == 0, c == C - 1)
                    mm.then_inc(v_psum, 1)

                def prepare(b, u, h):
                    if h == COLUMNS:
                        columns(b)
                    if KEYS <= h < KEYS + KV:
                        key_group(b, u, h - KEYS)
                    if VALUES <= h < VALUES + J:
                        value_tile(b, u, h - VALUES)

                def queries(i, c):
                    k, u, h = TWO * i + c, c // H % 2, c % H
                    pe.wait_ge(q_ready, at(k))
                    if h == 0:
                        pe.wait_ge(xt_ready, at(2 * i + c // H + 1))
                    for d in range(C):
                        mm = split_product(pe, ps_q[:, 0:S], [w[:, d, h * DH:(h + 1) * DH] for w in W["wq"]],
                                           [x[:, d, :] for x in xt[u]], d == 0, d == C - 1)
                    mm.then_inc(q_psum, 1)

                def scores(i, c):
                    k, u, h = TWO * i + c, c // H % 2, c % H
                    pe.wait_ge(q_ready, at(k + 1))
                    pe.wait_ge(exp_ready, at(k - 1))
                    if h == 0:
                        pe.wait_ge(k_ready, at(KV * (2 * i + c // H + 1)))
                    for j in range(J):
                        mm = split_product(pe, ps_s[c % 2][:, j, :], [x[:, j * P:(j + 1) * P] for x in qt[c % 2]],
                                           [x[:, h // GROUP, :] for x in keys[u]], True, True)
                    mm.then_inc(s_psum, 1)

                def transposes(i, c):
                    k = TWO * i + c
                    pe.wait_ge(p_ready, at(k + 1))
                    pe.wait_ge(pt_ready, at(k - 1))
                    for t in range(J):
                        for j in range(J):
                            mm = pe.transpose(ps_pt[c % 2][:, t, j * P:(j + 1) * P], prob[c % 2][:, j, t * P:(t + 1) * P],
                                              W["ident"][:, :])
                    mm.then_inc(pt_psum, 1)

                def values(i, c):
                    k, u, h = TWO * i + c, c // H % 2, c % H
                    g = h // GROUP
                    pe.wait_ge(pt_ready, at(k + 1))
                    pe.wait_ge(o_ready, at(k))
                    if h == 0:
                        pe.wait_ge(v_ready, at(J * (2 * i + c // H + 1)))
                    for t in range(J):
                        mm = split_product(pe, ps_o[:, 0:S], [v[:, t, g * DH:(g + 1) * DH] for v in vals[u]],
                                           [x[:, t, :] for x in prob_t[c % 2]], t == 0, t == J - 1)
                    mm.then_inc(o_psum, 1)

                def outputs(i, c):
                    k, h = TWO * i + c, c % H
                    pe.wait_ge(o_ready, at(k + 1))
                    if h == 0:
                        pe.wait_ge(x_added, at(2 * i + c // H))
                    for j in range(J):
                        left = [x[:, j * P:(j + 1) * P] for x in ot[c % 2]]
                        right = [w[:, h, :] for w in W["wo"]]
                        for n, (l, r) in enumerate(((left[1], right[0]), (left[0], right[1]), (left[0], right[0]))):
                            mm = pe.matmul(ps_y[:, j, :], l, r, start=(h == 0 and j == 0 and n == 0),
                                           stop=(h == H - 1 and n == 2), skip_group_check=True)
                    mm.then_inc(y_psum, 1)

                def step(i, c):
                    if exists(i, c + 3):
                        scores(i, c + 3)
                    if exists(i, c + 4):
                        queries(i, c + 4)
                    if exists(i, c):
                        outputs(i, c)
                    if exists(i, c + 1):
                        values(i, c + 1)
                    if exists(i, c + 2):
                        transposes(i, c + 2)
                    if c >= 0 and next_batch(i, c // H):
                        prepare(2 * i + c // H + 1, 1 - c // H, c % H)

                for h in range(H):
                    prepare(0, 0, h)
                for c in range(-4, 0):
                    step(0, c)
                with pe.Fori(0, LOOPS) as i:
                    for c in range(TWO):
                        step(i, c)
                for c in range(TWO):
                    step(LOOPS, c)

            @block.scalar
            def _(act):
                for s in (q_hi, exp_ready, pt_hi, o_hi, xt_hi, k_hi, v_hi):
                    act.sem_inc(s, CREDIT)

                def prepare(b, u, h):
                    if h == COLUMNS:
                        act.wait_ge(xt_psum, at(b + 1))
                        act.activation(xt[u][0][:, :, :], ps_prep[:, :].rearrange("p (c s) -> p c s", c=C), ACT.Copy).then_inc(xt_hi, 1)
                    if KEYS <= h < KEYS + KV:
                        g = h - KEYS
                        act.wait_ge(k_psum, at(KV * b + g + 1))
                        act.activation(keys[u][0][:, g, :], ps_prep[:, 0:S], ACT.Identity, bias=bias(H, g)).then_inc(k_hi, 1)
                    if VALUES <= h < VALUES + J:
                        j = h - VALUES
                        act.wait_ge(v_psum, at(J * b + j + 1))
                        act.activation(vals[u][0][:, j, :], ps_prep[:, :], ACT.Copy).then_inc(v_hi, 1)

                def queries(i, c):
                    k = TWO * i + c
                    act.wait_ge(q_psum, at(k + 1))
                    act.wait_ge(s_psum, at(k - 1))
                    act.activation(qt[c % 2][0][:, :], ps_q[:, 0:S], ACT.Identity, bias=bias(0, c % H)).then_inc(q_hi, 1)

                def exponentials(i, c):
                    k = TWO * i + c
                    act.wait_ge(max_ready, at(k + 1))
                    act.wait_ge(pt_psum, at(k - 1))
                    for j in range(J):
                        op = act.activation(prob[c % 2][:, j, :], ps_s[c % 2][:, j, :], ACT.Exp, scale=SCALE,
                                            bias=neg_max[c % 2][:, j:j + 1], accum_out=row_sum[c % 2][:, j:j + 1])
                    op.then_inc(exp_ready, 1)

                def transposed(i, c):
                    k = TWO * i + c
                    act.wait_ge(pt_psum, at(k + 1))
                    act.wait_ge(o_psum, at(k - 1))
                    act.activation(prob_t[c % 2][0][:, :, :], ps_pt[c % 2][:, :, :], ACT.Copy).then_inc(pt_hi, 1)

                def outputs(i, c):
                    k = TWO * i + c
                    act.wait_ge(o_psum, at(k + 1))
                    act.wait_ge(y_psum, at(k - 1))
                    act.activation(ot[c % 2][0][:, :], ps_o[:, 0:S], ACT.Identity, bias=bias(H + KV, c % H // GROUP)).then_inc(o_hi, 1)

                def step(i, c):
                    if exists(i, c + 1):
                        transposed(i, c + 1)
                    if exists(i, c + 4):
                        queries(i, c + 4)
                    if exists(i, c + 3):
                        exponentials(i, c + 3)
                    if exists(i, c + 1):
                        outputs(i, c + 1)
                    if c >= 0 and next_batch(i, c // H):
                        prepare(2 * i + c // H + 1, 1 - c // H, c % H)

                for h in range(H):
                    prepare(0, 0, h)
                for c in range(-4, 0):
                    step(0, c)
                with act.Fori(0, LOOPS) as i:
                    for c in range(TWO):
                        step(i, c)
                for c in range(TWO):
                    step(LOOPS, c)

            @block.vector
            def _(dve):
                for s in (q_ready, max_ready, p_ready, pt_ready, o_ready, xt_ready, k_ready, v_ready, x_added,
                          var_ready, xn_ready, combined):
                    dve.sem_inc(s, CREDIT)

                def prepare(b, u, h):
                    if h == COMBINE:
                        dve.wait_ge(gather_dma, DMA * J * K * (b + 1))
                        combine(dve, X, W, gathered, b, combined)
                    if h == MOMENTS:
                        dve.drain()
                        for j in range(J):
                            dve.bn_stats(stats[:, j, :], X[:, b, j, :])
                        dve.drain()
                        for j in range(J):
                            dve.bn_aggr(moments[:, j, :], stats[:, j, :])
                        dve.drain()
                        dve.tensor_scalar(variance[:, :], moments[:, :, 1], EPS, None, ALU.add).then_inc(var_ready, 1)
                    if h == NORMALISE:
                        dve.wait_ge(rstd_ready, at(b + 1))
                        dve.wait_ge(xt_psum, at(b))
                        for j in range(J):
                            op = dve.tensor_scalar(xn[:, j, :], X[:, b, j, :], moments[:, j, 0:1], rstd[:, j:j + 1],
                                                   ALU.subtract, ALU.mult)
                        op.then_inc(xn_ready, 1)
                        dve.drain()
                        dve.tensor_tensor(X[:, b, :, :], X[:, b, :, :], W["bo"][:, :].unsqueeze(1).to_broadcast([P, J, D]), ALU.add)
                    if h == COLUMNS:
                        dve.wait_ge(xt_hi, at(b + 1))
                        dve.tensor_tensor(xt[u][1][:, :, :], ps_prep[:, :].rearrange("p (c s) -> p c s", c=C),
                                          xt[u][0][:, :, :].bitcast(F32), ALU.subtract).then_inc(xt_ready, 1)
                    if KEYS <= h < KEYS + KV:
                        g = h - KEYS
                        dve.wait_ge(k_hi, at(KV * b + g + 1))
                        dve.scalar_tensor_tensor(out=keys[u][1][:, g, :], in0=ps_prep[:, 0:S], scalar=bias(H, g),
                                                 in1=keys[u][0][:, g, :].bitcast(F32), op0=ALU.add,
                                                 op1=ALU.subtract).then_inc(k_ready, 1)
                    if VALUES <= h < VALUES + J:
                        j = h - VALUES
                        dve.wait_ge(v_hi, at(J * b + j + 1))
                        dve.tensor_tensor(vals[u][1][:, j, :], ps_prep[:, :], vals[u][0][:, j, :].bitcast(F32),
                                          ALU.subtract).then_inc(v_ready, 1)

                def maxima(i, c):
                    k = TWO * i + c
                    dve.wait_ge(s_psum, at(k + 1))
                    dve.tensor_reduce(row_max[:, :], ps_s[c % 2][:, :, :], AX.X, ALU.max)
                    dve.drain()
                    dve.wait_ge(exp_ready, at(k - 1))
                    dve.tensor_scalar(neg_max[c % 2][:, :], row_max[:, :], -SCALE, None, ALU.mult).then_inc(max_ready, 1)

                def transposed(i, c):
                    k = TWO * i + c
                    dve.wait_ge(pt_hi, at(k + 1))
                    dve.tensor_tensor(prob_t[c % 2][1][:, :, :], ps_pt[c % 2][:, :, :],
                                      prob_t[c % 2][0][:, :, :].bitcast(F32), ALU.subtract).then_inc(pt_ready, 1)

                def queries(i, c):
                    k = TWO * i + c
                    dve.wait_ge(q_hi, at(k + 1))
                    dve.scalar_tensor_tensor(out=qt[c % 2][1][:, :], in0=ps_q[:, 0:S], scalar=bias(0, c % H),
                                             in1=qt[c % 2][0][:, :].bitcast(F32), op0=ALU.add,
                                             op1=ALU.subtract).then_inc(q_ready, 1)

                def normalised(i, c):
                    k = TWO * i + c
                    dve.wait_ge(exp_ready, at(k + 1))
                    dve.reciprocal(row_rec[:, :], row_sum[c % 2][:, :])
                    dve.drain()
                    for j in range(J):
                        op = dve.tensor_scalar(prob[c % 2][:, j, :], prob[c % 2][:, j, :], row_rec[:, j:j + 1], None, ALU.mult)
                    op.then_inc(p_ready, 1)

                def outputs(i, c):
                    k = TWO * i + c
                    dve.wait_ge(o_hi, at(k + 1))
                    dve.scalar_tensor_tensor(out=ot[c % 2][1][:, :], in0=ps_o[:, 0:S], scalar=bias(H + KV, c % H // GROUP),
                                             in1=ot[c % 2][0][:, :].bitcast(F32), op0=ALU.add,
                                             op1=ALU.subtract).then_inc(o_ready, 1)

                def step(i, c):
                    if exists(i, c + 1):
                        transposed(i, c + 1)
                    if exists(i, c + 3):
                        maxima(i, c + 3)
                    if exists(i, c + 4):
                        queries(i, c + 4)
                    if exists(i, c + 3):
                        normalised(i, c + 3)
                    if exists(i, c + 1):
                        outputs(i, c + 1)
                    if c >= 0 and next_batch(i, c // H):
                        prepare(2 * i + c // H + 1, 1 - c // H, c % H)
                    if c >= 0 and c % H == H - 1:
                        b = 2 * i + c // H
                        dve.wait_ge(y_psum, at(H * (b + 1)))
                        dve.tensor_tensor(X[:, b, :, :], ps_y[:, :, :], X[:, b, :, :], ALU.add).then_inc(x_added, 1)

                for h in range(H):
                    prepare(0, 0, h)
                for c in range(-4, 0):
                    step(0, c)
                with dve.Fori(0, LOOPS) as i:
                    for c in range(TWO):
                        step(i, c)
                for c in range(TWO):
                    step(LOOPS, c)


def macaron(nc, a):
    with ExitStack() as ctx:
        m = Memory(nc, ctx, "all")

        def halves(name, shape, m=m):
            return [m.sb(f"{name}_{part}", shape, F32R) for part in ("hi", "lo")]

        W = {
            "x": m.sb("x", [P, NB, J, D]),
            "gate": halves("gate", [P, C, HS]),
            "up": halves("up", [P, C, HS]),
            "router": halves("router", [P, C, P]),
            "shared_down": m.sb("shared_down", [P, HC, D]),
            "bo": m.sb("bo", [P, D]),
            "bias": m.sb("bias", [P, 25]),
            "ident": m.sb("ident", [P, P]),
            "before": m.sb("before", [P, P], BF16),
            "ones": m.sb("ones", [P, P], BF16),
            "expert_of": m.sb("expert_of", [P, E]),
            "half": m.sb("half", [P, J]),
            "slot_of": m.sb("slot_of", [P, NB, J * K], U32),
            "weight": m.sb("weight", [P, NB, J * K]),
            "slot_x": nc.dram_tensor("slot_x", (E * CAP, D), F32, kind="Internal").ap(),
            "slot_y": nc.dram_tensor("slot_y", (E * CAP, D), F32, kind="Internal").ap(),
        }
        with ExitStack() as until_attention:
            m_attn = Memory(nc, until_attention, "all")
            for name, shape in (("wq", [P, C, H * DH]), ("wk", [P, C, KV * DH]), ("wv", [P, C, KV * DH]), ("wo", [P, H, D])):
                W[name] = halves(name, shape, m_attn)
            setup_phase(nc, W, a)
            ffn_phase(nc, W, a, 0)
            attention_phase(nc, W, a)
        ffn_phase(nc, W, a, 1)


_INS = ["L0_attn_x", "L0_attn_Wq", "L0_attn_bq", "L0_attn_Wk", "L0_attn_bk", "L0_attn_Wv", "L0_attn_bv", "L0_attn_Wo",
        "L0_attn_bo", "L0_ffn_Wr", "L0_ffn_router_bias", "L0_ffn_Wg", "L0_ffn_Wu", "L0_ffn_Wd", "L0_ffn_Sg", "L0_ffn_Su",
        "L0_ffn_Sd"]


def kernel(**inputs):
    import numpy as _np
    import concourse.bacc as _bacc
    from concourse.bass_utils import run_bass_kernel_spmd as _run

    nc = _bacc.Bacc("TRN2", target_bir_lowering=False, num_devices=1)
    arrays, args = {}, {}
    for name in _INS:
        x = _np.ascontiguousarray(inputs[name])
        arrays[f"in_{name}"] = x
        args[name] = nc.dram_tensor(f"in_{name}", x.shape, mybir.dt.from_np(x.dtype), kind="ExternalInput").ap()
    args["out"] = nc.dram_tensor("out_0", arrays["in_L0_attn_x"].shape, F32, kind="ExternalOutput").ap()
    macaron(nc, args)
    r = _run(nc, [arrays], core_ids=[0])
    return r.results[0]["out_0"]
```

```python
from contextlib import ExitStack

import concourse.bass as bass
from concourse import mybir

F32 = mybir.dt.float32
F32R = mybir.dt.float32r
BF16 = mybir.dt.bfloat16
U32 = mybir.dt.uint32
ALU = mybir.AluOpType
ACT = mybir.ActivationFunctionType
AX = mybir.AxisListType

P = 128
D = 256
C = D // P
NB = 8
S = 256
J = S // P
H, DH, KV = 16, 128, 4
GROUP = H // KV
E, K, HID, CAP = 64, 4, 64, 64
HS = 512
HC = HS // P
SCALE = float(DH) ** -0.5
EPS = 1e-5
DROPPED = 8192
CREDIT = 2
DMA = 16


def at(n):
    return n + CREDIT


def settle(engine, passed):
    engine.sem_inc(passed, 1)


def split_product(pe, out, left, right, start, stop):
    pe.matmul(out, left[1], right[0], start=start, stop=False)
    pe.matmul(out, left[0], right[1], start=False, stop=False)
    return pe.matmul(out, left[0], right[0], start=False, stop=stop)


class Memory:

    def __init__(self, nc, ctx, phase):
        self.nc, self.ctx, self.phase = nc, ctx, phase

    def sb(self, name, shape, dt=F32):
        return self.ctx.enter_context(self.nc.sbuf_tensor(f"{self.phase}_{name}", shape, dt))

    def ps(self, name, shape, dt=F32):
        return self.ctx.enter_context(self.nc.psum_tensor(f"{self.phase}_ps_{name}", shape, dt))

    def sem(self, name):
        return self.nc.alloc_semaphore(f"{self.phase}_{name}")

    def sems(self, names):
        return [self.sem(n) for n in names.split()]


def setup_phase(nc, W, a):
    with ExitStack() as ctx:
        m = Memory(nc, ctx, "setup")
        raw_gate = m.sb("raw_gate", [P, C, HS])
        raw_up = m.sb("raw_up", [P, C, HS])
        raw_router = m.sb("raw_router", [P, C, P])
        bias_rows = m.sb("bias_rows", [25, P])
        zeros = m.sb("zeros", [P, 8 * D])
        bias_cols = m.ps("bias_cols", [P, 512])
        made, filled, x_in, w_in, b_in, zero_out, cols_done, hi_done, lo_done, pool_done = m.sems(
            "made filled x_in w_in b_in zero_out cols_done hi_done lo_done pool_done")
        with nc.Block() as block:

            @block.sync
            def _(sp):
                sp.dma_start(W["x"][:, :, :, :], a["L0_attn_x"].rearrange("b (j p) d -> p b j d", p=P)).then_inc(x_in, DMA)
                for s in range(2):
                    half = HS // 2
                    sp.dma_start(raw_gate[:, :, s * half:(s + 1) * half],
                                 a["L0_ffn_Sg"][s].rearrange("(p c) h -> p c h", c=C)).then_inc(w_in, DMA)
                    sp.dma_start(raw_up[:, :, s * half:(s + 1) * half],
                                 a["L0_ffn_Su"][s].rearrange("(p c) h -> p c h", c=C)).then_inc(w_in, DMA)
                sp.dma_start(W["shared_down"][:, :, :],
                             a["L0_ffn_Sd"].rearrange("s (q p) d -> p (s q) d", p=P)).then_inc(w_in, DMA)
                sp.dma_start(W["bo"][:, :], a["L0_attn_bo"].partition_broadcast(P)).then_inc(w_in, DMA)
                sp.wait_ge(filled, 1)
                sp.dma_start(raw_router[:, :, 0:E], a["L0_ffn_Wr"].rearrange("(p c) e -> p c e", c=C)).then_inc(w_in, DMA)
                sp.dma_start(bias_rows[0:16, :], a["L0_attn_bq"].rearrange("(h p) -> h p", p=P)).then_inc(b_in, DMA)
                sp.dma_start(bias_rows[16:20, :], a["L0_attn_bk"].rearrange("(h p) -> h p", p=P)).then_inc(b_in, DMA)
                sp.dma_start(bias_rows[20:24, :], a["L0_attn_bv"].rearrange("(h p) -> h p", p=P)).then_inc(b_in, DMA)
                sp.dma_start(bias_rows[24:25, 0:E], a["L0_ffn_router_bias"].rearrange("(h p) -> h p", p=E)).then_inc(b_in, DMA)
                slots = W["slot_x"].rearrange("(p r) d -> p (r d)", p=P)
                for n in range(4):
                    sp.dma_start(slots[:, n * 8 * D:(n + 1) * 8 * D], zeros[:, :]).then_inc(zero_out, DMA)
                sp.wait_ge(x_in, DMA)
                sp.wait_ge(zero_out, 4 * DMA)

            @block.gpsimd
            def _(pool):
                pool.memset(W["ident"][:, :], 0.0).then_inc(pool_done, 1)
                pool.memset(W["before"][:, :], 1.0).then_inc(pool_done, 1)
                pool.memset(W["ones"][:, :], 1.0)
                pool.memset(W["half"][:, :], -0.5)
                pool.iota(W["first_slot_of"][:, :], pattern=[[CAP, E]], base=0, channel_multiplier=0,
                          allow_small_or_imprecise_dtypes=True)
                pool.wait_ge(pool_done, 2)
                pool.affine_select(out=W["ident"][:, :], in_=W["ident"][:, :], compare_op=ALU.not_equal, fill=1.0,
                                   base=0, pattern=[[-1, P]], channel_multiplier=1)
                pool.affine_select(out=W["before"][:, :], in_=W["before"][:, :], compare_op=ALU.is_gt, fill=0.0,
                                   base=0, pattern=[[1, P]], channel_multiplier=-1).then_inc(made, 1)

            @block.vector
            def _(dve):
                dve.memset(raw_router[:, :, :], 0.0)
                dve.memset(bias_rows[:, :], 0.0)
                dve.memset(zeros[:, :], 0.0).then_inc(filled, 1)
                dve.wait_ge(hi_done, 1)
                dve.tensor_tensor(W["gate"][1][:, :, :], raw_gate[:, :, :], W["gate"][0][:, :, :].bitcast(F32), ALU.subtract)
                dve.wait_ge(hi_done, 2)
                dve.tensor_tensor(W["up"][1][:, :, :], raw_up[:, :, :], W["up"][0][:, :, :].bitcast(F32), ALU.subtract)
                dve.wait_ge(hi_done, 3)
                dve.tensor_tensor(W["router"][1][:, :, :], raw_router[:, :, :], W["router"][0][:, :, :].bitcast(F32), ALU.subtract)
                dve.wait_ge(cols_done, 1)
                dve.tensor_scalar(W["bias"][:, 0:H], bias_cols[:, 0:H], SCALE, None, ALU.mult)
                dve.tensor_copy(W["bias"][:, H:25], bias_cols[:, H:25])

            @block.scalar
            def _(act):
                act.wait_ge(w_in, 7 * DMA)
                act.activation(W["gate"][0][:, :, :], raw_gate[:, :, :], ACT.Copy).then_inc(hi_done, 1)
                act.activation(W["up"][0][:, :, :], raw_up[:, :, :], ACT.Copy).then_inc(hi_done, 1)
                act.activation(W["router"][0][:, :, :], raw_router[:, :, :], ACT.Copy).then_inc(hi_done, 1)

            @block.tensor
            def _(pe):
                pe.wait_ge(made, 1)
                pe.wait_ge(b_in, 4 * DMA)
                pe.transpose(bias_cols[:, 0:25], bias_rows[:, :], W["ident"][0:25, 0:25]).then_inc(cols_done, 1)


class Columns:

    def __init__(self, m, W, norm, xn, xt, bank):
        self.W, self.norm, self.xn, self.xt, self.bank = W, norm, xn, xt, bank
        self.stats = m.sb("stats", [P, J, 6])
        self.moments = m.sb("moments", [P, J, 2])
        self.variance = m.sb("variance", [P, J])
        self.minus_mean = m.sb("minus_mean", [P, J])
        self.scale_shift = m.sb("scale_shift", [P, 2, J])
        self.var_ready, self.scale_ready, self.rows_ready, self.hi_ready, self.psum, self.ready = m.sems(
            "var_ready scale_ready rows_ready hi_ready columns_psum columns_ready")

    def dve_credits(self, dve):
        dve.sem_inc(self.var_ready, CREDIT)
        dve.sem_inc(self.ready, CREDIT)

    def pool_credits(self, pool):
        pool.sem_inc(self.scale_ready, CREDIT)

    def act_credits(self, act):
        act.sem_inc(self.rows_ready, CREDIT)
        act.sem_inc(self.hi_ready, CREDIT)

    def pe_credits(self, pe):
        pe.sem_inc(self.psum, CREDIT)

    def dve_moments(self, dve, b):
        dve.wait_ge(self.scale_ready, at(b))
        settle(dve, self.W["passed_dve"])
        for j in range(J):
            dve.bn_stats(self.stats[:, j, :], self.W["x"][:, b, j, :])
        dve.drain()
        for j in range(J):
            dve.bn_aggr(self.moments[:, j, :], self.stats[:, j, :])
        dve.drain()
        dve.tensor_scalar(self.minus_mean[:, :], self.moments[:, :, 0], -1.0, None, ALU.mult)
        dve.tensor_scalar(self.variance[:, :], self.moments[:, :, 1], EPS, None, ALU.add).then_inc(self.var_ready, 1)

    def pool_scale(self, pool, b):
        pool.wait_ge(self.var_ready, at(b + 1))
        pool.tensor_tensor(self.scale_shift[:, 0, :], self.variance[:, :], self.W["half"][:, :], ALU.pow)
        pool.drain()
        pool.tensor_tensor(self.scale_shift[:, 1, :], self.minus_mean[:, :], self.scale_shift[:, 0, :], ALU.mult)
        pool.drain()
        pool.tensor_copy(self.norm[:, b, :, :], self.scale_shift[:, :, :]).then_inc(self.scale_ready, 1)

    def act_normalise(self, act, b, n):
        act.wait_ge(self.scale_ready, at(b + 1))
        act.wait_ge(self.psum, at(b + 1 - min(len(self.xn), CREDIT)))
        for j in range(J):
            op = act.activation(self.xn[n][:, j, :], self.W["x"][:, b, j, :], ACT.Identity,
                                scale=self.norm[:, b, 0, j:j + 1], bias=self.norm[:, b, 1, j:j + 1])
        op.then_inc(self.rows_ready, 1)

    def pe_transposes(self, pe, b, n):
        pe.wait_ge(self.rows_ready, at(b + 1))
        pe.wait_ge(self.ready, at(b))
        for c in range(C):
            for j in range(J):
                mm = pe.transpose(self.bank[:, c * S + j * P:c * S + (j + 1) * P], self.xn[n][:, j, c:D:C], self.W["ident"][:, :])
        mm.then_inc(self.psum, 1)

    def act_hi(self, act, b, u):
        act.wait_ge(self.psum, at(b + 1))
        act.activation(self.xt[u][0][:, :, :], self.bank.rearrange("p (c s) -> p c s", c=C), ACT.Copy).then_inc(self.hi_ready, 1)

    def dve_lo(self, dve, b, u):
        dve.wait_ge(self.hi_ready, at(b + 1))
        dve.tensor_tensor(self.xt[u][1][:, :, :], self.bank.rearrange("p (c s) -> p c s", c=C),
                          self.xt[u][0][:, :, :].bitcast(F32), ALU.subtract).then_inc(self.ready, 1)


class Router:

    def __init__(self, m, W, columns, ring, ps_logits_t, ps_logits, ps_rank):
        self.W, self.columns, self.ring = W, columns, ring
        self.ps_logits_t, self.ps_logits, self.ps_rank = ps_logits_t, ps_logits, ps_rank
        self.logits_t = m.sb("logits_t", [E, S])
        self.logits = m.sb("logits", [P, J, E])
        self.top = m.sb("top", [P, J, 8])
        self.top_at = m.sb("top_at", [P, J, 8], U32)
        self.first_slot = m.sb("first_slot", [P, J, K])
        self.below_top = m.sb("below_top", [P, J, K])
        self.expo = m.sb("expo", [P, J, K])
        self.expo_sum = m.sb("expo_sum", [P, J])
        self.expo_rec = m.sb("expo_rec", [P, J])
        self.chosen = m.sb("chosen", [P, J, K, E], BF16)
        self.mask_half = m.sb("mask_half", [P, J, K // 2, E], BF16)
        self.mask = m.sb("mask", [P, J, E], BF16)
        self.mask_sum = m.sb("mask_sum", [P, E], BF16)
        self.chosen_rank = m.sb("chosen_rank", [P, J, K, E])
        self.rank = m.sb("rank", [P, J * K])
        self.slot = m.sb("slot", [P, J * K])
        self.kept = m.sb("kept", [P, J * K])
        self.lost = m.sb("lost", [P, J * K])
        self.weight_raw = m.sb("weight_raw", [P, J, K])
        self.scatter_at = [m.sb(f"scatter_at{n}", [P, J * K], U32) for n in range(ring)]
        self.logits_t_psum, self.logits_psum, self.rank_psum = m.sems("logits_t_psum logits_psum rank_psum")
        self.logits_t_ready, self.logits_ready, self.expo_ready = m.sems("logits_t_ready logits_ready expo_ready")
        self.below_ready, self.mask_ready, self.slots_ready = m.sems("below_ready mask_ready slots_ready")
        self.scatter_dma = [m.sem(f"scatter_dma{n}") for n in range(ring)]

    def pe_credits(self, pe):
        for s in (self.logits_t_psum, self.logits_psum, self.rank_psum):
            pe.sem_inc(s, CREDIT)

    def act_credits(self, act):
        for s in (self.logits_t_ready, self.logits_ready, self.expo_ready):
            act.sem_inc(s, CREDIT)

    def dve_credits(self, dve):
        for s in (self.below_ready, self.mask_ready, self.slots_ready):
            dve.sem_inc(s, CREDIT)
        dve.memset(self.mask_sum[:, :], 0.0)

    def rows_sent(self, engine, n, before):
        if not isinstance(before, int) or before > 0:
            engine.wait_ge(self.scatter_dma[n], DMA * J * K * before)

    def pe_logits_t(self, pe, b, u):
        pe.wait_ge(self.columns.ready, at(b + 1))
        pe.wait_ge(self.logits_t_ready, at(b))
        for c in range(C):
            mm = split_product(pe, self.ps_logits_t, [w[:, c, :] for w in self.W["router"]],
                               [x[:, c, :] for x in self.columns.xt[u]], c == 0, c == C - 1)
        mm.then_inc(self.logits_t_psum, 1)

    def act_logits_t(self, act, b):
        act.wait_ge(self.logits_t_psum, at(b + 1))
        act.wait_ge(self.logits_psum, at(b))
        act.activation(self.logits_t[:, :], self.ps_logits_t[0:E, :], ACT.Identity,
                       bias=self.W["bias"][0:E, 24:25]).then_inc(self.logits_t_ready, 1)

    def pe_logits(self, pe, b):
        pe.wait_ge(self.logits_t_ready, at(b + 1))
        pe.wait_ge(self.slots_ready, at(b))
        settle(pe, self.W["passed_pe"])
        for j in range(J):
            mm = pe.transpose(self.ps_logits[:, j, :], self.logits_t[:, j * P:(j + 1) * P], self.W["ident"][0:E, 0:E])
        mm.then_inc(self.logits_psum, 1)

    def act_logits(self, act, b):
        act.wait_ge(self.logits_psum, at(b + 1))
        act.wait_ge(self.below_ready, at(b))
        act.activation(self.logits[:, :, :], self.ps_logits, ACT.Copy).then_inc(self.logits_ready, 1)

    def dve_choose(self, dve, b):
        dve.wait_ge(self.logits_ready, at(b + 1))
        dve.wait_ge(self.expo_ready, at(b))
        settle(dve, self.W["passed_dve"])
        for j in range(J):
            dve.max(self.top[:, j, :], self.logits[:, j, :])
        dve.drain()
        for j in range(J):
            dve.max_index(self.top_at[:, j, :], self.top[:, j, :], self.logits[:, j, :])
        dve.drain()
        dve.tensor_tensor(self.below_top[:, :, :], self.top[:, :, 0:K], self.top[:, :, 0:1].to_broadcast([P, J, K]),
                          ALU.subtract).then_inc(self.below_ready, 1)
        dve.tensor_scalar(self.first_slot[:, :, :], self.top_at[:, :, 0:K], float(CAP), None, ALU.mult)
        dve.drain()
        for j in range(J):
            dve.tensor_tensor(self.chosen[:, j, :, :], self.W["first_slot_of"][:, :].unsqueeze(1).to_broadcast([P, K, E]),
                              self.first_slot[:, j, :].unsqueeze(2).to_broadcast([P, K, E]), ALU.is_equal)
        dve.drain()
        dve.tensor_tensor(self.mask_half[:, :, :, :], self.chosen[:, :, 0:K // 2, :], self.chosen[:, :, K // 2:K, :], ALU.add)
        dve.drain()
        dve.tensor_tensor(self.mask[:, :, :], self.mask_half[:, :, 0, :], self.mask_half[:, :, 1, :], ALU.add).then_inc(self.mask_ready, 1)

    def act_expo(self, act, b):
        act.wait_ge(self.below_ready, at(b + 1))
        act.wait_ge(self.slots_ready, at(b))
        act.activation(self.expo[:, :, :], self.below_top[:, :, :], ACT.Exp).then_inc(self.expo_ready, 1)

    def pe_rank(self, pe, b):
        pe.wait_ge(self.mask_ready, at(b + 1))
        for j in range(J):
            pe.matmul(self.ps_rank[:, j, :], self.W["ones"][:, :], self.mask_sum[:, :], start=True, stop=False)
            for k in range(j):
                pe.matmul(self.ps_rank[:, j, :], self.W["ones"][:, :], self.mask[:, k, :], start=False, stop=False)
            mm = pe.matmul(self.ps_rank[:, j, :], self.W["before"][:, :], self.mask[:, j, :], start=False, stop=True)
        mm.then_inc(self.rank_psum, 1)

    def dve_place(self, dve, b, n, before):
        dve.wait_ge(self.rank_psum, at(b + 1))
        for j in range(J):
            dve.tensor_tensor(self.chosen_rank[:, j, :, :], self.chosen[:, j, :, :],
                              self.ps_rank[:, j, :].unsqueeze(1).to_broadcast([P, K, E]), ALU.mult)
        dve.tensor_tensor(self.mask_sum[:, :], self.mask_sum[:, :], self.mask[:, 0, :], ALU.add)
        dve.wait_ge(self.expo_ready, at(b + 1))
        dve.tensor_reduce(self.expo_sum[:, :], self.expo[:, :, :], AX.X, ALU.add)
        dve.drain()
        dve.tensor_tensor(self.mask_sum[:, :], self.mask_sum[:, :], self.mask[:, 1, :], ALU.add)
        dve.reciprocal(self.expo_rec[:, :], self.expo_sum[:, :])
        dve.tensor_reduce(self.rank[:, :], self.chosen_rank[:, :, :, :].rearrange("p j k e -> p (j k) e"), AX.X, ALU.add)
        dve.drain()
        dve.tensor_scalar(self.lost[:, :], self.rank[:, :], float(CAP), float(DROPPED), ALU.is_ge, ALU.mult)
        dve.scalar_tensor_tensor(out=self.slot[:, :], in0=self.rank[:, :], scalar=float(CAP - 1),
                                 in1=self.first_slot[:, :, :].rearrange("p j k -> p (j k)"), op0=ALU.min, op1=ALU.add)
        dve.tensor_scalar(self.kept[:, :], self.rank[:, :], float(CAP), 0.5, ALU.is_lt, ALU.mult)
        dve.tensor_tensor(self.weight_raw[:, :, :], self.expo[:, :, :], self.expo_rec[:, :].unsqueeze(2).to_broadcast([P, J, K]), ALU.mult)
        dve.drain()
        self.rows_sent(dve, n, before)
        dve.tensor_tensor(self.scatter_at[n][:, :], self.slot[:, :], self.lost[:, :], ALU.add).then_inc(self.slots_ready, 1)
        dve.tensor_copy(self.W["slot_of"][:, b, :], self.slot[:, :])
        dve.tensor_tensor(self.W["weight"][:, b, :], self.weight_raw[:, :, :].rearrange("p j k -> p (j k)"),
                          self.kept[:, :], ALU.mult)

    def pool_dispatch(self, pool, b, n):
        pool.wait_ge(self.slots_ready, at(b + 1))
        settle(pool, self.W["passed_pool"])
        for jk in range(J * K):
            pool.indirect_dma_start(
                self.W["slot_x"], bass.IndirectOffsetOnAxis(ap=self.scatter_at[n][:, jk:jk + 1], axis=0),
                self.columns.xn[n][:, jk // K, :], None, bounds_check=E * CAP - 1, oob_is_err=False,
            ).then_inc(self.scatter_dma[n], DMA)


class Shared:

    def __init__(self, m, W, columns, ps_gu, ps_y):
        self.W, self.columns, self.ps_gu, self.ps_y = W, columns, ps_gu, ps_y
        self.tanh = [m.sb(f"shared_tanh{n}", [P, 2, S]) for n in range(2)]
        self.hidden = m.sb("shared_hidden", [P, HC, S])
        self.gu_psum, self.y_psum, self.tanh_ready, self.hidden_ready, self.x_added = m.sems(
            "shared_gu_psum shared_y_psum shared_tanh_ready shared_hidden_ready shared_x_added")

    def pe_credits(self, pe):
        pe.sem_inc(self.gu_psum, CREDIT)
        pe.sem_inc(self.y_psum, CREDIT)

    def act_credits(self, act):
        act.sem_inc(self.tanh_ready, CREDIT)

    def dve_credits(self, dve):
        dve.sem_inc(self.hidden_ready, CREDIT)
        dve.sem_inc(self.x_added, CREDIT)

    def pe_gate_up(self, pe, b, u, half):
        if half == 0:
            pe.wait_ge(self.columns.ready, at(b + 1))
        for q in (2 * half, 2 * half + 1):
            pe.wait_ge(self.hidden_ready, at(2 * b + half - 1))
            for n, w in enumerate((self.W["gate"], self.W["up"])):
                for c in range(C):
                    mm = split_product(pe, self.ps_gu[:, q, n, :], [v[:, c, q * P:(q + 1) * P] for v in w],
                                       [x[:, c, :] for x in self.columns.xt[u]], c == 0, c == C - 1)
        mm.then_inc(self.gu_psum, 1)

    def act_tanh(self, act, b, half):
        act.wait_ge(self.gu_psum, at(2 * b + half + 1))
        act.wait_ge(self.hidden_ready, at(2 * b + half - 1))
        act.activation(self.tanh[half][:, :, :], self.ps_gu[:, 2 * half:2 * half + 2, 0, :], ACT.Tanh, scale=0.5
                       ).then_inc(self.tanh_ready, 1)

    def dve_hidden(self, dve, b, half):
        q = slice(2 * half, 2 * half + 2)
        dve.wait_ge(self.tanh_ready, at(2 * b + half + 1))
        dve.scalar_tensor_tensor(out=self.tanh[half][:, :, :], in0=self.tanh[half][:, :, :], scalar=1.0,
                                 in1=self.ps_gu[:, q, 0, :], op0=ALU.add, op1=ALU.mult)
        dve.drain()
        dve.wait_ge(self.y_psum, at(b))
        dve.tensor_tensor(self.hidden[:, q, :], self.tanh[half][:, :, :], self.ps_gu[:, q, 1, :], ALU.mult).then_inc(self.hidden_ready, 1)

    def pe_down(self, pe, b, j):
        pe.wait_ge(self.hidden_ready, at(2 * b + 2))
        pe.wait_ge(self.x_added, at(b))
        for q in range(HC):
            mm = pe.matmul(self.ps_y[:, j, :], self.hidden[:, q, j * P:(j + 1) * P],
                           self.W["shared_down"][:, q, :], start=(q == 0), stop=(q == HC - 1))
        if j == J - 1:
            mm.then_inc(self.y_psum, 1)

    def dve_add(self, dve, b):
        dve.wait_ge(self.y_psum, at(b + 1))
        dve.scalar_tensor_tensor(out=self.W["x"][:, b, :, :], in0=self.ps_y[:, :, :], scalar=0.25,
                                 in1=self.W["x"][:, b, :, :], op0=ALU.mult, op1=ALU.add).then_inc(self.x_added, 1)


class Experts:

    QE = 4
    PAIRS = QE // 2
    QUADS = E // QE
    RING = 4

    def __init__(self, nc, ctx, W, a, phase, banks_t, banks_gu, banks_y, split=None):
        m = Memory(nc, ctx, phase)
        self.W, self.a, self.split = W, a, split
        R, PAIRS = self.RING, self.PAIRS
        self.w_gate = [m.sb(f"w_gate{n}", [P, self.QE, C, HID]) for n in range(R)]
        self.w_up = [m.sb(f"w_up{n}", [P, self.QE, C, HID]) for n in range(R)]
        self.w_down = [m.sb(f"w_down{n}", [P, PAIRS, D]) for n in range(R)]
        self.slot_in = [m.sb(f"slot_in{n}", [P, PAIRS, D]) for n in range(R)]
        self.slot_out = [m.sb(f"slot_out{n}", [P, PAIRS, D]) for n in range(R)]
        self.slot_t = [m.sb(f"slot_t{n}", [P, PAIRS, C, P]) for n in range(2)]
        self.tanh = [m.sb(f"tanh{n}", [P, PAIRS, CAP]) for n in range(2)]
        self.gate = [m.sb(f"gate{n}", [P, PAIRS, CAP]) for n in range(2)]
        self.hidden = [m.sb(f"hidden{n}", [P, PAIRS, P]) for n in range(2)]
        self.ps_t = banks_t
        self.ps_gu = [b[:, 0:2 * PAIRS * CAP].rearrange("p (s r t) -> p s r t", s=2, t=CAP) for b in banks_gu]
        self.ps_y = [b[:, :].rearrange("p (r d) -> p r d", d=D) for b in banks_y]
        self.t_psum, self.gu_psum, self.y_psum = m.sems("t_psum gu_psum y_psum")
        self.t_ready, self.tanh_ready, self.out_ready, self.split_hi = m.sems("t_ready tanh_ready out_ready split_hi")
        self.hidden_ready, self.split_lo = m.sems("hidden_ready split_lo")
        self.w_dma = [m.sem(f"w_dma{n}") for n in range(R)]
        self.slot_dma = [m.sem(f"slot_dma{n}") for n in range(R)]
        self.store_dma = [m.sem(f"store_dma{n}") for n in range(R)]
        if split:
            self.raw_q = [m.sb(f"raw_q{n}", [P, C, DH]) for n in range(2)]
            self.raw_o = [m.sb(f"raw_o{n}", [P, D]) for n in range(2)]
            self.raw_dma = [m.sem(f"raw_dma{n}") for n in range(2)]

    def exists(self, i, n):
        return not isinstance(i, int) or 0 <= self.RING * i + n < self.QUADS

    def steps(self, engine, step):
        with engine.Fori(0, self.QUADS // self.RING - 1) as i:
            for n in range(self.RING):
                step(i, n)
        for n in range(self.RING):
            step(self.QUADS // self.RING - 1, n)

    def uses(self, i, n):
        return i + n // self.RING + 1

    def stored(self, engine):
        for n in range(self.RING):
            engine.wait_ge(self.store_dma[n], DMA * (self.QUADS // self.RING))


    def load_weights(self, sp, i, n):
        q, r = self.RING * i + n, n % self.RING
        for buffer, name in ((self.w_gate, "L0_ffn_Wg"), (self.w_up, "L0_ffn_Wu")):
            sp.dma_start(buffer[r][:, :, :, :], self.a[name].rearrange("e (p c) h -> p e c h", c=C)[
                :, bass.ds(q * self.QE, self.QE), :, :]).then_inc(self.w_dma[r], DMA)
        sp.dma_start(self.w_down[r][:, :, :], self.a["L0_ffn_Wd"].rearrange("(r two) h d -> (two h) r d", two=2)[
            :, bass.ds(q * self.PAIRS, self.PAIRS), :]).then_inc(self.w_dma[r], DMA)

    def load_slots(self, sp, i, n):
        q, r = self.RING * i + n, n % self.RING
        sp.dma_start(self.slot_in[r][:, :, :], self.W["slot_x"].rearrange("(q r p) d -> q p r d", p=P, r=self.PAIRS)[
            q]).then_inc(self.slot_dma[r], DMA)

    def load_split(self, sp, i, n):
        q = self.RING * i + n
        sp.dma_start(self.raw_q[n % 2][:, :, :], self.a["L0_attn_Wq"].rearrange("(p c) n -> p c n", c=C)[
            :, :, bass.ds(q * DH, DH)]).then_inc(self.raw_dma[n % 2], DMA)
        sp.dma_start(self.raw_o[n % 2][:, :], self.a["L0_attn_Wo"].rearrange("(h p) d -> h p d", p=P)[q]
                     ).then_inc(self.raw_dma[n % 2], DMA)

    def sp_steps(self, sp):
        def step(i, n):
            q, r = self.RING * i + n, n % self.RING
            if self.split and self.exists(i, n + 2):
                sp.wait_ge(self.split_lo, at(q + 1))
                self.load_split(sp, i, n + 2)
            sp.wait_ge(self.out_ready, at(q + 1))
            sp.dma_start(self.W["slot_y"].rearrange("(q r p) d -> q p r d", p=P, r=self.PAIRS)[q],
                         self.slot_out[r][:, :, :]).then_inc(self.store_dma[r], DMA)
            if self.exists(i, n + self.RING):
                self.load_weights(sp, i, n + self.RING)
                self.load_slots(sp, i, n + self.RING)

        for n in range(self.RING):
            self.load_slots(sp, 0, n)
        if self.split:
            for n in range(2):
                self.load_split(sp, 0, n)
        self.steps(sp, step)


    def pe_credits(self, pe):
        for s in (self.t_psum, self.gu_psum, self.y_psum):
            pe.sem_inc(s, CREDIT)

    def pe_steps(self, pe):
        W = self.W

        def columns(i, n):
            q = self.RING * i + n
            pe.wait_ge(self.slot_dma[n % self.RING], DMA * self.uses(i, n))
            pe.wait_ge(self.t_ready, at(q - 1))
            for r in range(self.PAIRS):
                for c in range(C):
                    mm = pe.transpose(self.ps_t[n % 2][:, r, c, :], self.slot_in[n % self.RING][:, r, c:D:C], W["ident"][:, :])
            mm.then_inc(self.t_psum, 1)

        def gate_up(i, n):
            q = self.RING * i + n
            pe.wait_ge(self.w_dma[n % self.RING], 3 * DMA * self.uses(i, n))
            pe.wait_ge(self.t_ready, at(q + 1))
            pe.wait_ge(self.hidden_ready, at(q - 1))
            settle(pe, self.W["passed_pe"])
            for k in range(self.QE):
                r, odd = k // 2, (k % 2) * CAP
                x = self.slot_t[n % 2][:, r, :, odd:odd + CAP]
                for s, w in enumerate((self.w_gate[n % self.RING], self.w_up[n % self.RING])):
                    for c in range(C):
                        mm = pe.matmul(self.ps_gu[n % 2][odd:odd + HID, s, r, :], w[:, k, c, :], x[:, c, :],
                                       start=(c == 0), stop=(c == C - 1))
            mm.then_inc(self.gu_psum, 1)

        def down(i, n):
            q = self.RING * i + n
            pe.wait_ge(self.hidden_ready, at(q + 1))
            pe.wait_ge(self.out_ready, at(q - 1))
            for r in range(self.PAIRS):
                mm = pe.matmul(self.ps_y[n % 2][:, r, :], self.hidden[n % 2][:, r, :], self.w_down[n % self.RING][:, r, :],
                               start=True, stop=True)
            mm.then_inc(self.y_psum, 1)

        def step(i, n):
            if self.exists(i, n + 1):
                gate_up(i, n + 1)
            if self.exists(i, n + 2):
                columns(i, n + 2)
            down(i, n)

        columns(0, 0)
        columns(0, 1)
        gate_up(0, 0)
        self.steps(pe, step)


    def act_credits(self, act):
        for s in (self.t_ready, self.tanh_ready, self.out_ready, self.split_hi):
            act.sem_inc(s, CREDIT)

    def act_steps(self, act):
        W = self.W

        def columns(i, n):
            q = self.RING * i + n
            act.wait_ge(self.t_psum, at(q + 1))
            act.wait_ge(self.gu_psum, at(q - 1))
            act.activation(self.slot_t[n % 2][:, :, :, :], self.ps_t[n % 2][:, :, :, :], ACT.Copy).then_inc(self.t_ready, 1)

        def tanh(i, n):
            q = self.RING * i + n
            act.wait_ge(self.gu_psum, at(q + 1))
            act.wait_ge(self.hidden_ready, at(q - 1))
            act.activation(self.tanh[n % 2][:, :, :], self.ps_gu[n % 2][:, 0, :, :], ACT.Tanh, scale=0.5
                           ).then_inc(self.tanh_ready, 1)

        def results(i, n):
            q = self.RING * i + n
            act.wait_ge(self.y_psum, at(q + 1))
            if not isinstance(i, int) or i > 0:
                act.wait_ge(self.store_dma[n], DMA * i)
            act.activation(self.slot_out[n][:, :, :], self.ps_y[n % 2][:, :, :], ACT.Copy).then_inc(self.out_ready, 1)

        def split(i, n):
            q = self.RING * i + n
            act.wait_ge(self.raw_dma[n % 2], 2 * DMA * (self.RING // 2 * i + n // 2 + 1))
            act.activation(W["wq"][0][:, :, bass.ds(q * DH, DH)], self.raw_q[n % 2][:, :, :], ACT.Copy, scale=SCALE)
            act.activation(W["wo"][0][:, q, :], self.raw_o[n % 2][:, :], ACT.Copy).then_inc(self.split_hi, 1)

        def step(i, n):
            if self.exists(i, n + 1):
                tanh(i, n + 1)
            if self.exists(i, n + 2):
                columns(i, n + 2)
            results(i, n)
            if self.split:
                split(i, n)

        columns(0, 0)
        columns(0, 1)
        tanh(0, 0)
        for n in range(self.RING):
            step(0, n)
        with act.Fori(1, self.QUADS // self.RING - 1) as i:
            for n in range(self.RING):
                step(i, n)
        for n in range(self.RING):
            step(self.QUADS // self.RING - 1, n)


    def dve_credits(self, dve):
        for s in (self.hidden_ready, self.split_lo):
            dve.sem_inc(s, CREDIT)
        for n in range(2):
            dve.memset(self.hidden[n][:, :, :], 0.0)

    def dve_steps(self, dve):
        W = self.W

        def hidden(i, n):
            q = self.RING * i + n
            dve.wait_ge(self.tanh_ready, at(q + 1))
            gate, up = self.ps_gu[n % 2][:, 0, :, :], self.ps_gu[n % 2][:, 1, :, :]
            dve.scalar_tensor_tensor(out=self.gate[n % 2][:, :, :], in0=self.tanh[n % 2][:, :, :], scalar=1.0, in1=gate,
                                     op0=ALU.add, op1=ALU.mult)
            dve.drain()
            dve.wait_ge(self.y_psum, at(q - 1))
            for odd in range(0, P, CAP):
                op = dve.scalar_tensor_tensor(out=self.hidden[n % 2][odd:odd + HID, :, odd:odd + CAP],
                                              in0=self.gate[n % 2][odd:odd + HID, :, :], scalar=0.5,
                                              in1=up[odd:odd + HID, :, :], op0=ALU.mult, op1=ALU.mult)
            op.then_inc(self.hidden_ready, 1)

        def split(i, n):
            q = self.RING * i + n
            dve.wait_ge(self.split_hi, at(q + 1))
            hi, lo = (w[:, :, bass.ds(q * DH, DH)] for w in W["wq"])
            dve.scalar_tensor_tensor(out=lo, in0=self.raw_q[n % 2][:, :, :], scalar=SCALE, in1=hi.bitcast(F32),
                                     op0=ALU.mult, op1=ALU.subtract)
            hi, lo = (w[:, q, :] for w in W["wo"])
            dve.tensor_tensor(lo, self.raw_o[n % 2][:, :], hi.bitcast(F32), ALU.subtract).then_inc(self.split_lo, 1)

        def step(i, n):
            if self.exists(i, n + 1):
                hidden(i, n + 1)
            if self.split:
                split(i, n)

        hidden(0, 0)
        self.steps(dve, step)


def first_ffn_phase(nc, W, a):
    RING = 4
    with ExitStack() as ctx:
        m = Memory(nc, ctx, "ffn0")
        ps_xt = m.ps("xt", [P, 512])
        ps_logits_t = m.ps("logits_t", [P, 512])
        ps_route = m.ps("route", [P, 512])
        ps_gu = m.ps("gate_up", [P, HC, 2, S])
        ps_y = m.ps("y", [P, J, D])
        logits_bank, rank_bank = (ps_route[:, n * J * E:(n + 1) * J * E].rearrange("p (j e) -> p j e", e=E) for n in range(2))
        xn = [m.sb(f"xn{n}", [P, J, D]) for n in range(RING)]
        xt = [[m.sb(f"xt{u}{part}", [P, C, S], F32R) for part in ("hi", "lo")] for u in range(2)]
        norm = m.sb("norm", [P, NB, 2, J])
        columns = Columns(m, W, norm, xn, xt, ps_xt[:, :])
        router = Router(m, W, columns, RING, ps_logits_t[:, 0:S], logits_bank, rank_bank)
        shared = Shared(m, W, columns, ps_gu, ps_y)
        gu_banks = [ps_gu[:, q, :, :].rearrange("p s t -> p (s t)") for q in range(HC)]
        experts = Experts(nc, ctx, W, a, "experts0",
                          [b[:, :].rearrange("p (r c m) -> p r c m", c=C, m=P) for b in (ps_xt, ps_logits_t)],
                          gu_banks[0:2], gu_banks[2:4], split=True)
        raw_kv = shared.hidden[:, :, :].rearrange("p q s -> p (q s)").rearrange("p (c n) -> p c n", c=C)
        kv_dma, raw_hi, raw_lo = m.sems("kv_dma raw_hi raw_lo")
        parts = (columns, router, shared, experts)

        def exists(i, n):
            return not isinstance(i, int) or RING * i + n < NB

        def rounds(engine, step):
            with engine.Fori(0, NB // RING - 1) as i:
                for n in range(RING):
                    step(i, n)
            for n in range(RING):
                step(NB // RING - 1, n)

        with nc.Block() as block:

            @block.sync
            def _(sp):
                for n in range(experts.RING):
                    experts.load_weights(sp, 0, n)
                sp.wait_ge(shared.y_psum, at(NB))
                sp.dma_start(raw_kv, a["L0_attn_Wk"].rearrange("(p c) n -> p c n", c=C)).then_inc(kv_dma, DMA)
                for n in range(RING):
                    router.rows_sent(sp, n, NB // RING)
                sp.wait_ge(raw_lo, 1)
                sp.dma_start(raw_kv, a["L0_attn_Wv"].rearrange("(p c) n -> p c n", c=C)).then_inc(kv_dma, DMA)
                experts.sp_steps(sp)
                experts.stored(sp)

            @block.gpsimd
            def _(pool):
                columns.pool_credits(pool)

                def step(i, n):
                    if exists(i, n + 3):
                        columns.pool_scale(pool, RING * i + n + 3)
                    router.pool_dispatch(pool, RING * i + n, n)

                for b in range(3):
                    columns.pool_scale(pool, b)
                rounds(pool, step)

            @block.tensor
            def _(pe):
                for part in parts:
                    part.pe_credits(pe)

                def step(i, n):
                    b, u = RING * i + n, n % 2
                    ahead = exists(i, n + 1)
                    shared.pe_gate_up(pe, b, u, 0)
                    if ahead:
                        columns.pe_transposes(pe, b + 1, (n + 1) % RING)
                    shared.pe_gate_up(pe, b, u, 1)
                    router.pe_rank(pe, b)
                    shared.pe_down(pe, b, 0)
                    if ahead:
                        router.pe_logits_t(pe, b + 1, 1 - u)
                    shared.pe_down(pe, b, 1)
                    if ahead:
                        router.pe_logits(pe, b + 1)

                columns.pe_transposes(pe, 0, 0)
                router.pe_logits_t(pe, 0, 0)
                router.pe_logits(pe, 0)
                rounds(pe, step)
                experts.pe_steps(pe)

            @block.scalar
            def _(act):
                for part in parts:
                    part.act_credits(act)

                def normalise(i, n):
                    r = n % RING
                    router.rows_sent(act, r, i + n // RING)
                    columns.act_normalise(act, RING * i + n, r)

                def step(i, n):
                    b, u = RING * i + n, n % 2
                    ahead = exists(i, n + 1)
                    shared.act_tanh(act, b, 0)
                    if ahead:
                        columns.act_hi(act, b + 1, 1 - u)
                    shared.act_tanh(act, b, 1)
                    if exists(i, n + 2):
                        normalise(i, n + 2)
                    if ahead:
                        router.act_logits_t(act, b + 1)
                        router.act_logits(act, b + 1)
                        router.act_expo(act, b + 1)

                normalise(0, 0)
                columns.act_hi(act, 0, 0)
                normalise(0, 1)
                router.act_logits_t(act, 0)
                router.act_logits(act, 0)
                router.act_expo(act, 0)
                rounds(act, step)
                for n, w in enumerate((W["wk"], W["wv"])):
                    act.wait_ge(kv_dma, DMA * (n + 1))
                    act.activation(w[0][:, :, :], raw_kv, ACT.Copy).then_inc(raw_hi, 1)
                experts.act_steps(act)

            @block.vector
            def _(dve):
                for part in parts:
                    part.dve_credits(dve)

                def step(i, n):
                    b, u = RING * i + n, n % 2
                    ahead = exists(i, n + 1)
                    shared.dve_hidden(dve, b, 0)
                    if ahead:
                        columns.dve_lo(dve, b + 1, 1 - u)
                    if exists(i, n + 3):
                        columns.dve_moments(dve, b + 3)
                    shared.dve_hidden(dve, b, 1)
                    router.dve_place(dve, b, n, i)
                    if ahead:
                        router.dve_choose(dve, b + 1)
                    shared.dve_add(dve, b)

                columns.dve_moments(dve, 0)
                columns.dve_moments(dve, 1)
                columns.dve_lo(dve, 0, 0)
                columns.dve_moments(dve, 2)
                router.dve_choose(dve, 0)
                rounds(dve, step)
                for n, w in enumerate((W["wk"], W["wv"])):
                    dve.wait_ge(raw_hi, n + 1)
                    dve.tensor_tensor(w[1][:, :, :], raw_kv, w[0][:, :, :].bitcast(F32), ALU.subtract).then_inc(raw_lo, 1)
                experts.dve_steps(dve)


def last_ffn_phase(nc, W, a):
    with ExitStack() as ctx:
        m = Memory(nc, ctx, "ffn1")
        ps_xt = m.ps("xt", [P, 512])
        ps_t = m.ps("t", [P, 512])
        ps_gu = m.ps("gate_up", [P, HC, 2, S])
        ps_y = m.ps("y", [P, J, D])
        xn = [m.sb(f"xn{n}", [P, J, D]) for n in range(2)]
        xt = [[m.sb(f"xt{u}{part}", [P, C, S], F32R) for part in ("hi", "lo")] for u in range(2)]
        columns = Columns(m, W, W["norm1"], xn, xt, ps_xt[:, :])
        shared = Shared(m, W, columns, ps_gu, ps_y)
        gu_banks = [ps_gu[:, q, :, :].rearrange("p s t -> p (s t)") for q in range(HC)]
        experts = Experts(nc, ctx, W, a, "experts1",
                          [b[:, :].rearrange("p (r c m) -> p r c m", c=C, m=P) for b in (ps_xt, ps_t)],
                          gu_banks[0:2], gu_banks[2:4])
        gather_at = [m.sb(f"gather_at{u}", [P, J * K], U32) for u in range(2)]
        gathered = [m.sb(f"gathered{u}", [P, J * K, D]) for u in range(2)]
        index_ready, combined, out_dma = m.sems("index_ready combined out_dma")
        gather_dma = [m.sem(f"gather_dma{u}") for u in range(2)]
        parts = (columns, shared, experts)

        def exists(i, n):
            return not isinstance(i, int) or 2 * i + n < NB

        def rounds(engine, step):
            with engine.Fori(0, NB // 2 - 1) as i:
                for n in range(2):
                    step(i, n)
            for n in range(2):
                step(NB // 2 - 1, n)

        with nc.Block() as block:

            @block.sync
            def _(sp):
                for n in range(experts.RING):
                    experts.load_weights(sp, 0, n)
                experts.sp_steps(sp)
                experts.stored(sp)
                with sp.Fori(0, NB) as b:
                    sp.wait_ge(combined, at(b + 1))
                    sp.dma_start(a["out"].rearrange("b (j p) d -> b p j d", p=P)[b], W["x"][:, b, :, :]).then_inc(out_dma, DMA)
                sp.wait_ge(out_dma, NB * DMA)

            @block.gpsimd
            def _(pool):
                pool.sem_inc(columns.scale_ready, NB)
                columns.pool_credits(pool)
                pool.sem_inc(index_ready, CREDIT)
                experts.stored(pool)
                with pool.Fori(0, NB // 2) as i:
                    for u in range(2):
                        b = 2 * i + u
                        pool.wait_ge(combined, at(b - 1))
                        settle(pool, W["passed_pool"])
                        pool.tensor_copy(gather_at[u][:, :], W["slot_of"][:, b, :]).then_inc(index_ready, 1)
                        pool.wait_ge(index_ready, at(b + 1))
                        settle(pool, W["passed_pool"])
                        for jk in range(J * K):
                            pool.indirect_dma_start(
                                gathered[u][:, jk, :], None, W["slot_y"],
                                bass.IndirectOffsetOnAxis(ap=gather_at[u][:, jk:jk + 1], axis=0),
                            ).then_inc(gather_dma[u], DMA)

            @block.tensor
            def _(pe):
                for part in parts:
                    part.pe_credits(pe)

                def step(i, n):
                    b, u = 2 * i + n, n % 2
                    shared.pe_gate_up(pe, b, u, 0)
                    if exists(i, n + 1):
                        columns.pe_transposes(pe, b + 1, 1 - u)
                    shared.pe_gate_up(pe, b, u, 1)
                    for j in range(J):
                        shared.pe_down(pe, b, j)

                experts.pe_steps(pe)
                columns.pe_transposes(pe, 0, 0)
                rounds(pe, step)

            @block.scalar
            def _(act):
                for part in parts:
                    part.act_credits(act)

                def step(i, n):
                    b, u = 2 * i + n, n % 2
                    shared.act_tanh(act, b, 0)
                    if exists(i, n + 1):
                        columns.act_hi(act, b + 1, 1 - u)
                    shared.act_tanh(act, b, 1)
                    if exists(i, n + 2):
                        columns.act_normalise(act, b + 2, u)

                columns.act_normalise(act, 0, 0)
                columns.act_normalise(act, 1, 1)
                experts.act_steps(act)
                columns.act_hi(act, 0, 0)
                rounds(act, step)

            @block.vector
            def _(dve):
                for part in parts:
                    part.dve_credits(dve)
                dve.sem_inc(combined, CREDIT)

                def finish(b, u, uses):
                    shared.dve_add(dve, b)
                    dve.drain()
                    dve.wait_ge(gather_dma[u], DMA * J * K * uses)
                    combine(dve, W, gathered[u], b, combined)

                def step(i, n):
                    b, u = 2 * i + n, n % 2
                    shared.dve_hidden(dve, b, 0)
                    if exists(i, n + 1):
                        columns.dve_lo(dve, b + 1, 1 - u)
                    shared.dve_hidden(dve, b, 1)
                    finish(b, u, i + 1)

                experts.dve_steps(dve)
                columns.dve_lo(dve, 0, 0)
                rounds(dve, step)


def combine(engine, W, gathered, b, done):
    for k in range(K):
        for j in range(J):
            op = engine.scalar_tensor_tensor(out=W["x"][:, b, j, :], in0=gathered[:, j * K + k, :],
                                             scalar=W["weight"][:, b, j * K + k:j * K + k + 1], in1=W["x"][:, b, j, :],
                                             op0=ALU.mult, op1=ALU.add)
        if k < K - 1:
            engine.drain()
    op.then_inc(done, 1)


def attention_phase(nc, W, a):
    HEADS = NB * H
    with ExitStack() as ctx:
        m = Memory(nc, ctx, "attn")
        m_route = Memory(nc, ctx, "route1")
        X = W["x"]
        gather_at = m.sb("gather_at", [P, J * K], U32)
        gathered = m.sb("gathered", [P, J * K, D])
        weight = m.sb("weight", [P, J * K])
        routed = m.sb("routed", [P, J, D])

        def halves(name, shape, m=m):
            return [m.sb(f"{name}_{part}", shape, F32R) for part in ("hi", "lo")]

        xn = [m.sb("xn", [P, J, D])]
        xt = [halves(f"xt{u}", [P, C, S]) for u in range(2)]
        keys = [halves(f"keys{u}", [P, KV, S]) for u in range(2)]
        vals = [halves(f"vals{u}", [P, J, KV * DH]) for u in range(2)]
        qt = [halves(f"qt{n}", [P, S]) for n in range(2)]
        prob = [m.sb(f"prob{n}", [P, J, S]) for n in range(2)]
        prob_t = [halves(f"prob_t{n}", [P, J, S]) for n in range(2)]
        ot = [halves(f"ot{n}", [P, S]) for n in range(2)]
        neg_max = [m.sb(f"neg_max{n}", [P, J]) for n in range(2)]
        row_sum = [m.sb(f"row_sum{n}", [P, J]) for n in range(2)]
        row_rec = m.sb("row_rec", [P, J])
        norm = m.sb("norm", [P, NB, 2, J])

        ps_prep = m.ps("prep", [P, 512])
        ps_q = m.ps("q", [P, 512])
        ps_s = [m.ps(f"s{n}", [P, J, S]) for n in range(2)]
        ps_pt = [m.ps(f"pt{n}", [P, J, S]) for n in range(2)]
        ps_o = m.ps("o", [P, 512])
        ps_y = m.ps("y", [P, J, D])

        columns = Columns(m, W, norm, xn, xt, ps_prep[:, :])
        columns1 = Columns(m_route, W, W["norm1"], [m_route.sb("xn", [P, J, D])],
                           [halves("xt", [P, C, S], m_route)], ps_prep[:, :])
        logits_bank, rank_bank = (ps_prep[:, n * J * E:(n + 1) * J * E].rearrange("p (j e) -> p j e", e=E) for n in range(2))
        router = Router(m_route, W, columns1, 1, ps_prep[:, 0:S], logits_bank, rank_bank)
        parts = (columns, columns1, router)

        q_psum, s_psum, pt_psum, o_psum, y_psum, k_psum, v_psum = m.sems("q_psum s_psum pt_psum o_psum y_psum k_psum v_psum")
        q_hi, exp_ready, pt_hi, o_hi, k_hi, v_hi = m.sems("q_hi exp_ready pt_hi o_hi k_hi v_hi")
        q_ready, max_ready, p_ready, pt_ready, o_ready, k_ready, v_ready, x_added = m.sems(
            "q_ready max_ready p_ready pt_ready o_ready k_ready v_ready x_added")
        index_ready, combined, bias_added, gather_dma = m.sems("index_ready combined bias_added gather_dma")

        LOOPS = NB // 2 - 1
        TWO = 2 * H

        def exists(i, c):
            return not isinstance(i, int) or 0 <= TWO * i + c < HEADS

        def next_batch(i, c):
            return c >= 0 and (not isinstance(i, int) or 2 * i + c // H + 1 < NB)

        def last_batch(i, c):
            return c >= 0 and (not isinstance(i, int) or 2 * i + c // H >= 1)

        def bias(first, n):
            return W["bias"][:, first + n:first + n + 1]

        MOMENTS, NORMALISE, COLUMNS, KEYS, VALUES = 3, 5, 6, 7, 11
        MOMENTS1, NORMALISE1, COLUMNS1, LOGITS_T, LOGITS, CHOOSE, RANK = 0, 1, 2, 4, 5, 5, 13

        def walk(engine, step):
            for c in range(-5, H):
                step(0, c)
            with engine.Fori(0, LOOPS) as i:
                for c in range(H, H + TWO):
                    step(i, c)
            for c in range(H, TWO):
                step(LOOPS, c)

        with nc.Block() as block:

            @block.gpsimd
            def _(pool):
                columns.pool_credits(pool)
                columns1.pool_credits(pool)
                for s in (index_ready, combined, bias_added):
                    pool.sem_inc(s, CREDIT)

                def fetch(b):
                    pool.wait_ge(combined, at(b))
                    settle(pool, W["passed_pool"])
                    pool.tensor_copy(weight[:, :], W["weight"][:, b, :])
                    pool.tensor_copy(gather_at[:, :], W["slot_of"][:, b, :]).then_inc(index_ready, 1)
                    pool.wait_ge(index_ready, at(b + 1))
                    settle(pool, W["passed_pool"])
                    for jk in range(J * K):
                        pool.indirect_dma_start(
                            gathered[:, jk, :], None, W["slot_y"],
                            bass.IndirectOffsetOnAxis(ap=gather_at[:, jk:jk + 1], axis=0),
                        ).then_inc(gather_dma, DMA)

                def prepare(b):
                    pool.wait_ge(gather_dma, DMA * J * K * (b + 1))
                    settle(pool, W["passed_pool"])
                    rows = gathered[:, :, :].rearrange("p (j k) d -> p j k d", k=K)
                    pool.tensor_tensor(gathered[:, :, :], gathered[:, :, :], weight[:, :].unsqueeze(2).to_broadcast([P, J * K, D]), ALU.mult)
                    pool.drain()
                    pool.tensor_tensor(rows[:, :, 0:2, :], rows[:, :, 0:2, :], rows[:, :, 2:4, :], ALU.add)
                    pool.drain()
                    pool.tensor_tensor(routed[:, :, :], rows[:, :, 0, :], rows[:, :, 1, :], ALU.add)
                    pool.drain()
                    pool.tensor_tensor(X[:, b, :, :], X[:, b, :, :], routed[:, :, :], ALU.add).then_inc(combined, 1)
                    columns.pool_scale(pool, b)
                    pool.wait_ge(columns.rows_ready, at(b + 1))
                    settle(pool, W["passed_pool"])
                    pool.tensor_tensor(X[:, b, :, :], X[:, b, :, :], W["bo"][:, :].unsqueeze(1).to_broadcast([P, J, D]),
                                       ALU.add).then_inc(bias_added, 1)

                fetch(0)
                prepare(0)
                fetch(1)
                prepare(1)
                fetch(2)
                with pool.Fori(1, NB - 2) as b:
                    columns1.pool_scale(pool, b - 1)
                    prepare(b + 1)
                    fetch(b + 2)
                    router.pool_dispatch(pool, b - 1, 0)
                columns1.pool_scale(pool, NB - 3)
                prepare(NB - 1)
                router.pool_dispatch(pool, NB - 3, 0)
                for b in (NB - 2, NB - 1):
                    columns1.pool_scale(pool, b)
                    router.pool_dispatch(pool, b, 0)
                router.rows_sent(pool, 0, NB)

            @block.tensor
            def _(pe):
                for part in parts:
                    part.pe_credits(pe)
                for s in (q_psum, s_psum, pt_psum, o_psum, y_psum, k_psum, v_psum):
                    pe.sem_inc(s, CREDIT)

                def key_group(b, u, g):
                    pe.wait_ge(columns.ready, at(b + 1))
                    pe.wait_ge(k_ready, at(KV * b + g))
                    for c in range(C):
                        mm = split_product(pe, ps_prep[:, 0:S], [w[:, c, g * DH:(g + 1) * DH] for w in W["wk"]],
                                           [x[:, c, :] for x in xt[u]], c == 0, c == C - 1)
                    mm.then_inc(k_psum, 1)

                def value_tile(b, u, j):
                    pe.wait_ge(k_ready, at(KV * (b + 1)))
                    pe.wait_ge(v_ready, at(J * b + j))
                    for c in range(C):
                        mm = split_product(pe, ps_prep[:, :], [x[:, c, j * P:(j + 1) * P] for x in xt[u]],
                                           [w[:, c, :] for w in W["wv"]], c == 0, c == C - 1)
                    mm.then_inc(v_psum, 1)

                def prepare(b, u, h):
                    if h == COLUMNS:
                        columns.pe_transposes(pe, b, 0)
                    if KEYS <= h < KEYS + KV:
                        key_group(b, u, h - KEYS)
                    if VALUES <= h < VALUES + J:
                        value_tile(b, u, h - VALUES)

                def route(b, h):
                    if h == COLUMNS1:
                        pe.wait_ge(router.slots_ready, at(b))
                        columns1.pe_transposes(pe, b, 0)
                    if h == LOGITS_T:
                        router.pe_logits_t(pe, b, 0)
                    if h == LOGITS:
                        router.pe_logits(pe, b)
                    if h == COLUMNS:
                        pe.wait_ge(router.logits_ready, at(b + 1))
                    if h == RANK:
                        if not isinstance(b, int) or b + 2 < NB:
                            pe.wait_ge(v_ready, at(J * (b + 3)))
                        router.pe_rank(pe, b)

                def queries(i, c):
                    k, u, h = TWO * i + c, c // H % 2, c % H
                    pe.wait_ge(q_ready, at(k))
                    if h == 0:
                        pe.wait_ge(columns.ready, at(2 * i + c // H + 1))
                    for d in range(C):
                        mm = split_product(pe, ps_q[:, 0:S], [w[:, d, h * DH:(h + 1) * DH] for w in W["wq"]],
                                           [x[:, d, :] for x in xt[u]], d == 0, d == C - 1)
                    mm.then_inc(q_psum, 1)

                def scores(i, c):
                    k, u, h = TWO * i + c, c // H % 2, c % H
                    pe.wait_ge(q_ready, at(k + 1))
                    pe.wait_ge(exp_ready, at(k - 1))
                    if h == 0:
                        pe.wait_ge(k_ready, at(KV * (2 * i + c // H + 1)))
                    for j in range(J):
                        mm = split_product(pe, ps_s[c % 2][:, j, :], [x[:, j * P:(j + 1) * P] for x in qt[c % 2]],
                                           [x[:, h // GROUP, :] for x in keys[u]], True, True)
                    mm.then_inc(s_psum, 1)

                def transposes(i, c):
                    k = TWO * i + c
                    pe.wait_ge(p_ready, at(k + 1))
                    pe.wait_ge(pt_ready, at(k - 1))
                    for t in range(J):
                        for j in range(J):
                            mm = pe.transpose(ps_pt[c % 2][:, t, j * P:(j + 1) * P], prob[c % 2][:, j, t * P:(t + 1) * P],
                                              W["ident"][:, :])
                    mm.then_inc(pt_psum, 1)

                def values(i, c):
                    k, u, h = TWO * i + c, c // H % 2, c % H
                    g = h // GROUP
                    pe.wait_ge(pt_ready, at(k + 1))
                    pe.wait_ge(o_ready, at(k))
                    if h == 0:
                        pe.wait_ge(v_ready, at(J * (2 * i + c // H + 1)))
                    for t in range(J):
                        mm = split_product(pe, ps_o[:, 0:S], [v[:, t, g * DH:(g + 1) * DH] for v in vals[u]],
                                           [x[:, t, :] for x in prob_t[c % 2]], t == 0, t == J - 1)
                    mm.then_inc(o_psum, 1)

                def outputs(i, c):
                    k, h = TWO * i + c, c % H
                    pe.wait_ge(o_ready, at(k + 1))
                    if h == 0:
                        pe.wait_ge(x_added, at(2 * i + c // H))
                    for j in range(J):
                        left = [x[:, j * P:(j + 1) * P] for x in ot[c % 2]]
                        right = [w[:, h, :] for w in W["wo"]]
                        for n, (l, r) in enumerate(((left[1], right[0]), (left[0], right[1]), (left[0], right[0]))):
                            mm = pe.matmul(ps_y[:, j, :], l, r, start=(h == 0 and j == 0 and n == 0),
                                           stop=(h == H - 1 and n == 2), skip_group_check=True)
                    mm.then_inc(y_psum, 1)

                def step(i, c):
                    if exists(i, c + 2):
                        transposes(i, c + 2)
                    if exists(i, c + 5):
                        queries(i, c + 5)
                    if exists(i, c + 4):
                        scores(i, c + 4)
                    if last_batch(i, c):
                        route(2 * i + c // H - 1, c % H)
                    if next_batch(i, c):
                        prepare(2 * i + c // H + 1, 1 - c // H % 2, c % H)
                    if exists(i, c):
                        outputs(i, c)
                    if exists(i, c + 1):
                        values(i, c + 1)

                for h in range(H):
                    prepare(0, 0, h)
                walk(pe, step)
                for h in range(H):
                    route(NB - 1, h)

            @block.scalar
            def _(act):
                for part in parts:
                    part.act_credits(act)
                for s in (q_hi, exp_ready, pt_hi, o_hi, k_hi, v_hi):
                    act.sem_inc(s, CREDIT)

                def prepare(b, u, h):
                    if h == NORMALISE:
                        columns.act_normalise(act, b, 0)
                    if h == COLUMNS:
                        columns.act_hi(act, b, u)
                    if KEYS <= h < KEYS + KV:
                        g = h - KEYS
                        act.wait_ge(k_psum, at(KV * b + g + 1))
                        act.activation(keys[u][0][:, g, :], ps_prep[:, 0:S], ACT.Identity, bias=bias(H, g)).then_inc(k_hi, 1)
                    if VALUES <= h < VALUES + J:
                        j = h - VALUES
                        act.wait_ge(v_psum, at(J * b + j + 1))
                        act.activation(vals[u][0][:, j, :], ps_prep[:, :], ACT.Copy).then_inc(v_hi, 1)

                def route(b, h):
                    if h == NORMALISE1:
                        router.rows_sent(act, 0, b)
                        columns1.act_normalise(act, b, 0)
                    if h == COLUMNS1:
                        columns1.act_hi(act, b, 0)
                    if h == LOGITS_T:
                        router.act_logits_t(act, b)
                    if h == LOGITS:
                        router.act_logits(act, b)
                    if h == CHOOSE + 1:
                        router.act_expo(act, b)

                def queries(i, c):
                    k = TWO * i + c
                    act.wait_ge(q_psum, at(k + 1))
                    act.wait_ge(s_psum, at(k - 1))
                    act.activation(qt[c % 2][0][:, :], ps_q[:, 0:S], ACT.Identity, bias=bias(0, c % H)).then_inc(q_hi, 1)

                def exponentials(i, c):
                    k = TWO * i + c
                    act.wait_ge(max_ready, at(k + 1))
                    act.wait_ge(pt_psum, at(k - 1))
                    for j in range(J):
                        op = act.activation(prob[c % 2][:, j, :], ps_s[c % 2][:, j, :], ACT.Exp,
                                            bias=neg_max[c % 2][:, j:j + 1], accum_out=row_sum[c % 2][:, j:j + 1])
                    op.then_inc(exp_ready, 1)

                def transposed(i, c):
                    k = TWO * i + c
                    act.wait_ge(pt_psum, at(k + 1))
                    act.wait_ge(o_psum, at(k - 1))
                    act.activation(prob_t[c % 2][0][:, :, :], ps_pt[c % 2][:, :, :], ACT.Copy).then_inc(pt_hi, 1)

                def outputs(i, c):
                    k = TWO * i + c
                    act.wait_ge(o_psum, at(k + 1))
                    act.wait_ge(y_psum, at(k - 1))
                    act.activation(ot[c % 2][0][:, :], ps_o[:, 0:S], ACT.Identity, bias=bias(H + KV, c % H // GROUP)).then_inc(o_hi, 1)

                def step(i, c):
                    if exists(i, c):
                        outputs(i, c)
                    if exists(i, c + 3):
                        exponentials(i, c + 3)
                    if exists(i, c + 2):
                        transposed(i, c + 2)
                    if exists(i, c + 5):
                        queries(i, c + 5)
                    if last_batch(i, c):
                        route(2 * i + c // H - 1, c % H)
                    if next_batch(i, c):
                        prepare(2 * i + c // H + 1, 1 - c // H % 2, c % H)

                for h in range(H):
                    prepare(0, 0, h)
                walk(act, step)
                for h in range(H):
                    route(NB - 1, h)

            @block.vector
            def _(dve):
                for part in parts:
                    part.dve_credits(dve)
                for s in (q_ready, max_ready, p_ready, pt_ready, o_ready, k_ready, v_ready, x_added):
                    dve.sem_inc(s, CREDIT)

                def prepare(b, u, h):
                    if h == MOMENTS:
                        dve.wait_ge(combined, at(b + 1))
                        columns.dve_moments(dve, b)
                    if h == COLUMNS:
                        columns.dve_lo(dve, b, u)
                    if KEYS <= h < KEYS + KV:
                        g = h - KEYS
                        dve.wait_ge(k_hi, at(KV * b + g + 1))
                        dve.scalar_tensor_tensor(out=keys[u][1][:, g, :], in0=ps_prep[:, 0:S], scalar=bias(H, g),
                                                 in1=keys[u][0][:, g, :].bitcast(F32), op0=ALU.add,
                                                 op1=ALU.subtract).then_inc(k_ready, 1)
                    if VALUES <= h < VALUES + J:
                        j = h - VALUES
                        dve.wait_ge(v_hi, at(J * b + j + 1))
                        dve.tensor_tensor(vals[u][1][:, j, :], ps_prep[:, :], vals[u][0][:, j, :].bitcast(F32),
                                          ALU.subtract).then_inc(v_ready, 1)

                def route(b, h):
                    if h == MOMENTS1:
                        dve.drain()
                        columns1.dve_moments(dve, b)
                    if h == COLUMNS1:
                        columns1.dve_lo(dve, b, 0)
                    if h == CHOOSE:
                        router.dve_choose(dve, b)
                    if h == RANK:
                        router.dve_place(dve, b, 0, b)

                def maxima(i, c):
                    k = TWO * i + c
                    dve.wait_ge(s_psum, at(k + 1))
                    dve.wait_ge(exp_ready, at(k - 1))
                    dve.tensor_reduce(neg_max[c % 2][:, :], ps_s[c % 2][:, :, :], AX.X, ALU.max, negate=True).then_inc(max_ready, 1)

                def transposed(i, c):
                    k = TWO * i + c
                    dve.wait_ge(pt_hi, at(k + 1))
                    dve.tensor_tensor(prob_t[c % 2][1][:, :, :], ps_pt[c % 2][:, :, :],
                                      prob_t[c % 2][0][:, :, :].bitcast(F32), ALU.subtract).then_inc(pt_ready, 1)

                def queries(i, c):
                    k = TWO * i + c
                    dve.wait_ge(q_hi, at(k + 1))
                    dve.scalar_tensor_tensor(out=qt[c % 2][1][:, :], in0=ps_q[:, 0:S], scalar=bias(0, c % H),
                                             in1=qt[c % 2][0][:, :].bitcast(F32), op0=ALU.add,
                                             op1=ALU.subtract).then_inc(q_ready, 1)

                def normalised(i, c):
                    k = TWO * i + c
                    dve.wait_ge(exp_ready, at(k + 1))
                    dve.reciprocal(row_rec[:, :], row_sum[c % 2][:, :])
                    dve.drain()
                    for j in range(J):
                        op = dve.tensor_scalar(prob[c % 2][:, j, :], prob[c % 2][:, j, :], row_rec[:, j:j + 1], None, ALU.mult)
                    op.then_inc(p_ready, 1)

                def outputs(i, c):
                    k = TWO * i + c
                    dve.wait_ge(o_hi, at(k + 1))
                    dve.scalar_tensor_tensor(out=ot[c % 2][1][:, :], in0=ps_o[:, 0:S], scalar=bias(H + KV, c % H // GROUP),
                                             in1=ot[c % 2][0][:, :].bitcast(F32), op0=ALU.add,
                                             op1=ALU.subtract).then_inc(o_ready, 1)

                def step(i, c):
                    if exists(i, c):
                        outputs(i, c)
                    if exists(i, c + 3):
                        normalised(i, c + 3)
                    if exists(i, c + 2):
                        transposed(i, c + 2)
                    if exists(i, c + 5):
                        queries(i, c + 5)
                    if exists(i, c + 4):
                        maxima(i, c + 4)
                    if last_batch(i, c):
                        route(2 * i + c // H - 1, c % H)
                    if next_batch(i, c):
                        prepare(2 * i + c // H + 1, 1 - c // H % 2, c % H)
                    if c >= 0 and c % H == H - 1:
                        b = 2 * i + c // H
                        dve.wait_ge(bias_added, at(b + 1))
                        dve.wait_ge(y_psum, at(H * (b + 1)))
                        dve.tensor_tensor(X[:, b, :, :], ps_y[:, :, :], X[:, b, :, :], ALU.add).then_inc(x_added, 1)

                for h in range(H):
                    prepare(0, 0, h)
                walk(dve, step)
                for h in range(H):
                    route(NB - 1, h)


def macaron(nc, a):
    with ExitStack() as ctx:
        m = Memory(nc, ctx, "all")

        def halves(name, shape, m=m):
            return [m.sb(f"{name}_{part}", shape, F32R) for part in ("hi", "lo")]

        W = {
            "x": m.sb("x", [P, NB, J, D]),
            "gate": halves("gate", [P, C, HS]),
            "up": halves("up", [P, C, HS]),
            "router": halves("router", [P, C, P]),
            "shared_down": m.sb("shared_down", [P, HC, D]),
            "bo": m.sb("bo", [P, D]),
            "bias": m.sb("bias", [P, 25]),
            "ident": m.sb("ident", [P, P]),
            "before": m.sb("before", [P, P], BF16),
            "ones": m.sb("ones", [P, P], BF16),
            "first_slot_of": m.sb("first_slot_of", [P, E]),
            "half": m.sb("half", [P, J]),
            "slot_of": m.sb("slot_of", [P, NB, J * K], U32),
            "weight": m.sb("weight", [P, NB, J * K]),
            "norm1": m.sb("norm1", [P, NB, 2, J]),
            "passed_pe": m.sem("passed_pe"),
            "passed_pool": m.sem("passed_pool"),
            "passed_dve": m.sem("passed_dve"),
            "slot_x": nc.dram_tensor("slot_x", (E * CAP, D), F32, kind="Internal").ap(),
            "slot_y": nc.dram_tensor("slot_y", (E * CAP, D), F32, kind="Internal").ap(),
        }
        with ExitStack() as until_attention:
            m_attn = Memory(nc, until_attention, "all")
            for name, shape in (("wq", [P, C, H * DH]), ("wk", [P, C, KV * DH]), ("wv", [P, C, KV * DH]), ("wo", [P, H, D])):
                W[name] = halves(name, shape, m_attn)
            setup_phase(nc, W, a)
            first_ffn_phase(nc, W, a)
            attention_phase(nc, W, a)
        last_ffn_phase(nc, W, a)


_INS = ["L0_attn_x", "L0_attn_Wq", "L0_attn_bq", "L0_attn_Wk", "L0_attn_bk", "L0_attn_Wv", "L0_attn_bv", "L0_attn_Wo",
        "L0_attn_bo", "L0_ffn_Wr", "L0_ffn_router_bias", "L0_ffn_Wg", "L0_ffn_Wu", "L0_ffn_Wd", "L0_ffn_Sg", "L0_ffn_Su",
        "L0_ffn_Sd"]


def kernel(**inputs):
    import numpy as _np
    import concourse.bacc as _bacc
    from concourse.bass_utils import run_bass_kernel_spmd as _run

    nc = _bacc.Bacc("TRN2", target_bir_lowering=False, num_devices=1)
    arrays, args = {}, {}
    for name in _INS:
        x = _np.ascontiguousarray(inputs[name])
        arrays[f"in_{name}"] = x
        args[name] = nc.dram_tensor(f"in_{name}", x.shape, mybir.dt.from_np(x.dtype), kind="ExternalInput").ap()
    args["out"] = nc.dram_tensor("out_0", arrays["in_L0_attn_x"].shape, F32, kind="ExternalOutput").ap()
    macaron(nc, args)
    r = _run(nc, [arrays], core_ids=[0])
    return r.results[0]["out_0"]
```

```python
from contextlib import ExitStack

import concourse.bass as bass
from concourse import mybir

F32 = mybir.dt.float32
F32R = mybir.dt.float32r
BF16 = mybir.dt.bfloat16
U32 = mybir.dt.uint32
ALU = mybir.AluOpType
ACT = mybir.ActivationFunctionType
AX = mybir.AxisListType

P = 128
D = 256
C = D // P
NB = 8
S = 256
J = S // P
H, DH, KV = 16, 128, 4
GROUP = H // KV
E, K, HID, CAP = 64, 4, 64, 64
HS = 512
HC = HS // P
SCALE = float(DH) ** -0.5
EPS = 1e-5
DROPPED = 8192
SLOTS = E * CAP
ROWS = NB * S * K
NOWHERE = 2 * ROWS
TAG = 8 * SLOTS
WIDE = D + 2 * K
CREDIT = 2
DMA = 16


def at(n):
    return n + CREDIT


def settle(engine, passed):
    engine.sem_inc(passed, 1)


def split_product(pe, out, left, right, start, stop):
    pe.matmul(out, left[1], right[0], start=start, stop=False)
    pe.matmul(out, left[0], right[1], start=False, stop=False)
    return pe.matmul(out, left[0], right[0], start=False, stop=stop)


class Memory:

    def __init__(self, nc, ctx, kept, phase, part=None):
        self.nc, self.ctx, self.kept, self.phase, self.part = nc, ctx, kept, phase, part or phase

    def sb(self, name, shape, dt=F32):
        return self.ctx.enter_context(self.nc.sbuf_tensor(f"{self.phase}_{name}", shape, dt))

    def ps(self, name, shape, dt=F32):
        return self.ctx.enter_context(self.nc.psum_tensor(f"{self.phase}_ps_{name}", shape, dt))

    def sem(self, name):
        name = f"{self.part}_{name}"
        if name not in self.kept:
            self.kept[name] = self.nc.alloc_semaphore(name)
        return self.kept[name]

    def sems(self, names):
        return [self.sem(n) for n in names.split()]


def setup_phase(nc, W, a):
    with ExitStack() as ctx:
        m = Memory(nc, ctx, W["kept"], "setup")
        raw_gate = m.sb("raw_gate", [P, C, HS])
        raw_up = m.sb("raw_up", [P, C, HS])
        raw_router = m.sb("raw_router", [P, C, P])
        bias_rows = m.sb("bias_rows", [25, P])
        bias_cols = m.ps("bias_cols", [P, 512])
        made, filled, zeroed, first_in, router_in, gate_in, up_in, b_in, cols_done, hi_done, pool_done = m.sems(
            "made filled zeroed first_in router_in gate_in up_in b_in cols_done hi_done pool_done")
        x_view = a["L0_attn_x"].rearrange("b (j p) d -> p b j d", p=P)
        with nc.Block() as block:

            @block.sync
            def _(sp):
                sp.dma_start(W["x"][:, 0, :, :], x_view[:, 0, :, :]).then_inc(first_in, DMA)
                sp.wait_ge(filled, 1)
                sp.dma_start(raw_router[:, :, 0:E], a["L0_ffn_Wr"].rearrange("(p c) e -> p c e", c=C)).then_inc(router_in, DMA)
                half = HS // 2
                for raw, name, done in ((raw_gate, "L0_ffn_Sg", gate_in), (raw_up, "L0_ffn_Su", up_in)):
                    for s in range(2):
                        sp.dma_start(raw[:, :, s * half:(s + 1) * half],
                                     a[name][s].rearrange("(p c) h -> p c h", c=C)).then_inc(done, DMA)
                sp.dma_start(W["x"][:, 1:3, :, :], x_view[:, 1:3, :, :]).then_inc(W["x_in"], DMA)
                sp.dma_start(W["shared_down"][:, :, :],
                             a["L0_ffn_Sd"].rearrange("s (q p) d -> p (s q) d", p=P)).then_inc(W["down_in"], DMA)
                sp.dma_start(W["x"][:, 3:NB, :, :], x_view[:, 3:NB, :, :]).then_inc(W["x_rest_in"], DMA)
                slots = W["slot_x"].rearrange("(p r) d -> p (r d)", p=P)
                sp.wait_ge(zeroed, 1)
                for n in range(4):
                    sp.dma_start(slots[:, n * 8 * WIDE:(n + 1) * 8 * WIDE], W["zeros"]).then_inc(W["slots_zeroed"], DMA)

            @block.gpsimd
            def _(pool):
                pool.memset(W["ident"][:, :], 0.0).then_inc(pool_done, 1)
                pool.memset(W["before"][:, :], 1.0).then_inc(pool_done, 1)
                pool.memset(W["ones"][:, :], 1.0)
                pool.memset(W["half"][:, :], -0.5)
                pool.iota(W["own_slot"][:, :, :], pattern=[[P, SLOTS // P]], base=TAG, channel_multiplier=1,
                          allow_small_or_imprecise_dtypes=True)
                pool.iota(W["row_of"][:, :, :, :], pattern=[[P * K, NB * J], [1, K]], base=-NOWHERE, channel_multiplier=K,
                          allow_small_or_imprecise_dtypes=True)
                pool.iota(W["first_slot_of"][:, :], pattern=[[CAP, E]], base=0, channel_multiplier=0,
                          allow_small_or_imprecise_dtypes=True)
                pool.wait_ge(pool_done, 2)
                pool.affine_select(out=W["ident"][:, :], in_=W["ident"][:, :], compare_op=ALU.not_equal, fill=1.0,
                                   base=0, pattern=[[-1, P]], channel_multiplier=1)
                pool.affine_select(out=W["before"][:, :], in_=W["before"][:, :], compare_op=ALU.is_gt, fill=0.0,
                                   base=0, pattern=[[1, P]], channel_multiplier=-1).then_inc(made, 1)

            @block.vector
            def _(dve):
                dve.memset(raw_router[:, :, :], 0.0)
                dve.memset(bias_rows[:, :], 0.0).then_inc(filled, 1)
                dve.memset(W["zeros"], 0.0).then_inc(zeroed, 1)
                dve.wait_ge(hi_done, 1)
                dve.tensor_tensor(W["router"][1][:, :, :], raw_router[:, :, :], W["router"][0][:, :, :].bitcast(F32), ALU.subtract)
                dve.wait_ge(cols_done, 1)
                dve.tensor_scalar(W["bias"][:, 0:H], bias_cols[:, 0:H], SCALE, None, ALU.mult)
                dve.tensor_copy(W["bias"][:, H:25], bias_cols[:, H:25])
                dve.wait_ge(hi_done, 2)
                dve.tensor_tensor(W["gate"][1][:, :, :], raw_gate[:, :, :], W["gate"][0][:, :, :].bitcast(F32), ALU.subtract)
                dve.wait_ge(hi_done, 3)
                dve.tensor_tensor(W["up"][1][:, :, :], raw_up[:, :, :], W["up"][0][:, :, :].bitcast(F32), ALU.subtract)
                dve.wait_ge(first_in, DMA)

            @block.scalar
            def _(act):
                act.wait_ge(filled, 1)
                for first, last, name in ((0, 16, "L0_attn_bq"), (16, 20, "L0_attn_bk"), (20, 24, "L0_attn_bv")):
                    act.dma_start(bias_rows[first:last, :], a[name].rearrange("(h p) -> h p", p=P)).then_inc(b_in, DMA)
                act.dma_start(bias_rows[24:25, 0:E], a["L0_ffn_router_bias"].rearrange("(h p) -> h p", p=E)).then_inc(b_in, DMA)
                act.dma_start(W["bo"][:, :], a["L0_attn_bo"].partition_broadcast(P)).then_inc(W["bo_in"], DMA)
                act.wait_ge(router_in, DMA)
                act.activation(W["router"][0][:, :, :], raw_router[:, :, :], ACT.Copy).then_inc(hi_done, 1)
                act.wait_ge(gate_in, 2 * DMA)
                act.activation(W["gate"][0][:, :, :], raw_gate[:, :, :], ACT.Copy).then_inc(hi_done, 1)
                act.wait_ge(up_in, 2 * DMA)
                act.activation(W["up"][0][:, :, :], raw_up[:, :, :], ACT.Copy).then_inc(hi_done, 1)

            @block.tensor
            def _(pe):
                pe.wait_ge(made, 1)
                pe.wait_ge(b_in, 4 * DMA)
                pe.transpose(bias_cols[:, 0:25], bias_rows[:, :], W["ident"][0:25, 0:25]).then_inc(cols_done, 1)


class Columns:

    def __init__(self, m, W, norm, xn, xt, bank, norm_made=False):
        self.norm_made = norm_made
        self.W, self.norm, self.xn, self.xt, self.bank = W, norm, xn, xt, bank
        self.stats = m.sb("stats", [P, J, 6])
        self.moments = m.sb("moments", [P, J, 2])
        self.variance = m.sb("variance", [P, J])
        self.minus_mean = m.sb("minus_mean", [P, J])
        self.scale_shift = m.sb("scale_shift", [P, 2, J])
        self.var_ready, self.scale_ready, self.rows_ready, self.hi_ready, self.psum, self.ready = m.sems(
            "var_ready scale_ready rows_ready hi_ready columns_psum columns_ready")

    def dve_credits(self, dve):
        dve.sem_inc(self.var_ready, CREDIT)
        dve.sem_inc(self.ready, CREDIT)

    def pool_credits(self, pool):
        pool.sem_inc(self.scale_ready, CREDIT)

    def act_credits(self, act):
        act.sem_inc(self.rows_ready, CREDIT)
        act.sem_inc(self.hi_ready, CREDIT)

    def pe_credits(self, pe):
        pe.sem_inc(self.psum, CREDIT)

    def dve_moments(self, dve, b):
        dve.wait_ge(self.scale_ready, at(b))
        settle(dve, self.W["passed_dve"])
        for j in range(J):
            dve.bn_stats(self.stats[:, j, :], self.W["x"][:, b, j, :])
        dve.drain()
        for j in range(J):
            dve.bn_aggr(self.moments[:, j, :], self.stats[:, j, :])
        dve.drain()
        dve.tensor_scalar(self.minus_mean[:, :], self.moments[:, :, 0], -1.0, None, ALU.mult)
        dve.tensor_scalar(self.variance[:, :], self.moments[:, :, 1], EPS, None, ALU.add).then_inc(self.var_ready, 1)

    def pool_scale(self, pool, b):
        pool.wait_ge(self.var_ready, at(b + 1))
        pool.tensor_tensor(self.scale_shift[:, 0, :], self.variance[:, :], self.W["half"][:, :], ALU.pow)
        pool.drain()
        pool.tensor_tensor(self.scale_shift[:, 1, :], self.minus_mean[:, :], self.scale_shift[:, 0, :], ALU.mult)
        pool.drain()
        pool.tensor_copy(self.norm[:, b, :, :], self.scale_shift[:, :, :]).then_inc(self.scale_ready, 1)

    def act_normalise(self, act, b, n):
        if not self.norm_made:
            act.wait_ge(self.scale_ready, at(b + 1))
        act.wait_ge(self.psum, at(b + 1 - min(len(self.xn), CREDIT)))
        for j in range(J):
            op = act.activation(self.xn[n][:, j, 0:D], self.W["x"][:, b, j, :], ACT.Identity,
                                scale=self.norm[:, b, 0, j:j + 1], bias=self.norm[:, b, 1, j:j + 1])
        op.then_inc(self.rows_ready, 1)

    def pe_transposes(self, pe, b, n):
        pe.wait_ge(self.rows_ready, at(b + 1))
        pe.wait_ge(self.ready, at(b))
        for c in range(C):
            for j in range(J):
                mm = pe.transpose(self.bank[:, c * S + j * P:c * S + (j + 1) * P], self.xn[n][:, j, c:D:C], self.W["ident"][:, :])
        mm.then_inc(self.psum, 1)

    def act_hi(self, act, b, u):
        act.wait_ge(self.psum, at(b + 1))
        act.activation(self.xt[u][0][:, :, :], self.bank.rearrange("p (c s) -> p c s", c=C), ACT.Copy).then_inc(self.hi_ready, 1)

    def dve_lo(self, dve, b, u):
        dve.wait_ge(self.hi_ready, at(b + 1))
        dve.tensor_tensor(self.xt[u][1][:, :, :], self.bank.rearrange("p (c s) -> p c s", c=C),
                          self.xt[u][0][:, :, :].bitcast(F32), ALU.subtract).then_inc(self.ready, 1)


class Router:

    def __init__(self, m, W, columns, layer, ring, ps_logits_t, ps_logits, ps_rank):
        self.tag = (layer + 1) * TAG
        self.W, self.columns, self.ring = W, columns, ring
        self.ps_logits_t, self.ps_logits, self.ps_rank = ps_logits_t, ps_logits, ps_rank
        self.logits_t = m.sb("logits_t", [E, S])
        self.logits = m.sb("logits", [P, J, E])
        self.top = m.sb("top", [P, J, 8])
        self.top_at = m.sb("top_at", [P, J, 8], U32)
        self.first_slot = m.sb("first_slot", [P, J, K])
        self.below_top = m.sb("below_top", [P, J, K])
        self.expo = m.sb("expo", [P, J, K])
        self.expo_sum = m.sb("expo_sum", [P, J])
        self.expo_rec = m.sb("expo_rec", [P, J])
        self.chosen = m.sb("chosen", [P, J, K, E], BF16)
        self.mask_half = m.sb("mask_half", [P, J, K // 2, E], BF16)
        self.mask = m.sb("mask", [P, J, E], BF16)
        self.chosen_rank = m.sb("chosen_rank", [P, J, K, E])
        self.rank = m.sb("rank", [P, J * K])
        self.slot = m.sb("slot", [P, J * K])
        self.kept = m.sb("kept", [P, J * K])
        self.lost = m.sb("lost", [P, J * K])
        self.weight_raw = m.sb("weight_raw", [P, J, K])
        self.scatter_at = [m.sb(f"scatter_at{n}", [P, J * K], U32) for n in range(ring)]
        self.logits_t_psum, self.logits_psum, self.rank_psum = m.sems("logits_t_psum logits_psum rank_psum")
        self.logits_t_ready, self.logits_ready, self.expo_ready = m.sems("logits_t_ready logits_ready expo_ready")
        self.below_ready, self.mask_ready, self.rank_read, self.slots_ready, self.tags_ready = m.sems(
            "below_ready mask_ready rank_read slots_ready tags_ready")
        self.scatter_dma = [m.sem(f"scatter_dma{n}") for n in range(ring)]

    def pe_credits(self, pe):
        for s in (self.logits_t_psum, self.logits_psum, self.rank_psum):
            pe.sem_inc(s, CREDIT)

    def act_credits(self, act):
        for s in (self.logits_t_ready, self.logits_ready, self.expo_ready):
            act.sem_inc(s, CREDIT)

    def dve_credits(self, dve):
        for s in (self.below_ready, self.mask_ready, self.rank_read, self.slots_ready, self.tags_ready):
            dve.sem_inc(s, CREDIT)
        dve.memset(self.W["mask_sum"][:, :], 0.0)

    def act_rows(self, act, b, n):
        act.activation(self.columns.xn[n][:, :, D + K:WIDE], self.W["row_of"][:, b, :, :], ACT.Copy)

    def rows_sent(self, engine, n, before):
        if not isinstance(before, int) or before > 0:
            engine.wait_ge(self.scatter_dma[n], DMA * J * K * before)

    def pe_logits_t(self, pe, b, u):
        pe.wait_ge(self.columns.ready, at(b + 1))
        pe.wait_ge(self.logits_t_ready, at(b))
        for c in range(C):
            mm = split_product(pe, self.ps_logits_t, [w[:, c, :] for w in self.W["router"]],
                               [x[:, c, :] for x in self.columns.xt[u]], c == 0, c == C - 1)
        mm.then_inc(self.logits_t_psum, 1)

    def act_logits_t(self, act, b):
        act.wait_ge(self.logits_t_psum, at(b + 1))
        act.wait_ge(self.logits_psum, at(b))
        act.activation(self.logits_t[:, :], self.ps_logits_t[0:E, :], ACT.Identity,
                       bias=self.W["bias"][0:E, 24:25]).then_inc(self.logits_t_ready, 1)

    def pe_logits(self, pe, b):
        pe.wait_ge(self.logits_t_ready, at(b + 1))
        pe.wait_ge(self.slots_ready, at(b))
        settle(pe, self.W["passed_pe"])
        for j in range(J):
            mm = pe.transpose(self.ps_logits[:, j, :], self.logits_t[:, j * P:(j + 1) * P], self.W["ident"][0:E, 0:E])
        mm.then_inc(self.logits_psum, 1)

    def act_logits(self, act, b):
        act.wait_ge(self.logits_psum, at(b + 1))
        act.wait_ge(self.below_ready, at(b))
        act.activation(self.logits[:, :, :], self.ps_logits, ACT.Copy).then_inc(self.logits_ready, 1)

    def dve_choose(self, dve, b, parts=(0, 1, 2)):
        if 0 in parts:
            dve.wait_ge(self.logits_ready, at(b + 1))
            dve.wait_ge(self.expo_ready, at(b))
            settle(dve, self.W["passed_dve"])
            for j in range(J):
                dve.max(self.top[:, j, :], self.logits[:, j, :])
            dve.drain()
            for j in range(J):
                dve.max_index(self.top_at[:, j, :], self.top[:, j, :], self.logits[:, j, :])
            dve.drain()
        if 1 in parts:
            dve.tensor_tensor(self.below_top[:, :, :], self.top[:, :, 0:K], self.top[:, :, 0:1].to_broadcast([P, J, K]),
                              ALU.subtract).then_inc(self.below_ready, 1)
            dve.tensor_scalar(self.first_slot[:, :, :], self.top_at[:, :, 0:K], float(CAP), None, ALU.mult)
            dve.drain()
            for j in range(J):
                dve.tensor_tensor(self.chosen[:, j, :, :], self.W["first_slot_of"][:, :].unsqueeze(1).to_broadcast([P, K, E]),
                                  self.first_slot[:, j, :].unsqueeze(2).to_broadcast([P, K, E]), ALU.is_equal)
            dve.drain()
        if 2 in parts:
            dve.tensor_tensor(self.mask_half[:, :, :, :], self.chosen[:, :, 0:K // 2, :], self.chosen[:, :, K // 2:K, :], ALU.add)
            dve.drain()
            dve.tensor_tensor(self.mask[:, :, :], self.mask_half[:, :, 0, :], self.mask_half[:, :, 1, :], ALU.add).then_inc(self.mask_ready, 1)

    def act_expo(self, act, b):
        act.wait_ge(self.below_ready, at(b + 1))
        act.wait_ge(self.slots_ready, at(b))
        act.activation(self.expo[:, :, :], self.below_top[:, :, :], ACT.Exp).then_inc(self.expo_ready, 1)

    def pe_rank(self, pe, b):
        pe.wait_ge(self.mask_ready, at(b + 1))
        for j in range(J):
            pe.matmul(self.ps_rank[:, j, :], self.W["ones"][:, :], self.W["mask_sum"][:, :], start=True, stop=False)
            for k in range(j):
                pe.matmul(self.ps_rank[:, j, :], self.W["ones"][:, :], self.mask[:, k, :], start=False, stop=False)
            mm = pe.matmul(self.ps_rank[:, j, :], self.W["before"][:, :], self.mask[:, j, :], start=False, stop=True)
        mm.then_inc(self.rank_psum, 1)

    def dve_place(self, dve, b, n, before, parts=(0, 1, 2)):
        if 0 in parts:
            dve.wait_ge(self.rank_psum, at(b + 1))
            for j in range(J):
                op = dve.tensor_tensor(self.chosen_rank[:, j, :, :], self.chosen[:, j, :, :],
                                       self.ps_rank[:, j, :].unsqueeze(1).to_broadcast([P, K, E]), ALU.mult)
            op.then_inc(self.rank_read, 1)
            dve.tensor_tensor(self.W["mask_sum"][:, :], self.W["mask_sum"][:, :], self.mask[:, 0, :], ALU.add)
            dve.drain()
        if 1 in parts:
            dve.tensor_tensor(self.W["mask_sum"][:, :], self.W["mask_sum"][:, :], self.mask[:, 1, :], ALU.add)
            dve.wait_ge(self.expo_ready, at(b + 1))
            dve.tensor_reduce(self.expo_sum[:, :], self.expo[:, :, :], AX.X, ALU.add)
            dve.tensor_reduce(self.rank[:, :], self.chosen_rank[:, :, :, :].rearrange("p j k e -> p (j k) e"), AX.X, ALU.add)
            dve.drain()
        if 2 in parts:
            dve.reciprocal(self.expo_rec[:, :], self.expo_sum[:, :])
            dve.tensor_scalar(self.lost[:, :], self.rank[:, :], float(CAP), float(DROPPED), ALU.is_ge, ALU.mult)
            dve.scalar_tensor_tensor(out=self.slot[:, :], in0=self.rank[:, :], scalar=float(CAP - 1),
                                     in1=self.first_slot[:, :, :].rearrange("p j k -> p (j k)"), op0=ALU.min, op1=ALU.add)
            dve.tensor_scalar(self.kept[:, :], self.rank[:, :], float(CAP), 0.5, ALU.is_lt, ALU.mult)
            dve.drain()
            self.rows_sent(dve, n, before)
            dve.tensor_tensor(self.scatter_at[n][:, :], self.slot[:, :], self.lost[:, :], ALU.add).then_inc(self.slots_ready, 1)
            dve.scalar_tensor_tensor(out=self.columns.xn[n][:, :, D:D + K], in0=self.slot[:, :].rearrange("p (j k) -> p j k", k=K),
                                     scalar=float(self.tag), in1=self.lost[:, :].rearrange("p (j k) -> p j k", k=K),
                                     op0=ALU.add, op1=ALU.add).then_inc(self.tags_ready, 1)
            dve.tensor_tensor(self.weight_raw[:, :, :], self.expo[:, :, :], self.expo_rec[:, :].unsqueeze(2).to_broadcast([P, J, K]), ALU.mult)
            dve.drain()
            dve.tensor_tensor(self.W["weight"][:, b, :], self.weight_raw[:, :, :].rearrange("p j k -> p (j k)"),
                              self.kept[:, :], ALU.mult)

    def pool_dispatch(self, pool, b, n):
        pool.wait_ge(self.slots_ready, at(b + 1))
        pool.wait_ge(self.tags_ready, at(b + 1))
        settle(pool, self.W["passed_pool"])
        for jk in range(J * K):
            pool.indirect_dma_start(
                self.W["slot_x"], bass.IndirectOffsetOnAxis(ap=self.scatter_at[n][:, jk:jk + 1], axis=0),
                self.columns.xn[n][:, jk // K, :], None, bounds_check=SLOTS - 1, oob_is_err=False,
            ).then_inc(self.scatter_dma[n], DMA)


class Shared:

    def __init__(self, m, W, columns, ps_gu, ps_y):
        self.W, self.columns, self.ps_gu, self.ps_y = W, columns, ps_gu, ps_y
        self.tanh = [m.sb(f"shared_tanh{n}", [P, 2, S]) for n in range(2)]
        self.hidden = m.sb("shared_hidden", [P, HC, S])
        self.gu_psum, self.y_psum, self.tanh_ready, self.hidden_ready, self.x_added = m.sems(
            "shared_gu_psum shared_y_psum shared_tanh_ready shared_hidden_ready shared_x_added")

    def pe_credits(self, pe):
        pe.sem_inc(self.gu_psum, CREDIT)
        pe.sem_inc(self.y_psum, CREDIT)

    def act_credits(self, act):
        act.sem_inc(self.tanh_ready, CREDIT)

    def dve_credits(self, dve):
        dve.sem_inc(self.hidden_ready, CREDIT)
        dve.sem_inc(self.x_added, CREDIT)

    def pe_gate_up(self, pe, b, u, half):
        if half == 0:
            pe.wait_ge(self.columns.ready, at(b + 1))
        for q in (2 * half, 2 * half + 1):
            pe.wait_ge(self.hidden_ready, at(2 * b + half - 1))
            for n, w in enumerate((self.W["gate"], self.W["up"])):
                for c in range(C):
                    mm = split_product(pe, self.ps_gu[:, q, n, :], [v[:, c, q * P:(q + 1) * P] for v in w],
                                       [x[:, c, :] for x in self.columns.xt[u]], c == 0, c == C - 1)
        mm.then_inc(self.gu_psum, 1)

    def act_tanh(self, act, b, half):
        act.wait_ge(self.gu_psum, at(2 * b + half + 1))
        act.wait_ge(self.hidden_ready, at(2 * b + half - 1))
        act.activation(self.tanh[half][:, :, :], self.ps_gu[:, 2 * half:2 * half + 2, 0, :], ACT.Tanh, scale=0.5
                       ).then_inc(self.tanh_ready, 1)

    def dve_hidden(self, dve, b, half):
        q = slice(2 * half, 2 * half + 2)
        dve.wait_ge(self.tanh_ready, at(2 * b + half + 1))
        dve.scalar_tensor_tensor(out=self.tanh[half][:, :, :], in0=self.tanh[half][:, :, :], scalar=1.0,
                                 in1=self.ps_gu[:, q, 0, :], op0=ALU.add, op1=ALU.mult)
        dve.drain()
        dve.wait_ge(self.y_psum, at(b))
        dve.tensor_tensor(self.hidden[:, q, :], self.tanh[half][:, :, :], self.ps_gu[:, q, 1, :], ALU.mult).then_inc(self.hidden_ready, 1)

    def pe_down(self, pe, b, half):
        pe.wait_ge(self.hidden_ready, at(2 * b + half + 1))
        if half == 0:
            pe.wait_ge(self.x_added, at(b))
        for j in range(J):
            for q in (2 * half, 2 * half + 1):
                mm = pe.matmul(self.ps_y[:, j, :], self.hidden[:, q, j * P:(j + 1) * P], self.W["shared_down"][:, q, :],
                               start=(q == 0 and j == 0), stop=(q == HC - 1), skip_group_check=True)
        if half == 1:
            mm.then_inc(self.y_psum, 1)

    def dve_add(self, dve, b):
        dve.wait_ge(self.y_psum, at(b + 1))
        dve.scalar_tensor_tensor(out=self.W["x"][:, b, :, :], in0=self.ps_y[:, :, :], scalar=0.25,
                                 in1=self.W["x"][:, b, :, :], op0=ALU.mult, op1=ALU.add).then_inc(self.x_added, 1)


class Experts:

    QE = 4
    PAIRS = QE // 2
    QUADS = E // QE
    RING0 = 4
    SLOTS = 4

    def __init__(self, nc, ctx, W, a, layer, banks_t, banks_gu, banks_y, ring, split=None):
        m = Memory(nc, ctx, W["kept"], f"experts{layer}", "experts")
        self.W, self.a, self.split, self.layer, self.RING = W, a, split, layer, ring
        R, PAIRS, SLOTS = ring, self.PAIRS, self.SLOTS
        self.w_before = [layer * self.QUADS // self.RING0 if n < self.RING0 else 0 for n in range(R)]
        self.w_gate = [m.sb(f"w_gate{n}", [P, self.QE, C, HID]) for n in range(R)]
        self.w_up = [m.sb(f"w_up{n}", [P, self.QE, C, HID]) for n in range(R)]
        self.w_down = [m.sb(f"w_down{n}", [P, PAIRS, D]) for n in range(R)]
        self.slot_in = [m.sb(f"slot_in{n}", [P, PAIRS, WIDE]) for n in range(SLOTS)]
        self.slot_out = [m.sb(f"slot_out{n}", [P, PAIRS, D]) for n in range(SLOTS)]
        self.mine = m.sb("mine", [P, PAIRS, K])
        self.my_rows = m.sb("my_rows", [P, PAIRS, K])
        self.row = m.sb("row", [P, PAIRS])
        self.row_at = [m.sb(f"row_at{n}", [P, PAIRS], U32) for n in range(SLOTS)]
        self.slot_t = [m.sb(f"slot_t{n}", [P, PAIRS, C, P]) for n in range(2)]
        self.tanh = [m.sb(f"tanh{n}", [P, PAIRS, CAP]) for n in range(2)]
        self.gate = [m.sb(f"gate{n}", [P, PAIRS, CAP]) for n in range(2)]
        self.hidden = [m.sb(f"hidden{n}", [P, PAIRS, P]) for n in range(2)]
        self.ps_t = banks_t
        self.ps_gu = [b[:, 0:2 * PAIRS * CAP].rearrange("p (s r t) -> p s r t", s=2, t=CAP) for b in banks_gu]
        self.ps_y = [b[:, :].rearrange("p (r d) -> p r d", d=D) for b in banks_y]
        self.t_psum, self.gu_psum, self.y_psum = m.sems("t_psum gu_psum y_psum")
        self.t_ready, self.tanh_ready, self.out_ready, self.split_hi = m.sems("t_ready tanh_ready out_ready split_hi")
        self.hidden_ready, self.row_ready, self.split_lo = m.sems("hidden_ready row_ready split_lo")
        self.w_dma = [m.sem(f"w_dma{n}") for n in range(R)]
        self.slot_dma = [m.sem(f"slot_dma{n}") for n in range(SLOTS)]
        self.routed_dma = [m.sem(f"routed_dma{n}") for n in range(SLOTS)]
        if split:
            self.raw_copied, self.raw_dma = m.sems("raw_copied raw_dma")

    def exists(self, i, n):
        return not isinstance(i, int) or 0 <= self.RING * i + n < self.QUADS

    def steps(self, engine, step):
        with engine.Fori(0, self.QUADS // self.RING - 1) as i:
            for n in range(self.RING):
                step(i, n)
        for n in range(self.RING):
            step(self.QUADS // self.RING - 1, n)

    def at(self, n):
        return at(n + self.layer * self.QUADS)

    def weight_uses(self, i, n):
        return i + n // self.RING + 1 + self.w_before[n % self.RING]

    def slot_uses(self, i, n):
        return self.RING // self.SLOTS * i + n // self.SLOTS + 1 + self.layer * (self.QUADS // self.SLOTS)

    def stored(self, engine):
        for n in range(self.SLOTS):
            engine.wait_ge(self.routed_dma[n], DMA * self.PAIRS * (1 + self.layer) * (self.QUADS // self.SLOTS))


    def load_weights(self, sp, i, n):
        q, r = self.RING * i + n, n % self.RING
        for buffer, name in ((self.w_gate, "L0_ffn_Wg"), (self.w_up, "L0_ffn_Wu")):
            sp.dma_start(buffer[r][:, :, :, :], self.a[name].rearrange("e (p c) h -> p e c h", c=C)[
                :, bass.ds(q * self.QE, self.QE), :, :]).then_inc(self.w_dma[r], DMA)
        sp.dma_start(self.w_down[r][:, :, :], self.a["L0_ffn_Wd"].rearrange("(r two) h d -> (two h) r d", two=2)[
            :, bass.ds(q * self.PAIRS, self.PAIRS), :]).then_inc(self.w_dma[r], DMA)

    def load_slots(self, sp, i, n):
        q, r = self.RING * i + n, n % self.RING
        sp.dma_start(self.slot_in[n % self.SLOTS][:, :, :], self.W["slot_x"].rearrange("(q r p) d -> q p r d", p=P, r=self.PAIRS)[
            q]).then_inc(self.slot_dma[n % self.SLOTS], DMA)

    def copy_split(self, sp):
        for raw, name in ((self.W["raw_wq"], "L0_attn_Wq"), (self.W["raw_wo"], "L0_attn_Wo")):
            sp.dma_start(raw[:, :], self.a[name][:, :]).then_inc(self.raw_copied, DMA)

    def load_split(self, sp, part):
        if part == 0:
            sp.wait_ge(self.raw_copied, 2 * DMA)
            sp.dma_start(self.W["wq"][1][:, :, :].bitcast(F32), self.W["raw_wq"].rearrange("(p c) n -> p c n", c=C)
                         ).then_inc(self.raw_dma, DMA)
        else:
            sp.dma_start(self.W["wo"][1][:, :, :].bitcast(F32), self.W["raw_wo"].rearrange("(h p) d -> p h d", p=P)
                         ).then_inc(self.raw_dma, DMA)

    def sp_first(self, sp):
        for n in range(self.SLOTS):
            self.load_slots(sp, 0, n)

    def sp_steps(self, sp):
        def step(i, n):
            q = self.RING * i + n
            if self.exists(i, n + self.SLOTS):
                sp.wait_ge(self.t_psum, self.at(q + 1))
                sp.wait_ge(self.row_ready, self.at(q + 1))
                self.load_slots(sp, i, n + self.SLOTS)
            if self.exists(i, n + self.RING):
                sp.wait_ge(self.y_psum, self.at(q + 1))
                self.load_weights(sp, i, n + self.RING)

        self.steps(sp, step)


    def pool_steps(self, pool):
        def step(i, n):
            q, r = self.RING * i + n, n % self.SLOTS
            pool.wait_ge(self.row_ready, self.at(q + 1))
            pool.wait_ge(self.out_ready, self.at(q + 1))
            settle(pool, self.W["passed_pool"])
            for pair in range(self.PAIRS):
                pool.indirect_dma_start(
                    self.W["routed"], bass.IndirectOffsetOnAxis(ap=self.row_at[r][:, pair:pair + 1], axis=0),
                    self.slot_out[r][:, pair, :], None, bounds_check=ROWS - 1, oob_is_err=False,
                ).then_inc(self.routed_dma[r], DMA)

        self.steps(pool, step)


    def pe_credits(self, pe):
        if self.layer == 0:
            for s in (self.t_psum, self.gu_psum, self.y_psum):
                pe.sem_inc(s, CREDIT)

    def pe_steps(self, pe):
        W = self.W

        def columns(i, n):
            q = self.RING * i + n
            pe.wait_ge(self.slot_dma[n % self.SLOTS], DMA * self.slot_uses(i, n))
            pe.wait_ge(self.t_ready, self.at(q - 1))
            for r in range(self.PAIRS):
                for c in range(C):
                    mm = pe.transpose(self.ps_t[n % 2][:, r, c, :], self.slot_in[n % self.SLOTS][:, r, c:D:C], W["ident"][:, :])
            mm.then_inc(self.t_psum, 1)

        def gate_up(i, n):
            q = self.RING * i + n
            pe.wait_ge(self.w_dma[n % self.RING], 3 * DMA * self.weight_uses(i, n))
            pe.wait_ge(self.t_ready, self.at(q + 1))
            pe.wait_ge(self.hidden_ready, self.at(q - 1))
            settle(pe, self.W["passed_pe"])
            for k in range(self.QE):
                r, odd = k // 2, (k % 2) * CAP
                x = self.slot_t[n % 2][:, r, :, odd:odd + CAP]
                for s, w in enumerate((self.w_gate[n % self.RING], self.w_up[n % self.RING])):
                    for c in range(C):
                        mm = pe.matmul(self.ps_gu[n % 2][odd:odd + HID, s, r, :], w[:, k, c, :], x[:, c, :],
                                       start=(c == 0), stop=(c == C - 1))
            mm.then_inc(self.gu_psum, 1)

        def down(i, n):
            q = self.RING * i + n
            pe.wait_ge(self.hidden_ready, self.at(q + 1))
            pe.wait_ge(self.out_ready, self.at(q - 1))
            for r in range(self.PAIRS):
                mm = pe.matmul(self.ps_y[n % 2][:, r, :], self.hidden[n % 2][:, r, :], self.w_down[n % self.RING][:, r, :],
                               start=True, stop=True)
            mm.then_inc(self.y_psum, 1)

        def step(i, n):
            if self.exists(i, n + 1):
                gate_up(i, n + 1)
            if self.exists(i, n + 2):
                columns(i, n + 2)
            down(i, n)

        columns(0, 0)
        columns(0, 1)
        gate_up(0, 0)
        self.steps(pe, step)


    def act_credits(self, act):
        if self.layer == 0:
            for s in (self.t_ready, self.tanh_ready, self.out_ready, self.split_hi):
                act.sem_inc(s, CREDIT)

    def act_steps(self, act):
        W = self.W

        def columns(i, n):
            q = self.RING * i + n
            act.wait_ge(self.t_psum, self.at(q + 1))
            act.wait_ge(self.gu_psum, self.at(q - 1))
            act.activation(self.slot_t[n % 2][:, :, :, :], self.ps_t[n % 2][:, :, :, :], ACT.Copy).then_inc(self.t_ready, 1)

        def tanh(i, n):
            q = self.RING * i + n
            act.wait_ge(self.gu_psum, self.at(q + 1))
            act.wait_ge(self.hidden_ready, self.at(q - 1))
            act.activation(self.tanh[n % 2][:, :, :], self.ps_gu[n % 2][:, 0, :, :], ACT.Tanh, scale=0.5
                           ).then_inc(self.tanh_ready, 1)

        def results(i, n):
            q = self.RING * i + n
            act.wait_ge(self.y_psum, self.at(q + 1))
            if not isinstance(i, int) or self.layer or self.RING * i + n >= self.SLOTS:
                act.wait_ge(self.routed_dma[n % self.SLOTS], DMA * self.PAIRS * (self.slot_uses(i, n) - 1))
            act.activation(self.slot_out[n % self.SLOTS][:, :, :], self.ps_y[n % 2][:, :, :], ACT.Copy).then_inc(self.out_ready, 1)

        def split(i, n):
            q = self.RING * i + n
            act.activation(W["wq"][0][:, :, bass.ds(q * DH, DH)], W["wq"][1][:, :, bass.ds(q * DH, DH)].bitcast(F32), ACT.Copy, scale=SCALE)
            act.activation(W["wo"][0][:, q, :], W["wo"][1][:, q, :].bitcast(F32), ACT.Copy).then_inc(self.split_hi, 1)

        def step(i, n):
            if self.exists(i, n + 1):
                tanh(i, n + 1)
            if self.exists(i, n + 2):
                columns(i, n + 2)
            results(i, n)
            if self.split:
                split(i, n)

        if self.split:
            act.wait_ge(self.raw_dma, 2 * DMA)
        columns(0, 0)
        columns(0, 1)
        tanh(0, 0)
        for n in range(self.RING):
            step(0, n)
        if self.QUADS // self.RING > 2:
            with act.Fori(1, self.QUADS // self.RING - 1) as i:
                for n in range(self.RING):
                    step(i, n)
        for n in range(self.RING):
            step(self.QUADS // self.RING - 1, n)


    def dve_credits(self, dve):
        if self.layer == 0:
            for s in (self.hidden_ready, self.row_ready, self.split_lo):
                dve.sem_inc(s, CREDIT)
        for n in range(2):
            dve.memset(self.hidden[n][:, :, :], 0.0)

    def dve_steps(self, dve):
        W = self.W

        def hidden(i, n):
            q = self.RING * i + n
            dve.wait_ge(self.tanh_ready, self.at(q + 1))
            gate, up = self.ps_gu[n % 2][:, 0, :, :], self.ps_gu[n % 2][:, 1, :, :]
            dve.scalar_tensor_tensor(out=self.gate[n % 2][:, :, :], in0=self.tanh[n % 2][:, :, :], scalar=1.0, in1=gate,
                                     op0=ALU.add, op1=ALU.mult)
            dve.drain()
            dve.wait_ge(self.y_psum, self.at(q - 1))
            for odd in range(0, P, CAP):
                op = dve.scalar_tensor_tensor(out=self.hidden[n % 2][odd:odd + HID, :, odd:odd + CAP],
                                              in0=self.gate[n % 2][odd:odd + HID, :, :], scalar=0.5,
                                              in1=up[odd:odd + HID, :, :], op0=ALU.mult, op1=ALU.mult)
            op.then_inc(self.hidden_ready, 1)

        def split(i, n):
            q = self.RING * i + n
            dve.wait_ge(self.split_hi, self.at(q + 1))
            hi, lo = (w[:, :, bass.ds(q * DH, DH)] for w in W["wq"])
            dve.scalar_tensor_tensor(out=lo, in0=lo.bitcast(F32), scalar=SCALE, in1=hi.bitcast(F32),
                                     op0=ALU.mult, op1=ALU.subtract)
            hi, lo = (w[:, q, :] for w in W["wo"])
            dve.tensor_tensor(lo, lo.bitcast(F32), hi.bitcast(F32), ALU.subtract).then_inc(self.split_lo, 1)

        def rows(i, n):
            q, r = self.RING * i + n, n % self.SLOTS
            dve.wait_ge(self.slot_dma[r], DMA * self.slot_uses(i, n))
            dve.tensor_tensor(self.mine[:, :, :], self.slot_in[r][:, :, D:D + K],
                              W["own_slot"][:, q, :].unsqueeze(2).to_broadcast([P, self.PAIRS, K]), ALU.is_equal)
            dve.drain()
            dve.tensor_tensor(self.my_rows[:, :, :], self.mine[:, :, :], self.slot_in[r][:, :, D + K:WIDE], ALU.mult)
            dve.drain()
            dve.tensor_reduce(self.row[:, :], self.my_rows[:, :, :], AX.X, ALU.add)
            dve.drain()
            if not isinstance(i, int) or self.layer or self.RING * i + n >= self.SLOTS:
                dve.wait_ge(self.routed_dma[r], DMA * self.PAIRS * (self.slot_uses(i, n) - 1))
            dve.tensor_scalar(self.row_at[r][:, :], self.row[:, :], float(NOWHERE), None, ALU.add).then_inc(self.row_ready, 1)

        def step(i, n):
            if self.exists(i, n + 1):
                hidden(i, n + 1)
            rows(i, n)
            if self.split:
                split(i, n)

        hidden(0, 0)
        for n in range(self.RING):
            step(0, n)
        if self.QUADS // self.RING > 2:
            with dve.Fori(1, self.QUADS // self.RING - 1) as i:
                for n in range(self.RING):
                    step(i, n)
        for n in range(self.RING):
            step(self.QUADS // self.RING - 1, n)


def first_ffn_phase(nc, W, a):
    RING = 4
    with ExitStack() as ctx:
        m = Memory(nc, ctx, W["kept"], "ffn0")
        ps_xt = m.ps("xt", [P, 512])
        ps_logits_t = m.ps("logits_t", [P, 512])
        ps_route = m.ps("route", [P, 512])
        ps_gu = m.ps("gate_up", [P, HC, 2, S])
        ps_y = m.ps("y", [P, J, D])
        logits_bank, rank_bank = (ps_route[:, n * J * E:(n + 1) * J * E].rearrange("p (j e) -> p j e", e=E) for n in range(2))
        xn = [m.sb(f"xn{n}", [P, J, WIDE]) for n in range(RING)]
        xt = [[m.sb(f"xt{u}{part}", [P, C, S], F32R) for part in ("hi", "lo")] for u in range(2)]
        norm = m.sb("norm", [P, NB, 2, J])
        columns = Columns(m, W, norm, xn, xt, ps_xt[:, :])
        router = Router(m, W, columns, 0, RING, ps_logits_t[:, 0:S], logits_bank, rank_bank)
        shared = Shared(m, W, columns, ps_gu, ps_y)
        gu_banks = [ps_gu[:, q, :, :].rearrange("p s t -> p (s t)") for q in range(HC)]
        experts = Experts(nc, ctx, W, a, 0,
                          [b[:, :].rearrange("p (r c m) -> p r c m", c=C, m=P) for b in (ps_xt, ps_logits_t)],
                          gu_banks[0:2], gu_banks[2:4], Experts.RING0, split=True)
        raw_kv = shared.hidden[:, :, :].rearrange("p q s -> p (q s)").rearrange("p (c n) -> p c n", c=C)
        kv_dma, raw_hi, raw_lo = m.sems("kv_dma raw_hi raw_lo")
        parts = (columns, router, shared, experts)

        def exists(i, n):
            return not isinstance(i, int) or RING * i + n < NB

        def rounds(engine, step):
            with engine.Fori(0, NB // RING - 1) as i:
                for n in range(RING):
                    step(i, n)
            for n in range(RING):
                step(NB // RING - 1, n)

        with nc.Block() as block:

            @block.sync
            def _(sp):
                for n in range(experts.RING):
                    experts.load_weights(sp, 0, n)
                rows = W["routed"].rearrange("(p r) d -> p (r d)", p=P)
                for b in range(NB - 1):
                    sp.wait_ge(shared.hidden_ready, at(2 * b + 1))
                    if b == 0:
                        experts.copy_split(sp)
                    elif b in (3, 4):
                        experts.load_split(sp, b - 3)
                    else:
                        for n in {1: (0, 1), 2: (2, 3), 5: (4, 5), 6: (6, 7)}[b]:
                            sp.dma_start(rows[:, n * 8 * D:(n + 1) * 8 * D], W["zeros"][:, 0:8 * D]).then_inc(W["routed_zeroed"], DMA)
                sp.wait_ge(shared.y_psum, at(NB))
                sp.dma_start(raw_kv, a["L0_attn_Wk"].rearrange("(p c) n -> p c n", c=C)).then_inc(kv_dma, DMA)
                for n in range(RING):
                    router.rows_sent(sp, n, NB // RING)
                experts.sp_first(sp)
                sp.wait_ge(raw_lo, 1)
                sp.dma_start(raw_kv, a["L0_attn_Wv"].rearrange("(p c) n -> p c n", c=C)).then_inc(kv_dma, DMA)
                experts.sp_steps(sp)
                experts.stored(sp)

            @block.gpsimd
            def _(pool):
                columns.pool_credits(pool)

                def step(i, n):
                    if exists(i, n + 3):
                        columns.pool_scale(pool, RING * i + n + 3)
                    router.pool_dispatch(pool, RING * i + n, n)

                for b in range(3):
                    columns.pool_scale(pool, b)
                pool.wait_ge(W["slots_zeroed"], 4 * DMA)
                rounds(pool, step)
                pool.wait_ge(W["routed_zeroed"], 8 * DMA)
                experts.pool_steps(pool)

            @block.tensor
            def _(pe):
                for part in parts:
                    part.pe_credits(pe)

                def step(i, n):
                    b, u = RING * i + n, n % 2
                    ahead = exists(i, n + 1)
                    shared.pe_gate_up(pe, b, u, 0)
                    if ahead:
                        columns.pe_transposes(pe, b + 1, (n + 1) % RING)
                    if not ahead:
                        router.pe_rank(pe, b)
                    shared.pe_gate_up(pe, b, u, 1)
                    if ahead:
                        router.pe_rank(pe, b)
                    shared.pe_down(pe, b, 0)
                    if ahead:
                        router.pe_logits_t(pe, b + 1, 1 - u)
                    shared.pe_down(pe, b, 1)
                    if ahead:
                        router.pe_logits(pe, b + 1)

                columns.pe_transposes(pe, 0, 0)
                router.pe_logits_t(pe, 0, 0)
                router.pe_logits(pe, 0)
                pe.wait_ge(W["down_in"], DMA)
                rounds(pe, step)
                experts.pe_steps(pe)

            @block.scalar
            def _(act):
                for part in parts:
                    part.act_credits(act)

                def normalise(i, n):
                    r = n % RING
                    router.rows_sent(act, r, i + n // RING)
                    router.act_rows(act, RING * i + n, r)
                    columns.act_normalise(act, RING * i + n, r)

                def step(i, n):
                    b, u = RING * i + n, n % 2
                    ahead = exists(i, n + 1)
                    shared.act_tanh(act, b, 0)
                    if ahead:
                        columns.act_hi(act, b + 1, 1 - u)
                    shared.act_tanh(act, b, 1)
                    if exists(i, n + 2):
                        normalise(i, n + 2)
                    if ahead:
                        router.act_logits_t(act, b + 1)
                        router.act_logits(act, b + 1)
                        router.act_expo(act, b + 1)

                normalise(0, 0)
                columns.act_hi(act, 0, 0)
                act.wait_ge(W["x_in"], DMA)
                normalise(0, 1)
                router.act_logits_t(act, 0)
                router.act_logits(act, 0)
                router.act_expo(act, 0)
                rounds(act, step)
                act.wait_ge(W["slots_zeroed"], 4 * DMA)
                act.wait_ge(W["routed_zeroed"], 8 * DMA)
                for n, w in enumerate((W["wk"], W["wv"])):
                    act.wait_ge(kv_dma, DMA * (n + 1))
                    act.activation(w[0][:, :, :], raw_kv, ACT.Copy).then_inc(raw_hi, 1)
                    if n == 0:
                        experts.act_steps(act)

            @block.vector
            def _(dve):
                for part in parts:
                    part.dve_credits(dve)

                def step(i, n):
                    b, u = RING * i + n, n % 2
                    ahead = exists(i, n + 1)
                    shared.dve_hidden(dve, b, 0)
                    if ahead:
                        columns.dve_lo(dve, b + 1, 1 - u)
                    if exists(i, n + 3):
                        columns.dve_moments(dve, b + 3)
                    if not ahead:
                        router.dve_place(dve, b, n, i)
                    shared.dve_hidden(dve, b, 1)
                    if ahead:
                        router.dve_place(dve, b, n, i)
                    if ahead:
                        router.dve_choose(dve, b + 1)
                    shared.dve_add(dve, b)

                columns.dve_moments(dve, 0)
                columns.dve_lo(dve, 0, 0)
                dve.wait_ge(W["x_in"], DMA)
                columns.dve_moments(dve, 1)
                router.dve_choose(dve, 0)
                columns.dve_moments(dve, 2)
                dve.wait_ge(W["x_rest_in"], DMA)
                rounds(dve, step)
                for n, w in enumerate((W["wk"], W["wv"])):
                    dve.wait_ge(raw_hi, n + 1)
                    dve.tensor_tensor(w[1][:, :, :], raw_kv, w[0][:, :, :].bitcast(F32), ALU.subtract).then_inc(raw_lo, 1)
                    if n == 0:
                        experts.dve_steps(dve)


def last_ffn_phase(nc, W, a):
    EARLY = 6
    FETCH = 6
    POOLS = (1, 3)
    ORDER = (0, 2, 1, 4, 3, 5, 6, 7)
    LAST = NB - 1
    with ExitStack() as ctx:
        m = Memory(nc, ctx, W["kept"], "ffn1")
        m_route = Memory(nc, ctx, W["kept"], "route2", "route1")
        ps_xt = m.ps("xt", [P, 512])
        ps_t = m.ps("t", [P, 512])
        ps_route = m.ps("route", [P, 512])
        ps_gu = m.ps("gate_up", [P, HC, 2, S])
        ps_y = m.ps("y", [P, J, D])
        logits_bank, rank_bank = (ps_route[:, S + n * J * E:S + (n + 1) * J * E].rearrange("p (j e) -> p j e", e=E) for n in range(2))
        xn = [m.sb(f"xn{n}", [P, J, D]) for n in range(2)]
        xt = [[m.sb(f"xt{u}{part}", [P, C, S], F32R) for part in ("hi", "lo")] for u in range(2)]
        columns = Columns(m, W, W["norm1"], xn, xt, ps_xt[:, :], norm_made=True)
        columns1 = Columns(m_route, W, W["norm1"], [m_route.sb("xn", [P, J, WIDE])],
                           [[m_route.sb(f"xt_{part}", [P, C, S], F32R) for part in ("hi", "lo")]], ps_t[:, :])
        router = Router(m_route, W, columns1, 1, 1, ps_route[:, 0:S], logits_bank, rank_bank)
        shared = Shared(m, W, columns, ps_gu, ps_y)
        gu_banks = [ps_gu[:, q, :, :].rearrange("p s t -> p (s t)") for q in range(HC)]
        experts = Experts(nc, ctx, W, a, 1,
                          [b[:, :].rearrange("p (r c m) -> p r c m", c=C, m=P) for b in (ps_xt, ps_t)],
                          gu_banks[0:2], gu_banks[2:4], 2 * Experts.RING0)
        gathered = [m.sb(f"gathered{n}", [P, J * K, D]) for n in range(FETCH)]
        weight = m.sb("weight", [P, J * K])
        routed_sum = m.sb("routed_sum", [P, J, D])
        combined, combined_pool, out_dma = m.sems("combined combined_pool out_dma")
        gather_dma = [m.sem(f"gather_dma{n}") for n in range(FETCH)]
        parts = (columns, shared)

        def exists(b):
            return not isinstance(b, int) or b < NB

        with nc.Block() as block:

            @block.sync
            def _(sp):
                for n in range(experts.RING):
                    experts.load_weights(sp, 0, n)
                router.rows_sent(sp, 0, NB)
                experts.sp_first(sp)
                experts.sp_steps(sp)
                experts.stored(sp)

                def fetch(b):
                    sp.dma_start(gathered[b % FETCH][:, :, :].rearrange("p (j k) d -> p j (k d)", k=K),
                                 W["routed"].rearrange("(b j p k) d -> b p j (k d)", p=P, j=J, k=K)[b]
                                 ).then_inc(gather_dma[b % FETCH], DMA)

                for b in range(FETCH):
                    fetch(b)
                for b in ORDER:
                    if b in POOLS:
                        sp.wait_ge(combined_pool, POOLS.index(b) + 1)
                    else:
                        sp.wait_ge(combined, at(b + 1 - sum(p < b for p in POOLS)))
                    if b + FETCH < NB:
                        fetch(b + FETCH)
                    sp.dma_start(a["out"].rearrange("b (j p) d -> b p j d", p=P)[b], W["x"][:, b, :, :]).then_inc(out_dma, DMA)
                sp.wait_ge(out_dma, NB * DMA)

            @block.gpsimd
            def _(pool):
                columns1.pool_scale(pool, LAST)
                router.pool_dispatch(pool, LAST, 0)
                experts.pool_steps(pool)
                for n, b in enumerate(POOLS):
                    pool.drain()
                    pool.tensor_copy(weight[:, :], W["weight"][:, b, :])
                    pool.drain()
                    pool.wait_ge(gather_dma[b % FETCH], DMA * (b // FETCH + 1))
                    pool.wait_ge(shared.x_added, at(b + 1))
                    pool_combine(pool, W, gathered[b % FETCH], weight, routed_sum, b, combined_pool)

            @block.tensor
            def _(pe):
                for part in parts:
                    part.pe_credits(pe)

                def round_(b, u, between=lambda: None):
                    shared.pe_gate_up(pe, b, u, 0)
                    if exists(b + 1):
                        columns.pe_transposes(pe, b + 1, 1 - u)
                    between()
                    shared.pe_gate_up(pe, b, u, 1)
                    for half in range(2):
                        shared.pe_down(pe, b, half)

                columns.pe_transposes(pe, 0, 0)
                columns1.pe_transposes(pe, LAST, 0)
                round_(0, 0, lambda: router.pe_logits_t(pe, LAST, 0))
                router.pe_logits(pe, LAST)
                round_(1, 1, lambda: router.pe_rank(pe, LAST))
                for b in range(2, EARLY):
                    round_(b, b % 2)
                pe.wait_ge(columns.ready, at(EARLY + 1))
                experts.pe_steps(pe)
                pe.wait_ge(experts.out_ready, experts.at(experts.QUADS))
                for b in range(EARLY, NB):
                    round_(b, b % 2)

            @block.scalar
            def _(act):
                for part in parts:
                    part.act_credits(act)

                def round_(b, u, between=lambda: None):
                    shared.act_tanh(act, b, 0)
                    if exists(b + 1):
                        columns.act_hi(act, b + 1, 1 - u)
                    between()
                    shared.act_tanh(act, b, 1)
                    if exists(b + 2):
                        columns.act_normalise(act, b + 2, u)

                columns.act_normalise(act, 0, 0)
                columns.act_hi(act, 0, 0)
                router.rows_sent(act, 0, LAST)
                router.act_rows(act, LAST, 0)
                columns1.act_normalise(act, LAST, 0)
                columns1.act_hi(act, LAST, 0)
                columns.act_normalise(act, 1, 1)
                round_(0, 0, lambda: router.act_logits_t(act, LAST))
                router.act_logits(act, LAST)
                round_(1, 1, lambda: router.act_expo(act, LAST))
                for b in range(2, EARLY):
                    round_(b, b % 2)
                experts.act_steps(act)
                for b in range(EARLY, NB):
                    round_(b, b % 2)

            @block.vector
            def _(dve):
                for part in parts:
                    part.dve_credits(dve)
                dve.sem_inc(combined, CREDIT)
                experts.dve_credits(dve)

                def round_(b, u, between=lambda: None, close=lambda: None):
                    shared.dve_hidden(dve, b, 0)
                    if exists(b + 1):
                        columns.dve_lo(dve, b + 1, 1 - u)
                    between()
                    shared.dve_hidden(dve, b, 1)
                    close()
                    shared.dve_add(dve, b)

                def routed(b):
                    dve.drain()
                    dve.wait_ge(gather_dma[b % FETCH], DMA * (b // FETCH + 1))
                    combine(dve, W, gathered[b % FETCH], b, combined)

                dve.tensor_scalar(W["own_slot"][:, :, :], W["own_slot"][:, :, :], float(TAG), None, ALU.add)
                columns1.dve_moments(dve, LAST)
                columns.dve_lo(dve, 0, 0)
                columns1.dve_lo(dve, LAST, 0)
                round_(0, 0)
                router.dve_choose(dve, LAST)
                round_(1, 1)
                router.dve_place(dve, LAST, 0, LAST)
                for b in range(2, EARLY):
                    round_(b, b % 2)
                experts.dve_steps(dve)
                own = [b for b in range(NB) if b not in POOLS]
                for b in range(EARLY, NB):
                    round_(b, b % 2, close=lambda: routed(own[b - EARLY]))
                for b in own[NB - EARLY:]:
                    routed(b)


def combine(engine, W, gathered, b, done):
    for k in range(K):
        for j in range(J):
            op = engine.scalar_tensor_tensor(out=W["x"][:, b, j, :], in0=gathered[:, j * K + k, :],
                                             scalar=W["weight"][:, b, j * K + k:j * K + k + 1], in1=W["x"][:, b, j, :],
                                             op0=ALU.mult, op1=ALU.add)
        if k < K - 1:
            engine.drain()
    op.then_inc(done, 1)


def pool_combine(pool, W, gathered, weight, total, b, done):
    rows = gathered[:, :, :].rearrange("p (j k) d -> p j k d", k=K)
    pool.tensor_tensor(gathered[:, :, :], gathered[:, :, :], weight[:, :].unsqueeze(2).to_broadcast([P, J * K, D]), ALU.mult)
    pool.drain()
    pool.tensor_tensor(rows[:, :, 0:2, :], rows[:, :, 0:2, :], rows[:, :, 2:4, :], ALU.add)
    pool.drain()
    pool.tensor_tensor(total[:, :, :], rows[:, :, 0, :], rows[:, :, 1, :], ALU.add)
    pool.drain()
    pool.tensor_tensor(W["x"][:, b, :, :], W["x"][:, b, :, :], total[:, :, :], ALU.add).then_inc(done, 1)


def attention_phase(nc, W, a):
    HEADS = NB * H
    with ExitStack() as ctx:
        m = Memory(nc, ctx, W["kept"], "attn")
        m_route = Memory(nc, ctx, W["kept"], "route1")
        X = W["x"]
        gathered = m.sb("gathered", [P, J * K, D])
        weight = m.sb("weight", [P, J * K])
        routed = m.sb("routed", [P, J, D])

        def halves(name, shape, m=m):
            return [m.sb(f"{name}_{part}", shape, F32R) for part in ("hi", "lo")]

        xn = [m.sb("xn", [P, J, D])]
        xt = [halves(f"xt{u}", [P, C, S]) for u in range(2)]
        keys = [halves(f"keys{u}", [P, KV, S]) for u in range(2)]
        vals = [halves(f"vals{u}", [P, J, KV * DH]) for u in range(2)]
        qt = [halves(f"qt{n}", [P, S]) for n in range(2)]
        prob = [m.sb(f"prob{n}", [P, J, S]) for n in range(2)]
        prob_t = [halves(f"prob_t{n}", [P, J, S]) for n in range(2)]
        ot = [halves(f"ot{n}", [P, S]) for n in range(2)]
        neg_max = [m.sb(f"neg_max{n}", [P, J]) for n in range(2)]
        row_sum = [m.sb(f"row_sum{n}", [P, J]) for n in range(2)]
        row_rec = [m.sb(f"row_rec{n}", [P, J]) for n in range(2)]
        norm = m.sb("norm", [P, NB, 2, J])

        ps_prep = m.ps("prep", [P, 512])
        ps_q = m.ps("q", [P, 512])
        ps_s = [m.ps(f"s{n}", [P, J, S]) for n in range(2)]
        ps_pt = [m.ps(f"pt{n}", [P, J, S]) for n in range(2)]
        ps_o = m.ps("o", [P, 512])
        ps_y = m.ps("y", [P, J, D])

        first_banks = [t[:, :, :].rearrange("p j s -> p (j s)") for t in (*ps_s, *ps_pt, ps_y)] + [ps_prep[:, :]]

        columns = Columns(m, W, norm, xn, xt, ps_prep[:, :])
        columns1 = Columns(m_route, W, W["norm1"], [m_route.sb("xn", [P, J, WIDE])],
                           [halves("xt", [P, C, S], m_route)], ps_prep[:, :])
        logits_bank, rank_bank = (ps_prep[:, n * J * E:(n + 1) * J * E].rearrange("p (j e) -> p j e", e=E) for n in range(2))
        router = Router(m_route, W, columns1, 1, 1, ps_prep[:, 0:S], logits_bank, rank_bank)
        parts = (columns, columns1, router)

        q_psum, s_psum, pt_psum, o_psum, y_psum, k_psum, v_psum = m.sems("q_psum s_psum pt_psum o_psum y_psum k_psum v_psum")
        q_hi, exp_ready, p1_ready, pt_hi, o_hi, k_hi, v_hi = m.sems("q_hi exp_ready p1_ready pt_hi o_hi k_hi v_hi")
        q_ready, max_ready, rec_ready, p0_ready, pt_ready, o_ready, k_ready, v_ready, x_added = m.sems(
            "q_ready max_ready rec_ready p0_ready pt_ready o_ready k_ready v_ready x_added")
        combined, bias_added, gather_dma = m.sems("combined bias_added gather_dma")

        LOOPS = NB // 2 - 1
        TWO = 2 * H

        def exists(i, c):
            return not isinstance(i, int) or 0 <= TWO * i + c < HEADS

        def next_batch(i, c):
            return c >= 0 and (not isinstance(i, int) or 2 * i + c // H + 1 < NB)

        def last_batch(i, c):
            return c >= 0 and (not isinstance(i, int) or 2 * i + c // H >= 1)

        def prep_bank(b, n):
            return first_banks[n] if isinstance(b, int) and b == 0 else ps_prep[:, :]

        def bias(first, n):
            return W["bias"][:, first + n:first + n + 1]

        MOMENTS, NORMALISE, COLUMNS, KEYS, VALUES = 3, 5, 6, 7, 12
        MOMENTS1, NORMALISE1, COLUMNS1, LOGITS_T, LOGITS, CHOOSE, RANK = 0, 2, 3, 4, 5, 5, 11

        def walk(engine, step):
            for c in range(-5, H):
                step(0, c)
            with engine.Fori(0, LOOPS) as i:
                for c in range(H, H + TWO):
                    step(i, c)
            for c in range(H, TWO):
                step(LOOPS, c)

        with nc.Block() as block:

            @block.sync
            def _(sp):
                with sp.Fori(0, NB) as b:
                    sp.wait_ge(combined, at(b))
                    sp.dma_start(gathered[:, :, :].rearrange("p (j k) d -> p j (k d)", k=K),
                                 W["routed"].rearrange("(b j p k) d -> b p j (k d)", p=P, j=J, k=K)[b]).then_inc(gather_dma, DMA)

            @block.gpsimd
            def _(pool):
                columns.pool_credits(pool)
                columns1.pool_credits(pool)
                pool.sem_inc(bias_added, CREDIT)

                def prepare(b):
                    pool.tensor_copy(weight[:, :], W["weight"][:, b, :])
                    pool.drain()
                    pool.wait_ge(gather_dma, DMA * (b + 1))
                    settle(pool, W["passed_pool"])
                    pool_combine(pool, W, gathered, weight, routed, b, combined)
                    norms(b)

                def norms(b):
                    columns.pool_scale(pool, b)
                    pool.wait_ge(columns.rows_ready, at(b + 1))
                    settle(pool, W["passed_pool"])
                    pool.tensor_tensor(X[:, b, :, :], X[:, b, :, :], W["bo"][:, :].unsqueeze(1).to_broadcast([P, J, D]),
                                       ALU.add).then_inc(bias_added, 1)

                pool.wait_ge(W["bo_in"], DMA)
                norms(0)
                prepare(1)
                with pool.Fori(1, NB - 2) as b:
                    columns1.pool_scale(pool, b - 1)
                    prepare(b + 1)
                    router.pool_dispatch(pool, b - 1, 0)
                columns1.pool_scale(pool, NB - 3)
                prepare(NB - 1)
                router.pool_dispatch(pool, NB - 3, 0)
                columns1.pool_scale(pool, NB - 2)
                router.pool_dispatch(pool, NB - 2, 0)
                router.rows_sent(pool, 0, NB - 1)

            @block.tensor
            def _(pe):
                for part in parts:
                    part.pe_credits(pe)
                for s in (q_psum, s_psum, pt_psum, o_psum, y_psum, k_psum, v_psum):
                    pe.sem_inc(s, CREDIT)

                def key_group(b, u, g):
                    pe.wait_ge(columns.ready, at(b + 1))
                    if not isinstance(b, int) or b > 0:
                        pe.wait_ge(k_ready, at(KV * b + g))
                    for c in range(C):
                        mm = split_product(pe, prep_bank(b, g)[:, 0:S], [w[:, c, g * DH:(g + 1) * DH] for w in W["wk"]],
                                           [x[:, c, :] for x in xt[u]], c == 0, c == C - 1)
                    mm.then_inc(k_psum, 1)

                def value_tile(b, u, j):
                    if not isinstance(b, int) or b > 0:
                        pe.wait_ge(k_ready, at(KV * (b + 1)))
                        pe.wait_ge(v_ready, at(J * b + j))
                    for c in range(C):
                        mm = split_product(pe, prep_bank(b, KV + j), [x[:, c, j * P:(j + 1) * P] for x in xt[u]],
                                           [w[:, c, :] for w in W["wv"]], c == 0, c == C - 1)
                    mm.then_inc(v_psum, 1)

                def prepare(b, u, h):
                    if h == COLUMNS:
                        columns.pe_transposes(pe, b, 0)
                    if KEYS <= h < KEYS + KV:
                        key_group(b, u, h - KEYS)
                    if VALUES <= h < VALUES + J:
                        if h == VALUES and (not isinstance(b, int) or b >= 2):
                            pe.wait_ge(router.rank_read, at(b - 1))
                        value_tile(b, u, h - VALUES)

                def route(b, h):
                    if h == COLUMNS1:
                        pe.wait_ge(v_ready, at(J * (b + 2)))
                        columns1.pe_transposes(pe, b, 0)
                    if h == LOGITS_T:
                        router.pe_logits_t(pe, b, 0)
                    if h == LOGITS:
                        router.pe_logits(pe, b)
                    if h == COLUMNS:
                        pe.wait_ge(router.logits_ready, at(b + 1))
                    if h == RANK:
                        if not isinstance(b, int) or b + 2 < NB:
                            pe.wait_ge(k_ready, at(KV * (b + 3)))
                        router.pe_rank(pe, b)

                def queries(i, c):
                    k, u, h = TWO * i + c, c // H % 2, c % H
                    pe.wait_ge(q_ready, at(k))
                    if h == 0:
                        pe.wait_ge(columns.ready, at(2 * i + c // H + 1))
                    for d in range(C):
                        mm = split_product(pe, ps_q[:, 0:S], [w[:, d, h * DH:(h + 1) * DH] for w in W["wq"]],
                                           [x[:, d, :] for x in xt[u]], d == 0, d == C - 1)
                    mm.then_inc(q_psum, 1)

                def scores(i, c):
                    k, u, h = TWO * i + c, c // H % 2, c % H
                    pe.wait_ge(q_ready, at(k + 1))
                    pe.wait_ge(exp_ready, at(k - 1))
                    if h == 0:
                        pe.wait_ge(k_ready, at(KV * (2 * i + c // H + 1)))
                    for j in range(J):
                        mm = split_product(pe, ps_s[c % 2][:, j, :], [x[:, j * P:(j + 1) * P] for x in qt[c % 2]],
                                           [x[:, h // GROUP, :] for x in keys[u]], True, True)
                    mm.then_inc(s_psum, 1)

                def transposes(i, c):
                    k = TWO * i + c
                    pe.wait_ge(p0_ready, at(k + 1))
                    pe.wait_ge(p1_ready, at(k + 1))
                    pe.wait_ge(pt_ready, at(k - 1))
                    for t in range(J):
                        for j in range(J):
                            mm = pe.transpose(ps_pt[c % 2][:, t, j * P:(j + 1) * P], prob[c % 2][:, j, t * P:(t + 1) * P],
                                              W["ident"][:, :])
                    mm.then_inc(pt_psum, 1)

                def values(i, c):
                    k, u, h = TWO * i + c, c // H % 2, c % H
                    g = h // GROUP
                    pe.wait_ge(pt_ready, at(k + 1))
                    pe.wait_ge(o_ready, at(k))
                    if h == 0:
                        pe.wait_ge(v_ready, at(J * (2 * i + c // H + 1)))
                    for t in range(J):
                        mm = split_product(pe, ps_o[:, 0:S], [v[:, t, g * DH:(g + 1) * DH] for v in vals[u]],
                                           [x[:, t, :] for x in prob_t[c % 2]], t == 0, t == J - 1)
                    mm.then_inc(o_psum, 1)

                def outputs(i, c):
                    k, h = TWO * i + c, c % H
                    pe.wait_ge(o_ready, at(k + 1))
                    if h == 0:
                        pe.wait_ge(x_added, at(2 * i + c // H))
                    for j in range(J):
                        left = [x[:, j * P:(j + 1) * P] for x in ot[c % 2]]
                        right = [w[:, h, :] for w in W["wo"]]
                        for n, (l, r) in enumerate(((left[1], right[0]), (left[0], right[1]), (left[0], right[0]))):
                            mm = pe.matmul(ps_y[:, j, :], l, r, start=(h == 0 and j == 0 and n == 0),
                                           stop=(h == H - 1 and n == 2), skip_group_check=True)
                    mm.then_inc(y_psum, 1)

                def step(i, c):
                    if exists(i, c + 2):
                        transposes(i, c + 2)
                    if exists(i, c + 5):
                        queries(i, c + 5)
                    if exists(i, c + 4):
                        scores(i, c + 4)
                    if last_batch(i, c):
                        route(2 * i + c // H - 1, c % H)
                    if next_batch(i, c):
                        prepare(2 * i + c // H + 1, 1 - c // H % 2, c % H)
                    if exists(i, c):
                        outputs(i, c)
                    if exists(i, c + 1):
                        values(i, c + 1)

                for h in range(H):
                    prepare(0, 0, h)
                walk(pe, step)

            @block.scalar
            def _(act):
                for part in parts:
                    part.act_credits(act)
                for s in (q_hi, exp_ready, p1_ready, pt_hi, o_hi, k_hi, v_hi):
                    act.sem_inc(s, CREDIT)

                def prepare(b, u, h):
                    if h == NORMALISE:
                        columns.act_normalise(act, b, 0)
                    if h == COLUMNS:
                        columns.act_hi(act, b, u)
                    if KEYS <= h < KEYS + KV:
                        g = h - KEYS
                        act.wait_ge(k_psum, at(KV * b + g + 1))
                        act.activation(keys[u][0][:, g, :], prep_bank(b, g)[:, 0:S], ACT.Identity, bias=bias(H, g)).then_inc(k_hi, 1)
                    if VALUES <= h < VALUES + J:
                        j = h - VALUES
                        act.wait_ge(v_psum, at(J * b + j + 1))
                        act.activation(vals[u][0][:, j, :], prep_bank(b, KV + j), ACT.Copy).then_inc(v_hi, 1)

                def route(b, h):
                    if h == NORMALISE1:
                        router.rows_sent(act, 0, b)
                        router.act_rows(act, b, 0)
                        columns1.act_normalise(act, b, 0)
                    if h == COLUMNS1:
                        columns1.act_hi(act, b, 0)
                    if h == LOGITS_T:
                        router.act_logits_t(act, b)
                    if h == LOGITS:
                        router.act_logits(act, b)
                    if h == CHOOSE + 2:
                        router.act_expo(act, b)

                def queries(i, c):
                    k = TWO * i + c
                    act.wait_ge(q_psum, at(k + 1))
                    act.wait_ge(s_psum, at(k - 1))
                    act.activation(qt[c % 2][0][:, :], ps_q[:, 0:S], ACT.Identity, bias=bias(0, c % H)).then_inc(q_hi, 1)

                def exponentials(i, c):
                    k = TWO * i + c
                    act.wait_ge(max_ready, at(k + 1))
                    act.wait_ge(pt_psum, at(k - 1))
                    for j in range(J):
                        op = act.activation(prob[c % 2][:, j, :], ps_s[c % 2][:, j, :], ACT.Exp,
                                            bias=neg_max[c % 2][:, j:j + 1], accum_out=row_sum[c % 2][:, j:j + 1])
                    op.then_inc(exp_ready, 1)

                def transposed(i, c):
                    k = TWO * i + c
                    act.wait_ge(pt_psum, at(k + 1))
                    act.wait_ge(o_psum, at(k - 1))
                    act.activation(prob_t[c % 2][0][:, :, :], ps_pt[c % 2][:, :, :], ACT.Copy).then_inc(pt_hi, 1)

                def normalised(i, c):
                    k = TWO * i + c
                    act.wait_ge(rec_ready, at(k + 1))
                    act.activation(prob[c % 2][:, 1, :], prob[c % 2][:, 1, :], ACT.Copy, scale=row_rec[c % 2][:, 1:2]).then_inc(p1_ready, 1)

                def outputs(i, c):
                    k = TWO * i + c
                    act.wait_ge(o_psum, at(k + 1))
                    act.wait_ge(y_psum, at(k - 1))
                    act.activation(ot[c % 2][0][:, :], ps_o[:, 0:S], ACT.Identity, bias=bias(H + KV, c % H // GROUP)).then_inc(o_hi, 1)

                def step(i, c):
                    if exists(i, c):
                        outputs(i, c)
                    if exists(i, c + 3):
                        exponentials(i, c + 3)
                    if exists(i, c + 2):
                        transposed(i, c + 2)
                    if exists(i, c + 3):
                        normalised(i, c + 3)
                    if exists(i, c + 5):
                        queries(i, c + 5)
                    if last_batch(i, c):
                        route(2 * i + c // H - 1, c % H)
                    if next_batch(i, c):
                        prepare(2 * i + c // H + 1, 1 - c // H % 2, c % H)

                for h in range(H):
                    prepare(0, 0, h)
                walk(act, step)

            @block.vector
            def _(dve):
                for part in parts:
                    part.dve_credits(dve)
                for s in (q_ready, max_ready, rec_ready, p0_ready, pt_ready, o_ready, k_ready, v_ready, x_added, combined):
                    dve.sem_inc(s, CREDIT)

                def prepare(b, u, h):
                    if h == MOMENTS:
                        if isinstance(b, int) and b == 0:
                            dve.wait_ge(gather_dma, DMA)
                            combine(dve, W, gathered, b, combined)
                        dve.wait_ge(combined, at(b + 1))
                        columns.dve_moments(dve, b)
                    if h == COLUMNS:
                        columns.dve_lo(dve, b, u)
                    if KEYS <= h < KEYS + KV:
                        g = h - KEYS
                        dve.wait_ge(k_hi, at(KV * b + g + 1))
                        dve.scalar_tensor_tensor(out=keys[u][1][:, g, :], in0=prep_bank(b, g)[:, 0:S], scalar=bias(H, g),
                                                 in1=keys[u][0][:, g, :].bitcast(F32), op0=ALU.add,
                                                 op1=ALU.subtract).then_inc(k_ready, 1)
                    if VALUES <= h < VALUES + J:
                        j = h - VALUES
                        dve.wait_ge(v_hi, at(J * b + j + 1))
                        dve.tensor_tensor(vals[u][1][:, j, :], prep_bank(b, KV + j), vals[u][0][:, j, :].bitcast(F32),
                                          ALU.subtract).then_inc(v_ready, 1)

                def route(b, h):
                    if h == MOMENTS1:
                        dve.drain()
                        columns1.dve_moments(dve, b)
                    if h == COLUMNS1:
                        columns1.dve_lo(dve, b, 0)
                    if CHOOSE <= h < CHOOSE + 3:
                        router.dve_choose(dve, b, (h - CHOOSE,))
                    if RANK <= h < RANK + 3:
                        router.dve_place(dve, b, 0, b, (h - RANK,))

                def maxima(i, c):
                    k = TWO * i + c
                    dve.wait_ge(s_psum, at(k + 1))
                    dve.wait_ge(exp_ready, at(k - 1))
                    dve.tensor_reduce(neg_max[c % 2][:, :], ps_s[c % 2][:, :, :], AX.X, ALU.max, negate=True).then_inc(max_ready, 1)

                def transposed(i, c):
                    k = TWO * i + c
                    dve.wait_ge(pt_hi, at(k + 1))
                    dve.tensor_tensor(prob_t[c % 2][1][:, :, :], ps_pt[c % 2][:, :, :],
                                      prob_t[c % 2][0][:, :, :].bitcast(F32), ALU.subtract).then_inc(pt_ready, 1)

                def queries(i, c):
                    k = TWO * i + c
                    dve.wait_ge(q_hi, at(k + 1))
                    dve.scalar_tensor_tensor(out=qt[c % 2][1][:, :], in0=ps_q[:, 0:S], scalar=bias(0, c % H),
                                             in1=qt[c % 2][0][:, :].bitcast(F32), op0=ALU.add,
                                             op1=ALU.subtract).then_inc(q_ready, 1)

                def normalised(i, c):
                    k = TWO * i + c
                    dve.wait_ge(exp_ready, at(k + 1))
                    dve.wait_ge(p1_ready, at(k - 1))
                    dve.reciprocal(row_rec[c % 2][:, :], row_sum[c % 2][:, :]).then_inc(rec_ready, 1)
                    dve.drain()
                    dve.tensor_scalar(prob[c % 2][:, 0, :], prob[c % 2][:, 0, :], row_rec[c % 2][:, 0:1], None, ALU.mult).then_inc(p0_ready, 1)

                def outputs(i, c):
                    k = TWO * i + c
                    dve.wait_ge(o_hi, at(k + 1))
                    dve.scalar_tensor_tensor(out=ot[c % 2][1][:, :], in0=ps_o[:, 0:S], scalar=bias(H + KV, c % H // GROUP),
                                             in1=ot[c % 2][0][:, :].bitcast(F32), op0=ALU.add,
                                             op1=ALU.subtract).then_inc(o_ready, 1)

                def step(i, c):
                    if exists(i, c):
                        outputs(i, c)
                    if exists(i, c + 3):
                        normalised(i, c + 3)
                    if exists(i, c + 2):
                        transposed(i, c + 2)
                    if exists(i, c + 5):
                        queries(i, c + 5)
                    if exists(i, c + 4):
                        maxima(i, c + 4)
                    if last_batch(i, c):
                        route(2 * i + c // H - 1, c % H)
                    if next_batch(i, c):
                        prepare(2 * i + c // H + 1, 1 - c // H % 2, c % H)
                    if c >= 0 and c % H == H - 1:
                        b = 2 * i + c // H
                        dve.wait_ge(bias_added, at(b + 1))
                        dve.wait_ge(y_psum, at(H * (b + 1)))
                        dve.tensor_tensor(X[:, b, :, :], ps_y[:, :, :], X[:, b, :, :], ALU.add).then_inc(x_added, 1)

                for h in range(H):
                    prepare(0, 0, h)
                walk(dve, step)


def macaron(nc, a):
    with ExitStack() as ctx:
        kept = {}
        m = Memory(nc, ctx, kept, "all")

        def halves(name, shape, m=m):
            return [m.sb(f"{name}_{part}", shape, F32R) for part in ("hi", "lo")]

        W = {
            "kept": kept,
            "mask_sum": m.sb("mask_sum", [P, E], BF16),
            "x": m.sb("x", [P, NB, J, D]),
            "gate": halves("gate", [P, C, HS]),
            "up": halves("up", [P, C, HS]),
            "router": halves("router", [P, C, P]),
            "shared_down": m.sb("shared_down", [P, HC, D]),
            "bo": m.sb("bo", [P, D]),
            "bias": m.sb("bias", [P, 25]),
            "ident": m.sb("ident", [P, P]),
            "before": m.sb("before", [P, P], BF16),
            "ones": m.sb("ones", [P, P], BF16),
            "first_slot_of": m.sb("first_slot_of", [P, E]),
            "half": m.sb("half", [P, J]),
            "own_slot": m.sb("own_slot", [P, Experts.QUADS, Experts.PAIRS]),
            "row_of": m.sb("row_of", [P, NB, J, K]),
            "weight": m.sb("weight", [P, NB, J * K]),
            "norm1": m.sb("norm1", [P, NB, 2, J]),
            "passed_pe": m.sem("passed_pe"),
            "passed_pool": m.sem("passed_pool"),
            "passed_dve": m.sem("passed_dve"),
            "x_in": m.sem("x_in"),
            "x_rest_in": m.sem("x_rest_in"),
            "down_in": m.sem("down_in"),
            "slots_zeroed": m.sem("slots_zeroed"),
            "routed_zeroed": m.sem("routed_zeroed"),
            "bo_in": m.sem("bo_in"),
            "slot_x": nc.dram_tensor("slot_x", (SLOTS, WIDE), F32, kind="Internal").ap(),
            "routed": nc.dram_tensor("routed", (ROWS, D), F32, kind="Internal").ap(),
            "raw_wq": nc.dram_tensor("raw_wq", (D, H * DH), F32, kind="Internal").ap(),
            "raw_wo": nc.dram_tensor("raw_wo", (H * DH, D), F32, kind="Internal").ap(),
        }
        with ExitStack() as until_attention:
            m_attn = Memory(nc, until_attention, kept, "all")
            for name, shape in (("wq", [P, C, H * DH]), ("wk", [P, C, KV * DH]), ("wv", [P, C, KV * DH]), ("wo", [P, H, D])):
                W[name] = halves(name, shape, m_attn)
            W["zeros"] = W["wo"][0][:, :, :].rearrange("p h d -> p (h d)")[:, 0:8 * WIDE].bitcast(F32)
            setup_phase(nc, W, a)
            first_ffn_phase(nc, W, a)
            attention_phase(nc, W, a)
        last_ffn_phase(nc, W, a)


_INS = ["L0_attn_x", "L0_attn_Wq", "L0_attn_bq", "L0_attn_Wk", "L0_attn_bk", "L0_attn_Wv", "L0_attn_bv", "L0_attn_Wo",
        "L0_attn_bo", "L0_ffn_Wr", "L0_ffn_router_bias", "L0_ffn_Wg", "L0_ffn_Wu", "L0_ffn_Wd", "L0_ffn_Sg", "L0_ffn_Su",
        "L0_ffn_Sd"]


def kernel(**inputs):
    import numpy as _np
    import concourse.bacc as _bacc
    from concourse.bass_utils import run_bass_kernel_spmd as _run

    nc = _bacc.Bacc("TRN2", target_bir_lowering=False, num_devices=1)
    arrays, args = {}, {}
    for name in _INS:
        x = _np.ascontiguousarray(inputs[name])
        arrays[f"in_{name}"] = x
        args[name] = nc.dram_tensor(f"in_{name}", x.shape, mybir.dt.from_np(x.dtype), kind="ExternalInput").ap()
    args["out"] = nc.dram_tensor("out_0", arrays["in_L0_attn_x"].shape, F32, kind="ExternalOutput").ap()
    macaron(nc, args)
    r = _run(nc, [arrays], core_ids=[0])
    return r.results[0]["out_0"]
```
